# Optimizing a Trainium2 kernel written in Bass

```python
import numpy as np
import jax
import jax.numpy as jnp

def _softmax(x, axis=-1):
    return jax.nn.softmax(x, axis=axis)

def _gelu(x):
    return jax.nn.gelu(x, approximate=True)

def _silu(x):
    return jax.nn.silu(x)

def _sigmoid(x):
    return jax.nn.sigmoid(x)

def _layernorm(x, axis=-1, eps=1e-05):
    m = jnp.mean(x, axis=axis, keepdims=True)
    v = jnp.var(x, axis=axis, keepdims=True)
    return (x - m) / jnp.sqrt(v + eps)

def _scatter_add(tgt, idx, src, axis=0):
    return tgt.at[idx].add(src)

def _segment_sum(src, seg, n):
    return jax.ops.segment_sum(src, seg, n)
kernel_name = 'mk_macaron_d2_jaxref_r8_f5620a'

def setup_inputs(seed: int=0):
    np.random.seed(seed)
    _w = jnp.asarray

    def _L0_attn_setup():
        import math
        import jax, jax.numpy as jnp
        import numpy as np
        D_MODEL = 128
        N_HEADS = 16
        D_HEAD = D_MODEL // N_HEADS
        BLOCK = 256
        BATCH = 2
        SEQ = 256

        def _rotate(t, cos, sin):
            t1 = t[..., 0::2]
            t2 = t[..., 1::2]
            r1 = t1 * cos - t2 * sin
            r2 = t1 * sin + t2 * cos
            return jnp.stack([r1, r2], axis=-1).reshape(t.shape)
        key = jax.random.key(seed)
        k1, k2, k3 = jax.random.split(key, 3)
        x = jax.random.normal(k1, (BATCH, SEQ, D_MODEL), dtype=jnp.float32)
        Wqkv = jax.random.normal(k2, (3 * D_MODEL, D_MODEL), dtype=jnp.float32) * 0.02
        Wo = jax.random.normal(k3, (D_MODEL, D_MODEL), dtype=jnp.float32) * 0.02
        log_xi = jnp.full((N_HEADS,), math.log(BLOCK / 2.0), dtype=jnp.float32)
        pi_gate_logit = jnp.full((N_HEADS,), 2.0, dtype=jnp.float32)
        e_gate_logit = jnp.full((N_HEADS,), 2.0, dtype=jnp.float32)
        return {'x': x, 'Wqkv': Wqkv, 'Wo': Wo, 'log_xi': log_xi, 'pi_gate_logit': pi_gate_logit, 'e_gate_logit': e_gate_logit}
    _L0_attn_in = _L0_attn_setup()

    def _L0_ffn_setup():
        import jax, jax.numpy as jnp
        import numpy as np
        B, S, D, E, F = (4, 256, 128, 8, 512)
        key = jax.random.key(seed)
        k0, k1, k2, k3 = jax.random.split(key, 4)
        x = jax.random.normal(k0, (B, S, D), dtype=jnp.float32)
        wg = jax.random.normal(k1, (D, E), dtype=jnp.float32) * 0.02
        w_gate = jax.random.normal(k2, (E, D, F), dtype=jnp.float32) * 0.02
        w_down = jax.random.normal(k3, (E, F, D), dtype=jnp.float32) * 0.02
        return {'x': x, 'wg': wg, 'w_gate': w_gate, 'w_down': w_down}
    _L0_ffn_in = _L0_ffn_setup()

    def _L1_attn_setup():
        import jax, jax.numpy as jnp
        import numpy as np
        B, S, H, NH = (2, 256, 128, 16)
        HD = H // NH
        EPS = 1e-06

        def _layernorm(x, scale, bias):
            x32 = x.astype(jnp.float32)
            mean = jnp.mean(x32, axis=-1, keepdims=True)
            var = jnp.mean(jnp.square(x32 - mean), axis=-1, keepdims=True)
            return (x32 - mean) * jax.lax.rsqrt(var + EPS) * scale + bias
        key = jax.random.key(seed)
        ks = jax.random.split(key, 16)
        init = lambda k, shape, fan_in: jax.random.normal(k, shape, jnp.float32) / np.sqrt(fan_in)
        return {'x': jax.random.normal(ks[0], (B, S, H), jnp.float32), 'Wq': init(ks[1], (H, H), H), 'bq': jnp.zeros((H,), jnp.float32), 'Wk': init(ks[2], (H, H), H), 'bk': jnp.zeros((H,), jnp.float32), 'Wv': init(ks[3], (H, H), H), 'bv': jnp.zeros((H,), jnp.float32), 'q_scale': jnp.ones((HD,), jnp.float32), 'q_bias': jnp.zeros((HD,), jnp.float32), 'k_scale': jnp.ones((HD,), jnp.float32), 'k_bias': jnp.zeros((HD,), jnp.float32), 'v_scale': jnp.ones((HD,), jnp.float32), 'v_bias': jnp.zeros((HD,), jnp.float32), 'Wo': init(ks[4], (H, H), H), 'bo': jnp.zeros((H,), jnp.float32)}
    _L1_attn_in = _L1_attn_setup()

    def _L1_ffn_setup():
        import jax, jax.numpy as jnp
        import numpy as np
        D = 128
        H = 256
        E = 8
        K = 2
        B, T = (4, 256)
        key = jax.random.key(seed)
        ks = jax.random.split(key, 7)
        s = 0.02
        return {'x': jax.random.normal(ks[0], (B, T, D), dtype=jnp.float32), 'W1': jax.random.normal(ks[1], (E, D, 2 * H), dtype=jnp.float32) * s, 'b1': jnp.zeros((E, 2 * H), dtype=jnp.float32), 'W2': jax.random.normal(ks[2], (E, H, D), dtype=jnp.float32) * s, 'b2': jnp.zeros((E, D), dtype=jnp.float32), 'Wr': jax.random.normal(ks[3], (D, E), dtype=jnp.float32) * s, 'br': jnp.zeros((E,), dtype=jnp.float32)}
    _L1_ffn_in = _L1_ffn_setup()
    _d = {'L0_attn_x': _L0_attn_in['x'], 'L0_attn_Wqkv': _L0_attn_in['Wqkv'], 'L0_attn_Wo': _L0_attn_in['Wo'], 'L0_attn_log_xi': _L0_attn_in['log_xi'], 'L0_attn_pi_gate_logit': _L0_attn_in['pi_gate_logit'], 'L0_attn_e_gate_logit': _L0_attn_in['e_gate_logit'], 'L0_ffn_wg': _L0_ffn_in['wg'], 'L0_ffn_w_gate': _L0_ffn_in['w_gate'], 'L0_ffn_w_down': _L0_ffn_in['w_down'], 'L1_attn_Wq': _L1_attn_in['Wq'], 'L1_attn_bq': _L1_attn_in['bq'], 'L1_attn_Wk': _L1_attn_in['Wk'], 'L1_attn_bk': _L1_attn_in['bk'], 'L1_attn_Wv': _L1_attn_in['Wv'], 'L1_attn_bv': _L1_attn_in['bv'], 'L1_attn_q_scale': _L1_attn_in['q_scale'], 'L1_attn_q_bias': _L1_attn_in['q_bias'], 'L1_attn_k_scale': _L1_attn_in['k_scale'], 'L1_attn_k_bias': _L1_attn_in['k_bias'], 'L1_attn_v_scale': _L1_attn_in['v_scale'], 'L1_attn_v_bias': _L1_attn_in['v_bias'], 'L1_attn_Wo': _L1_attn_in['Wo'], 'L1_attn_bo': _L1_attn_in['bo'], 'L1_ffn_W1': _L1_ffn_in['W1'], 'L1_ffn_b1': _L1_ffn_in['b1'], 'L1_ffn_W2': _L1_ffn_in['W2'], 'L1_ffn_b2': _L1_ffn_in['b2'], 'L1_ffn_Wr': _L1_ffn_in['Wr'], 'L1_ffn_br': _L1_ffn_in['br']}
    _x0 = _d['L0_attn_x']
    _d['L0_attn_x'] = jax.random.normal(jax.random.fold_in(jax.random.key(seed), 1), (16, 256, 128), dtype=_x0.dtype)
    del _x0
    return _d

def reference(L0_attn_x, L0_attn_Wqkv, L0_attn_Wo, L0_attn_log_xi, L0_attn_pi_gate_logit, L0_attn_e_gate_logit, L0_ffn_wg, L0_ffn_w_gate, L0_ffn_w_down, L1_attn_Wq, L1_attn_bq, L1_attn_Wk, L1_attn_bk, L1_attn_Wv, L1_attn_bv, L1_attn_q_scale, L1_attn_q_bias, L1_attn_k_scale, L1_attn_k_bias, L1_attn_v_scale, L1_attn_v_bias, L1_attn_Wo, L1_attn_bo, L1_ffn_W1, L1_ffn_b1, L1_ffn_W2, L1_ffn_b2, L1_ffn_Wr, L1_ffn_br):

    def _L0_attn_ref(x, Wqkv, Wo, log_xi, pi_gate_logit, e_gate_logit):
        import math
        import jax, jax.numpy as jnp
        import numpy as np
        D_MODEL = 128
        N_HEADS = 16
        D_HEAD = D_MODEL // N_HEADS
        BLOCK = 256
        BATCH = 2
        SEQ = 256

        def _rotate(t, cos, sin):
            t1 = t[..., 0::2]
            t2 = t[..., 1::2]
            r1 = t1 * cos - t2 * sin
            r2 = t1 * sin + t2 * cos
            return jnp.stack([r1, r2], axis=-1).reshape(t.shape)
        b, n, d = x.shape
        H, dh = (N_HEADS, D_HEAD)
        qkv = (x @ Wqkv.T).reshape(b, n, 3, H, dh)
        q = jnp.transpose(qkv[:, :, 0], (0, 2, 1, 3))
        k = jnp.transpose(qkv[:, :, 1], (0, 2, 1, 3))
        v = jnp.transpose(qkv[:, :, 2], (0, 2, 1, 3))
        pi_g = jax.nn.sigmoid(pi_gate_logit)
        e_g = jax.nn.sigmoid(e_gate_logit)
        kfrac = jnp.arange(0, dh, 2, dtype=jnp.float32) / dh
        pi_inv_freq = jnp.float32(math.pi) ** (1.0 - kfrac)
        pos = jnp.arange(n, dtype=jnp.float32)
        theta = pos[:, None] * pi_inv_freq[None, :]
        theta = theta[None, :, :] * pi_g[:, None, None]
        cos, sin = (jnp.cos(theta), jnp.sin(theta))
        q_rot = _rotate(q, cos, sin)
        k_rot = _rotate(k, cos, sin)
        scores = jnp.einsum('bhqd,bhkd->bhqk', q_rot, k_rot) / jnp.float32(math.sqrt(dh))
        xi = jnp.exp(log_xi)
        i = jnp.arange(n, dtype=jnp.float32)
        d_mat = jnp.abs(i[:, None] - i[None, :])
        decay_bias = -(d_mat[None, :, :] / xi[:, None, None]) * e_g[:, None, None]
        scores = scores + decay_bias[None]
        causal = jnp.tril(jnp.ones((n, n), dtype=bool))
        scores = jnp.where(causal[None, None], scores, jnp.float32(-jnp.inf))
        attn = jax.nn.softmax(scores, axis=-1)
        out = jnp.einsum('bhqk,bhkd->bhqd', attn, v)
        out = jnp.transpose(out, (0, 2, 1, 3)).reshape(b, n, d)
        return out @ Wo.T

    def _L0_ffn_ref(x, wg, w_gate, w_down):
        import jax, jax.numpy as jnp
        import numpy as np
        B, S, D, E, F = (4, 256, 128, 8, 512)
        Bb, Ss, Dd = x.shape
        Ee = wg.shape[1]
        T = Bb * Ss
        C = 2 * T // Ee
        tokens = x.reshape(T, Dd)
        logits = tokens.astype(jnp.float32) @ wg.astype(jnp.float32)
        gates = jax.nn.softmax(logits, axis=-1)
        idx1 = jnp.argmax(gates, axis=-1)
        mask1 = jax.nn.one_hot(idx1, Ee, dtype=jnp.int32)
        logits_no1 = jnp.where(mask1 > 0, -jnp.inf, logits)
        idx2 = jnp.argmax(logits_no1, axis=-1)
        mask2 = jax.nn.one_hot(idx2, Ee, dtype=jnp.int32)
        g1 = jnp.take_along_axis(gates, idx1[:, None], axis=-1)[:, 0]
        g2 = jnp.take_along_axis(gates, idx2[:, None], axis=-1)[:, 0]
        denom = jnp.clip(g1 + g2, 1e-09, None)
        g1, g2 = (g1 / denom, g2 / denom)
        loc1 = jnp.cumsum(mask1, axis=0) - mask1
        loc2 = jnp.cumsum(mask2, axis=0) - mask2 + jnp.sum(mask1, axis=0, keepdims=True)
        loc1_s = jnp.sum(loc1 * mask1, axis=-1)
        loc2_s = jnp.sum(loc2 * mask2, axis=-1)
        keep1 = (loc1_s < C).astype(x.dtype)
        keep2 = (loc2_s < C).astype(x.dtype)
        f1 = idx1 * C + jnp.minimum(loc1_s, C - 1)
        f2 = idx2 * C + jnp.minimum(loc2_s, C - 1)
        disp = jnp.zeros((Ee * C, Dd), dtype=x.dtype)
        disp = disp.at[f1].add(tokens * keep1[:, None])
        disp = disp.at[f2].add(tokens * keep2[:, None])
        disp = disp.reshape(Ee, C, Dd)
        h = jax.nn.gelu(jnp.einsum('ecd,edf->ecf', disp, w_gate), approximate=False)
        eo = jnp.einsum('ecf,efd->ecd', h, w_down).reshape(Ee * C, Dd)
        out = (g1 * keep1)[:, None].astype(x.dtype) * eo[f1] + (g2 * keep2)[:, None].astype(x.dtype) * eo[f2]
        return out.reshape(Bb, Ss, Dd)

    def _L1_attn_ref(x, Wq, bq, Wk, bk, Wv, bv, q_scale, q_bias, k_scale, k_bias, v_scale, v_bias, Wo, bo):
        import jax, jax.numpy as jnp
        import numpy as np
        B, S, H, NH = (2, 256, 128, 16)
        HD = H // NH
        EPS = 1e-06

        def _layernorm(x, scale, bias):
            x32 = x.astype(jnp.float32)
            mean = jnp.mean(x32, axis=-1, keepdims=True)
            var = jnp.mean(jnp.square(x32 - mean), axis=-1, keepdims=True)
            return (x32 - mean) * jax.lax.rsqrt(var + EPS) * scale + bias
        b, s, _ = x.shape
        q = (x @ Wq + bq).reshape(b, s, NH, HD)
        k = (x @ Wk + bk).reshape(b, s, NH, HD)
        v = (x @ Wv + bv).reshape(b, s, NH, HD)
        q = _layernorm(q, q_scale, q_bias)
        k = _layernorm(k, k_scale, k_bias)
        v = _layernorm(v, v_scale, v_bias)
        scale = HD ** (-0.5)
        scores = jnp.einsum('bqhd,bkhd->bhqk', q, k) * scale
        probs = jax.nn.softmax(scores, axis=-1)
        out = jnp.einsum('bhqk,bkhd->bqhd', probs, v).reshape(b, s, NH * HD)
        return out @ Wo + bo

    def _L1_ffn_ref(x, W1, b1, W2, b2, Wr, br):
        import jax, jax.numpy as jnp
        import numpy as np
        D = 128
        H = 256
        E = 8
        K = 2
        B, T = (4, 256)
        Bb, Tt, Dd = x.shape
        xf = x.reshape(-1, Dd)
        logits = xf @ Wr + br
        topk_val, topk_idx = jax.lax.top_k(logits, K)
        scores = jax.nn.softmax(topk_val, axis=-1)
        h = jnp.einsum('nd,edh->enh', xf, W1) + b1[:, None, :]
        a, g = jnp.split(h, 2, axis=-1)
        act = jax.nn.silu(a) * g
        out_e = jnp.einsum('enh,ehd->end', act, W2) + b2[:, None, :]
        out_ne = out_e.transpose(1, 0, 2)
        gathered = jnp.take_along_axis(out_ne, topk_idx[:, :, None], axis=1)
        out = jnp.sum(gathered * scores[:, :, None], axis=1)
        return out.reshape(Bb, Tt, Dd)
    x = L0_attn_x
    x = x + 0.5 * _L0_ffn_ref(_layernorm(x, axis=-1), L0_ffn_wg, L0_ffn_w_gate, L0_ffn_w_down)
    x = x + _L0_attn_ref(_layernorm(x, axis=-1), L0_attn_Wqkv, L0_attn_Wo, L0_attn_log_xi, L0_attn_pi_gate_logit, L0_attn_e_gate_logit)
    x = x + 0.5 * _L0_ffn_ref(_layernorm(x, axis=-1), L0_ffn_wg, L0_ffn_w_gate, L0_ffn_w_down)
    x = x + 0.5 * _L1_ffn_ref(_layernorm(x, axis=-1), L1_ffn_W1, L1_ffn_b1, L1_ffn_W2, L1_ffn_b2, L1_ffn_Wr, L1_ffn_br)
    x = x + _L1_attn_ref(_layernorm(x, axis=-1), L1_attn_Wq, L1_attn_bq, L1_attn_Wk, L1_attn_bk, L1_attn_Wv, L1_attn_bv, L1_attn_q_scale, L1_attn_q_bias, L1_attn_k_scale, L1_attn_k_bias, L1_attn_v_scale, L1_attn_v_bias, L1_attn_Wo, L1_attn_bo)
    x = x + 0.5 * _L1_ffn_ref(_layernorm(x, axis=-1), L1_ffn_W1, L1_ffn_b1, L1_ffn_W2, L1_ffn_b2, L1_ffn_Wr, L1_ffn_br)
    return x

_drawn_inputs = setup_inputs


def setup_inputs(seed=0):
    import zlib

    import numpy as np

    out = dict(_drawn_inputs(seed))
    spreads = {'L0_attn_log_xi': (4.852030277252197, 0.6),
     'L0_attn_pi_gate_logit': (2.0, 0.6),
     'L0_attn_e_gate_logit': (2.0, 0.6),
     'L1_attn_bq': (0.0, 0.45),
     'L1_attn_bk': (0.0, 0.769),
     'L1_attn_bv': (0.0, 0.1),
     'L1_attn_q_scale': (1.0, 0.2),
     'L1_attn_q_bias': (0.0, 0.718),
     'L1_attn_k_scale': (1.0, 0.6),
     'L1_attn_k_bias': (0.0, 0.8),
     'L1_attn_v_scale': (1.0, 0.2),
     'L1_attn_v_bias': (0.0, 0.1),
     'L1_attn_bo': (0.0, 0.1),
     'L1_ffn_b1': (0.0, 0.8),
     'L1_ffn_b2': (0.0, 0.1),
     'L1_ffn_br': (0.0, 0.1)}
    factors = {'L0_attn_Wqkv': 5.736, 'L0_attn_Wo': 5.465, 'L1_ffn_W1': 8.0, 'L1_ffn_W2': 7.974}
    for name, (base, spread) in spreads.items():
        noise = np.random.default_rng([zlib.crc32(name.encode()), seed]).standard_normal(out[name].shape)
        drawn = base * np.exp(spread * noise) if base else spread * noise
        out[name] = jnp.asarray(drawn.astype(out[name].dtype))
    for name, factor in factors.items():
        out[name] = (out[name] * factor).astype(out[name].dtype)
    return out
```

```python
import concourse.bass as bass
from concourse import mybir
from concourse.alu_op_type import AluOpType as ALU
from contextlib import ExitStack

F32 = mybir.dt.float32
BF16 = mybir.dt.bfloat16
I32 = mybir.dt.int32
U32 = mybir.dt.uint32
ACT = mybir.ActivationFunctionType
AX = mybir.AxisListType.X

P = 128
D = 128
SEQ = 256
BATCHES = 16
TOKENS = BATCHES * SEQ
TILES = TOKENS // P
TPB = SEQ // P
E = 8
TOPK = 2
CAP = TOPK * TOKENS // E
ROWS = 256
REGION = TOKENS + ROWS
SPARE = E * REGION
SLOT_ROWS = SPARE + ROWS
MOE_TILES = (TOPK * TOKENS + E * (ROWS - 1)) // ROWS
MOE_TILES += MOE_TILES % 2
UP = 512
LN_EPS = 1e-5
HEADS = 16
DH = 8
XR = 64
PROD, DECAY, MAXR = 0, 48, 54
XQ = 2 * HEADS * XR
MASKED = -1e30
QK_EPS = 1e-6
WO0 = 3 * D
BI0 = WO0 + D
SC0 = BI0 + 3 * D
SB0 = SC0 + 3 * D
BO0 = SB0 + 3 * D
ONE0 = BO0 + D
GATE0 = WO0 + D
XI0 = GATE0 + 2 * HEADS
ANG0 = XI0 + HEADS
POS0 = ANG0 + 4 * TPB
MASK0 = POS0 + TPB
TWO_PI = 6.283185307179586
TWO_PI_HI = 6.28125
TWO_PI_LO = TWO_PI - TWO_PI_HI
HALF_PI = TWO_PI / 4
PI_BELOW = 3.1415925
ROUNDER = 1.5 * 2 ** 23


class Persistent:

    def __init__(self, nc, ctx):
        def sb(name, shape, dt):
            return ctx.enter_context(nc.sbuf_tensor(name, shape, dt))

        self.x = sb("x_res", [P, TILES, D], F32)
        self.ident = sb("ident", [P, P], F32)
        self.upper = sb("upper", [P, P], BF16)
        self.ones = sb("ones", [P, P], BF16)
        self.iota_e = sb("iota_e", [P, E], F32)
        self.base = sb("base", [P, E], F32)
        self.iota_rows = sb("iota_rows", [P, TOKENS // ROWS], F32)
        self.iota_tiles = sb("iota_tiles", [P, MOE_TILES], F32)
        self.neg_half = sb("neg_half", [P, 96], F32)
        self.no_rows = sb("no_rows", [P, TPB * TOPK], I32)
        self.zeros = sb("zeros", [P, ROWS // P * D], F32)
        self.rows_all = sb("rows_all", [P, TILES, TOPK], I32)
        self.gates = sb("gates", [P, TILES, TOPK], F32)
        self.table = sb("table", [P, MOE_TILES, 2], I32)
        self.counts = sb("counts", [P, E], I32)


def stage_semaphores(nc, ctx, tag):
    held = []

    def clear():
        nc.clear_and_free_semaphores(held)
        nc.all_engine_barrier()

    ctx.callback(clear)

    def sem(name):
        held.append(nc.alloc_semaphore(f"{tag}_{name}"))
        return held[-1]

    return sem


def setup_stage(nc, keep, x_in, consts):
    with ExitStack() as ctx:
        s_load = stage_semaphores(nc, ctx, "setup")("load")
        f = ctx.enter_context(nc.sbuf_tensor("const_f", [P, consts.shape[1]], F32))
        block = ctx.enter_context(nc.Block())

        @block.sync
        def _(sp):
            sp.dma_start(f[:, :], consts).then_inc(s_load, 16)
            sp.dma_start(keep.x[:, :, :], x_in.rearrange("(n p) d -> p n d", p=P)).then_inc(s_load, 16)
            sp.wait_ge(s_load, 32)

        @block.vector
        def _(dve):
            dve.wait_ge(s_load, 32)
            o = 0
            for dst in (keep.ident, keep.upper, keep.iota_e, keep.base, keep.iota_rows, keep.iota_tiles):
                n = dst.shape[1]
                nc.vector.tensor_copy(dst[:, :], f[:, o:o + n])
                o += n
            nc.vector.memset(keep.ones[:, :], 1.0)
            nc.vector.memset(keep.zeros[:, :], 0.0)
            nc.vector.memset(keep.no_rows[:, :], 0)
            nc.vector.memset(keep.neg_half[:, :], -0.5)


def wait(eng, sem, value):
    if isinstance(value, int) and value <= 0:
        return
    eng.wait_ge(sem, value)


class Chain:

    def __init__(self, eng, sem):
        self.eng, self.sem, self.n = eng, sem, 0

    def __call__(self, ins):
        ins.then_inc(self.sem, 1)
        self.n += 1
        self.eng.wait_ge(self.sem, self.n)

    def restart(self):
        self.eng.sem_clear(self.sem)
        self.n = 0


class Combine:

    def __init__(self, nc, keep, sb, sem, slots):
        self.nc, self.keep, self.slots = nc, keep, slots
        K4 = TPB * TOPK
        self.idx0 = sb("idx0", [P, 2, K4], I32)
        self.idx = sb("idx", [P, 2, K4], I32)
        self.got = sb("got", [P, 2, K4, D], F32)
        self.gate = sb("gate_b", [P, 2, K4], F32)
        self.used = sb("used", [P, 2], F32)
        self.s_got = [sem(f"got{u}") for u in range(2)]
        self.s_added = sem("added")

    def pool_gather(self, pool, chain, b, u):
        nc, keep = self.nc, self.keep
        chain(nc.gpsimd.tensor_copy(self.idx0[:, u, :].rearrange("p (t k) -> p t k", t=TPB),
                                    keep.rows_all[:, bass.ds(b * TPB, TPB), :]))
        wait(pool, self.s_added, b - 1)
        chain(nc.gpsimd.tensor_tensor(self.idx[:, u, :], self.idx0[:, u, :], keep.no_rows[:, :], ALU.add))
        for k in range(TPB * TOPK):
            pool.indirect_dma_start(
                self.got[:, u, k, :], None, self.slots,
                bass.IndirectOffsetOnAxis(ap=self.idx[:, u, k:k + 1].bitcast(U32), axis=0),
            ).then_inc(self.s_got[u], 16)

    def dve_add(self, dve, link, b, u):
        nc, keep = self.nc, self.keep
        link(nc.vector.tensor_copy(self.gate[:, u, :].rearrange("p (t k) -> p t k", t=TPB),
                                   keep.gates[:, bass.ds(b * TPB, TPB), :]))
        wait(dve, self.s_got[u], (b - u) * 8 * TPB * TOPK + 16 * TPB * TOPK)
        for k in range(TOPK):
            for t in range(TPB):
                ins = nc.vector.scalar_tensor_tensor(
                    out=keep.x[:, bass.ds(b * TPB + t, 1), :],
                    in0=self.got[:, u, t * TOPK + k, :].unsqueeze(1),
                    scalar=self.gate[:, u, t * TOPK + k:t * TOPK + k + 1],
                    in1=keep.x[:, bass.ds(b * TPB + t, 1), :],
                    op0=ALU.mult, op1=ALU.add)
                if t < TPB - 1:
                    ins.then_inc(link.sem, 1)
                    link.n += 1
                else:
                    link(ins)
        nc.vector.tensor_copy(self.used[:, u:u + 1], self.gate[:, u, 0:1]).then_inc(self.s_added, 1)


class Norm:

    def __init__(self, nc, keep, sb, sem, name, buffers=2):
        self.nc, self.keep, self.n = nc, keep, buffers
        self.stats = sb(f"{name}_stats", [P, 2, TPB, 6], F32)
        self.mv = sb(f"{name}_mv", [P, 2, TPB, 2], F32)
        self.vare = sb(f"{name}_vare", [P, 2, TPB], F32)
        self.rstd = sb(f"{name}_rstd", [P, 2, TPB], F32)
        self.out = sb(f"{name}_out", [P, 2, TPB, D], F32)
        self.s_var = sem(f"{name}_var")
        self.s_rstd = sem(f"{name}_rstd")
        self.s_out = sem(f"{name}_out")

    def dve_stats(self, dve, link, b, u):
        nc = self.nc
        for t in range(TPB):
            link(nc.vector.bn_stats(self.stats[:, u, t, :], self.keep.x[:, bass.ds(b * TPB + t, 1), :]))
        for t in range(TPB):
            link(nc.vector.bn_aggr(self.mv[:, u, t, :], self.stats[:, u, t, :]))
        nc.vector.tensor_scalar(self.vare[:, u, :], self.mv[:, u, :, 1], LN_EPS, None,
                                ALU.add).then_inc(self.s_var, 1)

    def pool_rstd(self, pool, b, u):
        wait(pool, self.s_var, b + 1)
        self.nc.gpsimd.tensor_tensor(self.rstd[:, u, :], self.vare[:, u, :], self.keep.neg_half[:, 0:TPB],
                                     ALU.pow).then_inc(self.s_rstd, 1)

    def dve_apply(self, dve, b, u):
        wait(dve, self.s_rstd, b + 1)
        for t in range(TPB):
            ins = self.nc.vector.tensor_scalar(
                self.out[:, u, t, :].unsqueeze(1), self.keep.x[:, bass.ds(b * TPB + t, 1), :],
                self.mv[:, u, t, 0:1], self.rstd[:, u, t:t + 1], ALU.subtract, ALU.mult)
        ins.then_inc(self.s_out, 1)


class Route:

    def __init__(self, nc, keep, sb, sem, slots, has_bias, capacity):
        self.nc, self.keep, self.slots, self.has_bias, self.capacity = nc, keep, slots, has_bias, capacity
        U = 2
        self.norm = Norm(nc, keep, sb, sem, "route")
        self.xnT = sb("xnT", [P, U, SEQ], F32)
        self.wr = sb("wr", [P, 2 * E], F32)
        self.lg = sb("lg", [P, U, TPB, E], F32)
        self.mx = sb("top", [P, U, TPB, 8], F32)
        self.mi = sb("top_i", [P, U, TPB, 8], U32)
        self.mif = sb("top_f", [P, U, TPB, TOPK], F32)
        self.M = sb("choice", [P, U, TPB, TOPK, E], BF16)
        self.M_all = sb("choice_all", [P, TILES, TOPK, E], BF16)
        self.R = sb("running", [P, TOPK, E], F32)
        self.A = sb("before", [P, U, TPB, TOPK, E], F32)
        self.B = sb("before_sum", [P, U, 2, TPB, E], F32)
        self.prod = sb("picked", [P, U, 2, TPB * TOPK, E], F32)
        self.rows_f = sb("rows_f", [P, U, TPB * TOPK], F32)
        self.rows0 = sb("rows0", [P, U, TPB * TOPK], I32)
        self.rows = sb("rows", [P, U, TPB * TOPK], I32)
        self.loc = sb("loc", [P, TILES, TOPK], F32)
        self.rowx = sb("rowx", [P, TILES, TOPK], F32)
        self.dl = sb("dl", [P, TILES], F32)
        many = TILES * TOPK
        self.shift = sb("shift", [P, 2, many, E], F32)
        self.rowy = sb("rowy", [P, 2, many], F32)
        self.g = sb("g", [P, 6, TILES], F32)
        self.ahead = sb("ahead", [P, TILES, E], F32)
        self.cnt = sb("cnt", [P, 6, E], F32)
        self.cmp = sb("cmp", [P, E, TOKENS // ROWS], F32)
        self.tt = sb("tt", [P, 3, MOE_TILES, E], F32)
        self.tr = sb("tr", [P, 6, MOE_TILES], F32)
        self.s_w = sem("router_w")
        self.s_T = sem("route_T")
        self.s_xnT = sem("route_xnT")
        self.s_L = sem("logits")
        self.s_M = sem("choices")
        self.s_P = sem("prefix")
        self.s_A = sem("prefix_used")
        self.s_rows = sem("row_numbers")
        self.s_scat = [sem(f"scattered{u}") for u in range(U)]
        self.s_dl = sem("logit_gap")
        self.s_exp = sem("gap_exp")
        self.s_tab = sem("table")
        self.s_zero = sem("tails")

    def sp_load(self, sp, router):
        sp.dma_start(self.wr[:, :], router).then_inc(self.s_w, 16)

    def dve_start(self, dve, link):
        link(self.nc.vector.memset(self.R[:, :, :], 0.0))
        dve.wait_ge(self.s_w, 16)

    def dve_norm(self, dve, b, u):
        wait(dve, self.s_scat[u], (b - u) * 8 * TPB * TOPK)
        self.norm.dve_apply(dve, b, u)

    def pe_T(self, pe, b, u, ps):
        wait(pe, self.norm.s_out, b + 1)
        for t in range(TPB):
            last = self.nc.tensor.transpose(ps[:, t * P:(t + 1) * P], self.norm.out[:, u, t, :], self.keep.ident[:, :])
        last.then_inc(self.s_T, 1)

    def act_T(self, act, b, u, ps):
        act.wait_ge(self.s_T, b + 1)
        self.nc.scalar.copy(self.xnT[:, u, :], ps[:, 0:SEQ]).then_inc(self.s_xnT, 1)

    def pe_L(self, pe, b, u, ps):
        pe.wait_ge(self.s_xnT, b + 1)
        for t in range(TPB):
            last = self.nc.tensor.matmul(ps[:, t * E:(t + 1) * E], self.xnT[:, u, t * P:(t + 1) * P],
                                         self.wr[:, 0:E], start=True, stop=True)
        last.then_inc(self.s_L, 1)

    def dve_choose(self, dve, link, b, u, ps):
        nc, keep = self.nc, self.keep
        dve.wait_ge(self.s_L, b + 1)
        lg = self.lg[:, u, :, :]
        src = ps[:, 0:TPB * E].rearrange("p (t e) -> p t e", t=TPB)
        if self.has_bias:
            link(nc.vector.tensor_tensor(lg, src, self.wr[:, E:2 * E].unsqueeze(1).to_broadcast([P, TPB, E]), ALU.add))
        else:
            link(nc.vector.tensor_copy(lg, src))
        for t in range(TPB):
            link(nc.vector.max(self.mx[:, u, t, :], self.lg[:, u, t, :]))
        for t in range(TPB):
            link(nc.vector.max_index(self.mi[:, u, t, :], self.mx[:, u, t, :], self.lg[:, u, t, :]))
        nc.vector.tensor_tensor(self.dl[:, bass.ds(b * TPB, TPB)], self.mx[:, u, :, 1], self.mx[:, u, :, 0],
                                ALU.subtract).then_inc(self.s_dl, 1)
        link(nc.vector.tensor_copy(self.mif[:, u, :, :], self.mi[:, u, :, 0:TOPK]))
        nc.vector.tensor_tensor(
            self.M[:, u, :, :, :].rearrange("p t k e -> p (t k) e"),
            self.mif[:, u, :, :].rearrange("p t k -> p (t k)").unsqueeze(2).to_broadcast([P, TPB * TOPK, E]),
            keep.iota_e[:, :].unsqueeze(1).to_broadcast([P, TPB * TOPK, E]),
            ALU.is_equal).then_inc(self.s_M, 1)

    def pe_P(self, pe, b, u, ps):
        nc, keep = self.nc, self.keep
        pe.wait_ge(self.s_M, b + 1)
        m = [self.M[:, u, t, :, :].rearrange("p k e -> p (k e)") for t in range(TPB)]
        nc.tensor.matmul(ps[:, 0:16], keep.upper[:, :], m[0], start=True, stop=True)
        nc.tensor.matmul(ps[:, 16:32], keep.upper[:, :], m[1], start=True, stop=False)
        nc.tensor.matmul(ps[:, 16:32], keep.ones[:, :], m[0], start=False, stop=True)
        nc.tensor.matmul(ps[:, 32:48], keep.ones[:, :], m[0], start=True, stop=False)
        nc.tensor.matmul(ps[:, 32:48], keep.ones[:, :], m[1], start=False, stop=True).then_inc(self.s_P, 1)

    def dve_rows(self, dve, link, b, u, ps):
        nc, keep = self.nc, self.keep
        dve.wait_ge(self.s_M, b + 1)
        nc.vector.tensor_copy(self.M_all[:, bass.ds(b * TPB, TPB), :, :], self.M[:, u, :, :, :])
        dve.wait_ge(self.s_P, b + 1)
        link(nc.vector.tensor_tensor(
            self.A[:, u, :, :, :].rearrange("p t k e -> p t (k e)"),
            ps[:, 0:32].rearrange("p (t m) -> p t m", t=TPB),
            self.R[:, :, :].rearrange("p k e -> p (k e)").unsqueeze(1).to_broadcast([P, TPB, TOPK * E]), ALU.add))
        nc.vector.tensor_tensor(
            self.R[:, :, :], ps[:, 32:48].rearrange("p (k e) -> p k e", k=TOPK), self.R[:, :, :],
            ALU.add).then_inc(self.s_A, 1)
        link(nc.vector.tensor_tensor(self.B[:, u, 0, :, :], self.A[:, u, :, 0, :], self.A[:, u, :, 1, :], ALU.add))
        link(nc.vector.tensor_tensor(self.B[:, u, 1, :, :], self.B[:, u, 0, :, :],
                                     keep.base[:, :].unsqueeze(1).to_broadcast([P, TPB, E]), ALU.add))
        m = self.M[:, u, :, :, :]
        nc.vector.tensor_tensor(
            self.prod[:, u, 0, :, :], m.rearrange("p t k e -> p (t k) e"),
            self.A[:, u, :, :, :].rearrange("p t k e -> p (t k) e"), ALU.mult)
        link(nc.vector.tensor_tensor(
            self.prod[:, u, 1, :, :].rearrange("p (t k) e -> p t k e", t=TPB), m,
            self.B[:, u, 1, :, :].unsqueeze(2).to_broadcast([P, TPB, TOPK, E]), ALU.mult))
        nc.vector.tensor_reduce(
            self.loc[:, bass.ds(b * TPB, TPB), :],
            self.prod[:, u, 0, :, :].rearrange("p (t k) e -> p t k e", t=TPB), AX, ALU.add)
        link(nc.vector.tensor_reduce(self.rows_f[:, u, :], self.prod[:, u, 1, :, :], AX, ALU.add))
        nc.vector.tensor_copy(self.rowx[:, bass.ds(b * TPB, TPB), :],
                              self.rows_f[:, u, :].rearrange("p (t k) -> p t k", t=TPB))
        nc.vector.tensor_copy(self.rows0[:, u, :], self.rows_f[:, u, :]).then_inc(self.s_rows, 1)

    def pool_scatter(self, pool, chain, b, u):
        wait(pool, self.s_rows, b + 1)
        chain(self.nc.gpsimd.tensor_tensor(self.rows[:, u, :], self.rows0[:, u, :], self.keep.no_rows[:, :], ALU.add))
        for k in range(TPB * TOPK):
            pool.indirect_dma_start(
                self.slots, bass.IndirectOffsetOnAxis(ap=self.rows[:, u, k:k + 1].bitcast(U32), axis=0),
                self.norm.out[:, u, k // TOPK, :], None).then_inc(self.s_scat[u], 16)

    def pool_end(self, pool):
        for u in range(2):
            pool.wait_ge(self.s_scat[u], 8 * TPB * TOPK * BATCHES)

    def act_end(self, act):
        act.wait_ge(self.s_dl, BATCHES)
        self.nc.scalar.activation(self.g[:, 0, :], self.dl[:, :], ACT.Exp).then_inc(self.s_exp, 1)

    def dve_end(self, dve, link):
        nc, keep, g, cnt, tt, tr = self.nc, self.keep, self.g, self.cnt, self.tt, self.tr
        dve.wait_ge(self.s_A, BATCHES)
        nr = TOKENS // ROWS
        link(nc.vector.tensor_tensor(cnt[:, 0, :], self.R[:, 0, :], self.R[:, 1, :], ALU.add))
        link(nc.vector.tensor_copy(keep.counts[:, :], cnt[:, 0, :]))
        link(nc.vector.tensor_tensor(
            self.cmp[:, :, :], cnt[:, 0, :].unsqueeze(2).to_broadcast([P, E, nr]),
            keep.iota_rows[:, :].unsqueeze(1).to_broadcast([P, E, nr]), ALU.is_gt))
        link(nc.vector.tensor_reduce(cnt[:, 1, :], self.cmp[:, :, :], AX, ALU.add))
        link(nc.vector.memset(cnt[:, 5, :], 1.0))
        link(nc.vector.tensor_tensor_scan(cnt[:, 2, :], cnt[:, 5, :], cnt[:, 1, :], 0.0, ALU.mult, ALU.add))
        link(nc.vector.tensor_tensor(cnt[:, 3, :], cnt[:, 2, :], cnt[:, 1, :], ALU.subtract))
        link(nc.vector.scalar_tensor_tensor(
            out=cnt[:, 4, :], in0=cnt[:, 3, :], scalar=-float(ROWS), in1=keep.base[:, :],
            op0=ALU.mult, op1=ALU.add))
        jt = keep.iota_tiles[:, :].unsqueeze(2).to_broadcast([P, MOE_TILES, E])

        def per_e(row):
            return row.unsqueeze(1).to_broadcast([P, MOE_TILES, E])

        nc.vector.tensor_tensor(tt[:, 0, :, :], per_e(cnt[:, 2, :]), jt, ALU.is_gt)
        link(nc.vector.tensor_tensor(tt[:, 1, :, :], per_e(cnt[:, 3, :]), jt, ALU.is_le))
        link(nc.vector.tensor_tensor(tt[:, 2, :, :], tt[:, 0, :, :], tt[:, 1, :, :], ALU.mult))
        nc.vector.tensor_tensor(tt[:, 0, :, :], tt[:, 2, :, :], per_e(cnt[:, 4, :]), ALU.mult)
        link(nc.vector.tensor_tensor(tt[:, 1, :, :], tt[:, 2, :, :], per_e(keep.iota_e[:, :]), ALU.mult))
        link(nc.vector.tensor_reduce(tr[:, 0:3, :], tt[:, :, :, :], AX, ALU.add))
        nc.vector.tensor_scalar(tr[:, 5, :], tr[:, 2, :], -float(SPARE), float(SPARE), ALU.mult, ALU.add)
        link(nc.vector.scalar_tensor_tensor(
            out=tr[:, 3, :], in0=keep.iota_tiles[:, :], scalar=float(ROWS), in1=tr[:, 2, :],
            op0=ALU.mult, op1=ALU.mult))
        link(nc.vector.tensor_tensor(tr[:, 4, :], tr[:, 3, :], tr[:, 0, :], ALU.add))
        link(nc.vector.tensor_tensor(tr[:, 3, :], tr[:, 4, :], tr[:, 5, :], ALU.add))
        nc.vector.tensor_copy(keep.table[:, :, 0], tr[:, 1, :])
        nc.vector.tensor_copy(keep.table[:, :, 1], tr[:, 3, :]).then_inc(self.s_tab, 1)
        many = TILES * TOPK
        link(nc.vector.tensor_tensor(
            self.shift[:, 0, :, :], self.M_all[:, :, :, :].rearrange("p n k e -> p (n k) e"),
            cnt[:, 4, :].unsqueeze(1).to_broadcast([P, many, E]), ALU.mult))
        link(nc.vector.tensor_reduce(self.rowy[:, 0, :], self.shift[:, 0, :, :], AX, ALU.add))
        nc.vector.tensor_tensor(
            keep.rows_all[:, :, :].rearrange("p n k -> p (n k)"),
            self.rowx[:, :, :].rearrange("p n k -> p (n k)"), self.rowy[:, 0, :], ALU.subtract)
        dve.wait_ge(self.s_exp, 1)
        link(nc.vector.tensor_scalar(g[:, 1, :], g[:, 0, :], 1.0, 2.0, ALU.add, ALU.mult))
        link(nc.vector.reciprocal(g[:, 2, :], g[:, 1, :]))
        link(nc.vector.tensor_tensor(g[:, 3, :], g[:, 0, :], g[:, 2, :], ALU.mult))
        if self.capacity:
            link(nc.vector.tensor_tensor(
                self.ahead[:, :, :], self.M_all[:, :, 1, :],
                self.R[:, 0, :].unsqueeze(1).to_broadcast([P, TILES, E]), ALU.mult))
            link(nc.vector.tensor_reduce(g[:, 4, :], self.ahead[:, :, :], AX, ALU.add))
            link(nc.vector.tensor_tensor(g[:, 5, :], g[:, 4, :], self.loc[:, :, 1], ALU.add))
            nc.vector.scalar_tensor_tensor(
                out=keep.gates[:, :, 0], in0=self.loc[:, :, 0], scalar=float(CAP), in1=g[:, 2, :],
                op0=ALU.is_lt, op1=ALU.mult)
            nc.vector.scalar_tensor_tensor(
                out=keep.gates[:, :, 1], in0=g[:, 5, :], scalar=float(CAP), in1=g[:, 3, :],
                op0=ALU.is_lt, op1=ALU.mult)
        else:
            nc.vector.tensor_copy(keep.gates[:, :, 0], g[:, 2, :])
            nc.vector.tensor_copy(keep.gates[:, :, 1], g[:, 3, :])

    def sp_end(self, sp):
        sp.wait_ge(self.s_tab, 1)
        for e in range(E):
            c = sp.value_load(self.keep.counts[0:1, e:e + 1], min_val=0, max_val=TOKENS)
            sp.dma_start(self.slots[bass.ds(c + e * REGION, ROWS), :].rearrange("(p s) d -> p (s d)", p=P),
                         self.keep.zeros[:, :]).then_inc(self.s_zero, 16)
        sp.dma_start(self.slots[SPARE:SPARE + ROWS, :].rearrange("(p s) d -> p (s d)", p=P),
                     self.keep.zeros[:, :]).then_inc(self.s_zero, 16)
        sp.wait_ge(self.s_zero, 16 * (E + 1))


def pairs_of_steps(eng, first, lo, hi, last, step):
    for s in range(first, lo):
        step(s, s % 2)
    if hi > lo:
        with eng.Fori(0, (hi - lo) // 2) as i:
            for u in range(2):
                step(i * 2 + (lo + u), (lo + u) % 2)
    for s in range(hi, last + 1):
        step(s, s % 2)


def has(b):
    return not isinstance(b, int) or 0 <= b < BATCHES


def token_stage(nc, keep, tag, slots_in, slots_out, router=None, router_bias=False, capacity=False, out=None):
    with ExitStack() as ctx:
        def sb(name, shape, dt):
            return ctx.enter_context(nc.sbuf_tensor(f"{tag}_{name}", shape, dt))

        def pb(name, shape, dt):
            return ctx.enter_context(nc.psum_tensor(f"{tag}_{name}", shape, dt))

        sem = stage_semaphores(nc, ctx, tag)

        comb = Combine(nc, keep, sb, sem, slots_in) if slots_in is not None else None
        route = Route(nc, keep, sb, sem, slots_out, router_bias, capacity) if slots_out is not None else None
        psT = [pb(f"psT{u}", [P, 512], F32) for u in range(2)]
        psL = [pb(f"psL{u}", [P, 512], F32) for u in range(2)]
        psP = [pb(f"psP{u}", [P, 512], F32) for u in range(2)]
        s_dve = sem("dve_chain")
        s_pool = sem("pool_chain")
        s_out = sem("out")
        block = ctx.enter_context(nc.Block())

        @block.gpsimd
        def _(pool):
            chain = Chain(pool, s_pool)

            def step(s, u):
                if comb and has(s):
                    comb.pool_gather(pool, chain, s, u)
                if route and has(s - 1):
                    route.norm.pool_rstd(pool, s - 1, 1 - u)
                if route and has(s - 2):
                    route.pool_scatter(pool, chain, s - 2, u)
                chain.restart()

            pairs_of_steps(pool, 0, 2, BATCHES, BATCHES + 1, step)
            if route:
                route.pool_end(pool)

        @block.vector
        def _(dve):
            link = Chain(dve, s_dve)
            if route:
                route.dve_start(dve, link)
                link.restart()

            def step(s, u):
                if route and has(s - 1):
                    route.norm.dve_stats(dve, link, s - 1, 1 - u)
                if comb and has(s):
                    comb.dve_add(dve, link, s, u)
                if route and has(s - 1):
                    route.dve_norm(dve, s - 1, 1 - u)
                if route and has(s - 2):
                    route.dve_choose(dve, link, s - 2, u, psL[u])
                    route.dve_rows(dve, link, s - 2, u, psP[u])
                link.restart()

            pairs_of_steps(dve, 0, 2, BATCHES, BATCHES + 1, step)
            if route:
                route.dve_end(dve, link)

        @block.tensor
        def _(pe):
            if not route:
                return
            pe.wait_ge(route.s_w, 16)

            def step(s, u):
                if has(s - 1):
                    route.pe_T(pe, s - 1, 1 - u, psT[1 - u])
                if has(s - 2):
                    route.pe_P(pe, s - 2, u, psP[u])
                if has(s - 1):
                    route.pe_L(pe, s - 1, 1 - u, psL[1 - u])

            pairs_of_steps(pe, 1, 2, BATCHES, BATCHES + 1, step)

        @block.scalar
        def _(act):
            if not route:
                return

            def step(s, u):
                route.act_T(act, s, u, psT[u])

            pairs_of_steps(act, 0, 0, BATCHES, BATCHES - 1, step)
            route.act_end(act)

        @block.sync
        def _(sp):
            if route:
                route.sp_load(sp, router)
                route.sp_end(sp)
            if out is not None:
                sp.wait_ge(comb.s_added, BATCHES)
                sp.dma_start(out.rearrange("(n p) d -> p n d", p=P), keep.x[:, :, :]).then_inc(s_out, 16)
                sp.wait_ge(s_out, 16)


def attention_stage(nc, keep, tag, slots_in, slots_out, causal, params, router, router_bias, capacity):
    with ExitStack() as ctx:
        def sb(name, shape, dt):
            return ctx.enter_context(nc.sbuf_tensor(f"{tag}_{name}", shape, dt))

        def pb(name, shape, dt):
            return ctx.enter_context(nc.psum_tensor(f"{tag}_{name}", shape, dt))

        sem = stage_semaphores(nc, ctx, tag)

        QKV = 3 * D
        G = HEADS // 4
        UNITS = 16
        comb = Combine(nc, keep, sb, sem, slots_in)
        route = Route(nc, keep, sb, sem, slots_out, router_bias, capacity)
        norm = Norm(nc, keep, sb, sem, "attn")
        par = sb("par", [P, params.shape[1]], F32)
        wqkv = sb("wqkv", [P, QKV], F32)
        xaT = sb("xaT", [P, SEQ], F32)
        pr = sb("pr", [P, TPB, QKV], F32)
        pt = sb("pt", [P, TPB, QKV], F32)
        pt2 = sb("pt2", [P, TPB, QKV], F32)
        qk = sb("qk", [P, TPB, 2 * D], F32)
        left = sb("left", [P, TPB, 2 * D], F32)
        left2 = sb("left2", [P, TPB, 2 * D], F32)
        hv = sb("hv", [P, 4, TPB * 3 * HEADS], F32)
        ext = [sb(f"ext{u}", [P, TPB, 2, HEADS, XR], BF16) for u in range(2)]
        vx = [sb(f"vx{u}", [P, TPB, HEADS, 32], F32) for u in range(2)]
        QT = [sb(f"QT{u}", [P, HEADS // 2, SEQ], BF16) for u in range(2)]
        KT = [sb(f"KT{u}", [P, HEADS // 2, SEQ], BF16) for u in range(2)]
        QM = sb("QM", [P, HEADS // 2, SEQ], BF16)
        mx = [sb(f"mx{u}", [P, TPB, HEADS], F32) for u in range(2)]
        mleft = sb("mleft", [P, TPB, HEADS], F32)
        PT = sb("PT", [P, 4, 2, SEQ], F32)
        oT = [sb(f"oT{u}", [P, G, SEQ], F32) for u in range(2)]
        den = sb("den", [P, TPB, HEADS], F32)
        o = sb("o", [P, TPB, D], F32)
        onT = sb("onT", [P, SEQ], F32)
        identb = sb("identb", [P, P], BF16)
        psS = [pb(f"psS{n}", [P, 2, SEQ], F32) for n in range(2)]
        psE = [pb(f"psE{n}", [P, 2, SEQ], F32) for n in range(2)]
        psV = [pb(f"psV{n}", [P, 2, SEQ], F32) for n in range(2)]
        psA = pb("psA", [P, 512], F32)
        psD = pb("psD", [P, 512], F32)
        if causal:
            masks = sb("masks", [P, 2, P], BF16)
            cosn = sb("cosn", [P, 2, TPB, 2, 64], F32)
            ang = sb("ang", [P, 6, TPB * 64], F32)
            dec = sb("dec", [P, 6, HEADS], F32)
        s_par = sem("par")
        s_ready = sem("ready")
        s_gpi = sem("sigmoids")
        s_sin = sem("sines")
        s_dve = sem("dve_chain")
        s_pool = sem("pool_chain")
        s_act = sem("act_chain")
        s_xaT_ps = sem("xaT_ps")
        s_xaT = sem("xaT")
        s_proj = sem("proj")
        s_pr = sem("pr")
        s_sq = sem("sq")
        s_hv = sem("hv")
        s_hr = sem("hr")
        s_qk = sem("qk")
        s_v = sem("v")
        s_a = sem("part_a")
        s_l1 = sem("left1")
        s_b = sem("part_b")
        s_l2 = sem("left2")
        s_ext = sem("ext")
        s_X = sem("X")
        s_QK = sem("QK")
        s_S = sem("S")
        s_max = sem("max")
        s_m = sem("m")
        s_Xm = sem("Xm")
        s_QM = sem("QM")
        s_E = sem("E")
        s_e = sem("e")
        s_V = sem("V")
        s_oT = sem("oT")
        s_O = sem("O")
        s_o = sem("o")
        s_OT = sem("OT")
        s_onT = sem("onT")
        s_Y = sem("Y")
        s_x = sem("x")
        block = ctx.enter_context(nc.Block())

        def parts(u, w, g):
            return ext[u][:, :, w, :, g * DH:(g + 1) * DH]

        def both(u, g):
            return ext[u][:, :, :, :, g * DH:(g + 1) * DH].rearrange("p t w h d -> p (t w h) d")

        def flat(buf):
            return buf[:, :, :].rearrange("p t (g d) -> p (t g) d", d=DH)

        def one(buf, w):
            return buf[:, :, w * D:(w + 1) * D].rearrange("p t (h d) -> p t h d", d=DH)

        def unit_b(c):
            return c // 8, (c % 8) // 2, c % 2

        def unit_c(c):
            return c // 4, (c // 2) % 2, c % 2

        @block.sync
        def _(sp):
            sp.dma_start(par[:, :], params).then_inc(s_par, 16)
            route.sp_load(sp, router)
            route.sp_end(sp)

        @block.gpsimd
        def _(pool):
            chain = Chain(pool, s_pool)

            def head_prep(b):
                if causal:
                    pool.wait_ge(s_pr, TPB * (b + 1))
                    wait(pool, s_ext, b)
                    pairs = pr[:, :, 0:2 * D].rearrange("p t (f two) -> p t f two", two=2)
                    even, odd = pairs[:, :, :, 0], pairs[:, :, :, 1]
                    c, s = (cosn[:, n, :, :, :].rearrange("p t w f -> p t (w f)") for n in range(2))
                    w = [pt[:, :, n * D:(n + 1) * D] for n in range(3)] + [pt2[:, :, 0:D]]
                    dst = qk[:, :, :].rearrange("p t (f two) -> p t f two", two=2)
                    nc.gpsimd.tensor_tensor(w[0], even, c, ALU.mult).then_inc(s_pool, 1)
                    nc.gpsimd.tensor_tensor(w[1], odd, s, ALU.mult).then_inc(s_pool, 1)
                    nc.gpsimd.tensor_tensor(w[2], even, s, ALU.mult).then_inc(s_pool, 1)
                    chain.n += 3
                    chain(nc.gpsimd.tensor_tensor(w[3], odd, c, ALU.mult))
                    nc.gpsimd.tensor_tensor(dst[:, :, :, 0], w[0], w[1], ALU.subtract).then_inc(s_qk, 1)
                    nc.gpsimd.tensor_tensor(dst[:, :, :, 1], w[2], w[3], ALU.add).then_inc(s_qk, 1)
                else:
                    pool.wait_ge(s_pr, TPB * (b + 1))
                    nc.gpsimd.tensor_tensor(pt[:, :, :], pr[:, :, :], pr[:, :, :], ALU.mult).then_inc(s_sq, 1)
                    pool.wait_ge(s_hv, b + 1)
                    nc.gpsimd.tensor_tensor(hv[:, 2, :], hv[:, 1, :], keep.neg_half[:, :], ALU.pow).then_inc(s_hr, 1)
                    pool.wait_ge(s_hr, b + 1)
                    chain(nc.gpsimd.tensor_tensor(
                        pt2[:, :, :].rearrange("p t (h d) -> p (t h) d", d=DH),
                        pr[:, :, :].rearrange("p t (h d) -> p (t h) d", d=DH),
                        hv[:, 2, :].unsqueeze(2).to_broadcast([P, TPB * 3 * HEADS, DH]), ALU.mult))
                    chain(nc.gpsimd.tensor_tensor(
                        pt[:, :, :], pt2[:, :, :],
                        par[:, SC0:SC0 + QKV].unsqueeze(1).to_broadcast([P, TPB, QKV]), ALU.mult))
                    wait(pool, s_ext, b)
                    nc.gpsimd.tensor_tensor(
                        qk[:, :, :], pt[:, :, 0:2 * D],
                        par[:, SB0:SB0 + 2 * D].unsqueeze(1).to_broadcast([P, TPB, 2 * D]), ALU.add).then_inc(s_qk, 2)

            def rest(b, u):
                pool.wait_ge(s_a, b + 1)
                nc.gpsimd.tensor_tensor(flat(left), flat(qk), both(u, 0), ALU.subtract).then_inc(s_l1, 1)
                pool.wait_ge(s_b, b + 1)
                nc.gpsimd.tensor_tensor(flat(left2), flat(left), both(u, 4), ALU.subtract).then_inc(s_l2, 1)

            def step(s, u):
                if has(s + 1):
                    if isinstance(s, int) and s == -1:
                        comb.pool_gather(pool, chain, 0, 0)
                    norm.pool_rstd(pool, s + 1, 1 - u)
                if has(s - 2):
                    route.norm.pool_rstd(pool, s - 2, u)
                if has(s + 2):
                    comb.pool_gather(pool, chain, s + 2, u)
                if has(s + 1):
                    head_prep(s + 1)
                    rest(s + 1, 1 - u)
                if has(s - 2):
                    route.pool_scatter(pool, chain, s - 2, u)
                chain.restart()

            pool.wait_ge(s_ready, 1)
            pairs_of_steps(pool, -1, 2, 14, 17, step)
            route.pool_end(pool)

        @block.vector
        def _(dve):
            link = Chain(dve, s_dve)

            route.dve_start(dve, link)
            for u in range(2):
                nc.vector.memset(ext[u][:, :, :, :, :], 0.0).then_inc(s_dve, 1)
                nc.vector.memset(vx[u][:, :, :, :], 0.0).then_inc(s_dve, 1)
            link.n += 4
            link(nc.vector.tensor_copy(identb[:, :], keep.ident[:, :]))
            for u in range(2):
                nc.vector.memset(ext[u][:, :, 1, :, MAXR:MAXR + 2], 1.0)
                nc.vector.memset(vx[u][:, :, :, DH:DH + 1], 1.0)
            dve.wait_ge(s_par, 16)
            if causal:
                dve.wait_ge(s_gpi, 2)
                link(nc.vector.tensor_scalar(dec[:, 1:3, :], dec[:, 3:5, :], 1.0, None, ALU.add))
                link(nc.vector.reciprocal(dec[:, 3:5, :], dec[:, 1:3, :]))
                link(nc.vector.tensor_tensor(dec[:, 1, :], dec[:, 4, :], dec[:, 0, :], ALU.mult))
                for part in range(3):
                    for u in range(2):
                        for t in range(TPB):
                            ins = nc.vector.tensor_copy(ext[u][:, t, 0, :, DECAY + part], dec[:, 1 + part % 2, :])
                            nc.vector.tensor_copy(ext[u][:, t, 1, :, DECAY + 3 + part], dec[:, 1 + part % 2, :])
                            nc.vector.tensor_copy(ext[u][:, t, 1, :, DECAY + part],
                                                  par[:, POS0 + t:POS0 + t + 1].to_broadcast([P, HEADS]))
                            nc.vector.tensor_scalar(ext[u][:, t, 0, :, DECAY + 3 + part],
                                                    par[:, POS0 + t:POS0 + t + 1].to_broadcast([P, HEADS]),
                                                    -1.0, None, ALU.mult)
                    link(ins)
                    if part < 2:
                        link(nc.vector.tensor_tensor(dec[:, 1 + (part + 1) % 2, :], dec[:, 1 + part % 2, :],
                                                     ext[0][:, 0, 0, :, DECAY + part], ALU.subtract))
                for t in range(TPB):
                    ins = nc.vector.tensor_tensor(
                        ang[:, 0, t * 64:(t + 1) * 64].rearrange("p (h f) -> p h f", f=4),
                        par[:, ANG0 + 4 * t:ANG0 + 4 * t + 4].unsqueeze(1).to_broadcast([P, HEADS, 4]),
                        dec[:, 3, :].unsqueeze(2).to_broadcast([P, HEADS, 4]), ALU.mult)
                link(ins)
                link(nc.vector.tensor_scalar(ang[:, 1, :], ang[:, 0, :], 1 / TWO_PI, ROUNDER, ALU.mult, ALU.add))
                link(nc.vector.tensor_scalar(ang[:, 2, :], ang[:, 1, :], ROUNDER, None, ALU.subtract))
                link(nc.vector.scalar_tensor_tensor(out=ang[:, 1, :], in0=ang[:, 2, :], scalar=-TWO_PI_HI,
                                                    in1=ang[:, 0, :], op0=ALU.mult, op1=ALU.add))
                link(nc.vector.scalar_tensor_tensor(out=ang[:, 3, :], in0=ang[:, 2, :], scalar=-TWO_PI_LO,
                                                    in1=ang[:, 1, :], op0=ALU.mult, op1=ALU.add))
                link(nc.vector.tensor_scalar(ang[:, 0, :], ang[:, 3, :], PI_BELOW, -PI_BELOW, ALU.min, ALU.max))
                link(nc.vector.scalar_tensor_tensor(out=ang[:, 1, :], in0=ang[:, 0, :], scalar=-1.0,
                                                    in1=ang[:, 0, :], op0=ALU.mult, op1=ALU.max))
                nc.vector.tensor_scalar(ang[:, 2, :], ang[:, 1, :], -1.0, HALF_PI, ALU.mult,
                                        ALU.add).then_inc(s_sin, 1)
                dve.wait_ge(s_sin, 3)
                for n in range(2):
                    src = ang[:, 4 + n, :].rearrange("p (t f) -> p t f", t=TPB)
                    nc.vector.tensor_scalar(cosn[:, n, :, 0, :], src, DH ** -0.5, None, ALU.mult)
                    nc.vector.tensor_copy(cosn[:, n, :, 1, :], src)
                nc.vector.tensor_copy(masks[:, :, :].rearrange("p a b -> p (a b)"), par[:, MASK0:MASK0 + 2 * P])
                nc.vector.tensor_copy(wqkv[:, :], par[:, 0:QKV]).then_inc(s_ready, 1)
            else:
                mean = hv[:, :, 0:3 * HEADS]
                for n, col in enumerate((0, BI0)):
                    src = par[:, col:col + QKV].rearrange("p (h d) -> p h d", d=DH)
                    dst = (wqkv[:, :] if n == 0 else par[:, col:col + QKV]).rearrange("p (h d) -> p h d", d=DH)
                    link(nc.vector.tensor_reduce(mean[:, 0, :], src, AX, ALU.add))
                    link(nc.vector.tensor_scalar(mean[:, 1, :], mean[:, 0, :], 1.0 / DH, None, ALU.mult))
                    link(nc.vector.tensor_tensor(
                        dst, src, mean[:, 1, :].unsqueeze(2).to_broadcast([P, 3 * HEADS, DH]), ALU.subtract))
                link(nc.vector.tensor_scalar(par[:, SC0:SC0 + D], par[:, SC0:SC0 + D], DH ** -0.5, None, ALU.mult))
                nc.vector.tensor_scalar(par[:, SB0:SB0 + D], par[:, SB0:SB0 + D], DH ** -0.5, None,
                                        ALU.mult).then_inc(s_ready, 1)
            dve.wait_ge(s_ready, 1)
            link.restart()

            def project_out(b, t):
                dve.wait_ge(s_proj, TPB * b + t + 1)
                if t == 0:
                    wait(dve, s_v, b)
                nc.vector.tensor_tensor(pr[:, t, :], psA[:, 0:QKV], par[:, BI0:BI0 + QKV], ALU.add).then_inc(s_pr, 1)

            def head_var(b):
                dve.wait_ge(s_sq, b + 1)
                link(nc.vector.tensor_reduce(
                    hv[:, 0, :], pt[:, :, :].rearrange("p t (h d) -> p (t h) d", d=DH), AX, ALU.add))
                nc.vector.tensor_scalar(hv[:, 1, :], hv[:, 0, :], 1.0 / DH, QK_EPS, ALU.mult, ALU.add).then_inc(s_hv, 1)

            def values_out(b, u):
                wait(dve, s_V, UNITS * (b - 1))
                dve.wait_ge(s_qk, 2 * (b + 1))
                nc.vector.tensor_tensor(
                    vx[u][:, :, :, 0:DH], pt[:, :, 2 * D:QKV].rearrange("p t (h d) -> p t h d", d=DH),
                    par[:, SB0 + 2 * D:SB0 + QKV].rearrange("p (h d) -> p h d", d=DH).unsqueeze(1)
                    .to_broadcast([P, TPB, HEADS, DH]), ALU.add).then_inc(s_v, 1)

            def split_a(b, u):
                dve.wait_ge(s_qk, 2 * (b + 1))
                wait(dve, s_Xm, TPB * (b - 1))
                nc.vector.tensor_copy(both(u, 0), flat(qk)).then_inc(s_a, 1)
                dve.wait_ge(s_a, b + 1)
                nc.vector.tensor_copy(parts(u, 1, 1), parts(u, 1, 0))
                nc.vector.tensor_copy(parts(u, 1, 2), parts(u, 1, 0))
                nc.vector.tensor_copy(parts(u, 0, 3), parts(u, 0, 0))
                nc.vector.tensor_copy(parts(u, 0, 5), parts(u, 0, 0))

            def split_b(b, u):
                dve.wait_ge(s_l1, b + 1)
                nc.vector.tensor_copy(both(u, 4), flat(left)).then_inc(s_b, 1)
                dve.wait_ge(s_b, b + 1)
                nc.vector.tensor_copy(parts(u, 0, 1), parts(u, 0, 4))
                nc.vector.tensor_copy(parts(u, 1, 3), parts(u, 1, 4))

            def split_c(b, u):
                dve.wait_ge(s_l2, b + 1)
                nc.vector.tensor_copy(parts(u, 0, 2), one(left2, 0))
                nc.vector.tensor_copy(parts(u, 1, 5), one(left2, 1)).then_inc(s_ext, 1)

            def operands_out(b, u, n):
                t, w = n // 2, n % 2
                dve.wait_ge(s_X, 4 * b + n + 1)
                dst = (QT, KT)[w][u][:, :, t * P:(t + 1) * P].bitcast(U32)
                nc.vector.tensor_copy(dst, psA[:, :].bitcast(U32).rearrange("p (k q) -> p k q", k=8)).then_inc(s_QK, 1)

            def unit_max(b, u, c):
                t, g, r = unit_b(c)
                cols = P if causal and t == 0 else SEQ
                dve.wait_ge(s_S, UNITS * b + c + 1)
                nc.vector.tensor_reduce(mx[u][:, t, 4 * g + r:4 * g + r + 3:2], psS[c % 2][:, :, 0:cols],
                                        AX, ALU.max).then_inc(s_max, 1)

            def max_rows(b, u):
                dve.wait_ge(s_max, UNITS * (b + 1))
                dst = [ext[u][:, :, 0, :, MAXR + n] for n in range(2)]
                link(nc.vector.tensor_scalar(dst[0], mx[u][:, :, :], -1.0, None, ALU.mult))
                link(nc.vector.scalar_tensor_tensor(out=mleft[:, :, :], in0=mx[u][:, :, :], scalar=-1.0,
                                                    in1=dst[0], op0=ALU.mult, op1=ALU.subtract))
                nc.vector.tensor_copy(dst[1], mleft[:, :, :]).then_inc(s_m, 1)

            def queries_out(b, t):
                dve.wait_ge(s_Xm, TPB * b + t + 1)
                if t == 0:
                    wait(dve, s_E, UNITS * b)
                nc.vector.tensor_copy(QM[:, :, t * P:(t + 1) * P].bitcast(U32),
                                      psD[:, :].bitcast(U32).rearrange("p (k q) -> p k q", k=8)).then_inc(s_QM, 1)

            def weighted_out(b, u, n):
                dve.wait_ge(s_V, UNITS * b + 8 * (n + 1))
                if n == 0:
                    wait(dve, s_O, TPB * (b - 1))
                nc.vector.tensor_copy(oT[u][:, 2 * n:2 * n + 2, :], psV[n][:, :, :]).then_inc(s_oT, 1)

            def divide(b, t):
                dve.wait_ge(s_O, TPB * b + t + 1)
                heads = psD[:, :].rearrange("p (h d) -> p h d", d=32)
                if t == 0:
                    wait(dve, s_OT, b)
                link(nc.vector.reciprocal(den[:, t, :].unsqueeze(2), heads[:, :, DH:DH + 1]))
                nc.vector.tensor_tensor(
                    o[:, t, :].rearrange("p (h d) -> p h d", d=DH), heads[:, :, 0:DH],
                    den[:, t, :].unsqueeze(2).to_broadcast([P, HEADS, DH]), ALU.mult).then_inc(s_o, 1)

            def residual(b):
                dve.wait_ge(s_Y, b + 1)
                link(nc.vector.tensor_tensor(
                    keep.x[:, bass.ds(b * TPB, TPB), :], psD[:, 0:SEQ].rearrange("p (t d) -> p t d", t=TPB),
                    keep.x[:, bass.ds(b * TPB, TPB), :], ALU.add))

            def step(s, u):
                v = 1 - u
                a, bb, c, d = has(s + 1), has(s), has(s - 1), has(s - 2)
                if c:
                    queries_out(s - 1, 0)
                    queries_out(s - 1, 1)
                if a:
                    comb.dve_add(dve, link, s + 1, v)
                    norm.dve_stats(dve, link, s + 1, v)
                units = iter(range(UNITS))

                def maxima(k):
                    for _ in range(k):
                        cc = next(units)
                        if bb:
                            unit_max(s, u, cc)

                maxima(1)
                if a:
                    norm.dve_apply(dve, s + 1, v)
                if d:
                    divide(s - 2, 0)
                    divide(s - 2, 1)
                maxima(4)
                if a and not causal:
                    project_out(s + 1, 0)
                if d:
                    residual(s - 2)
                    route.norm.dve_stats(dve, link, s - 2, u)
                maxima(2)
                if a and not causal:
                    project_out(s + 1, 1)
                    head_var(s + 1)
                if d:
                    route.dve_norm(dve, s - 2, u)
                maxima(2)
                if c:
                    weighted_out(s - 1, v, 0)
                if a:
                    split_a(s + 1, v)
                maxima(2)
                if d:
                    route.dve_choose(dve, link, s - 2, u, psD)
                if a:
                    split_b(s + 1, v)
                maxima(2)
                if d:
                    route.dve_rows(dve, link, s - 2, u, psD)
                if a:
                    split_c(s + 1, v)
                maxima(3)
                if c:
                    weighted_out(s - 1, v, 1)
                if a and not causal:
                    values_out(s + 1, v)
                if bb:
                    max_rows(s, u)
                if a:
                    for n in range(4):
                        operands_out(s + 1, v, n)
                link.restart()

            pairs_of_steps(dve, -1, 2, 14, 17, step)
            route.dve_end(dve, link)

        @block.scalar
        def _(act):
            if causal:
                act.wait_ge(s_par, 16)
                nc.scalar.activation(dec[:, 3:5, :], par[:, GATE0:GATE0 + 2 * HEADS].rearrange("p (a h) -> p a h", a=2),
                                     ACT.Exp, scale=-1.0).then_inc(s_gpi, 1)
                nc.scalar.activation(dec[:, 0, :], par[:, XI0:XI0 + HEADS], ACT.Exp, scale=-1.0).then_inc(s_gpi, 1)
                act.wait_ge(s_sin, 1)
                nc.scalar.activation(ang[:, 5, :], ang[:, 0, :], ACT.Sin).then_inc(s_sin, 1)
                nc.scalar.activation(ang[:, 4, :], ang[:, 2, :], ACT.Sin).then_inc(s_sin, 1)

            def tiles_out(b):
                act.wait_ge(s_xaT_ps, b + 1)
                nc.scalar.copy(xaT[:, :], psA[:, 0:SEQ]).then_inc(s_xaT, 1)

            def project_out(b, t):
                act.wait_ge(s_proj, TPB * b + t + 1)
                if t == 0:
                    wait(act, s_qk, 2 * b)
                    wait(act, s_v, b)
                nc.scalar.copy(pr[:, t, :], psA[:, 0:QKV]).then_inc(s_pr, 1)

            def values_out(b, u):
                act.wait_ge(s_pr, TPB * (b + 1))
                wait(act, s_V, UNITS * (b - 1))
                nc.scalar.copy(vx[u][:, :, :, 0:DH],
                               pr[:, :, 2 * D:QKV].rearrange("p t (h d) -> p t h d", d=DH)).then_inc(s_v, 1)

            def unit_exp(b, c):
                g, r, kt = unit_c(c)
                q0 = P if causal and kt else 0
                act.wait_ge(s_E, UNITS * b + c + 1)
                wait(act, s_V, UNITS * b + c - 3)
                nc.scalar.activation(PT[:, c % 4, :, q0:SEQ], psE[c % 2][:, :, q0:SEQ], ACT.Exp).then_inc(s_e, 1)

            def step(s, u):
                a, c, d = has(s + 1), has(s - 1), has(s - 2)
                units = iter(range(UNITS))

                def exps(k):
                    for _ in range(k):
                        cc = next(units)
                        if c:
                            unit_exp(s - 1, cc)

                exps(2)
                if a:
                    tiles_out(s + 1)
                exps(2)
                if d:
                    act.wait_ge(s_OT, s - 2 + 1)
                    nc.scalar.copy(onT[:, :], psD[:, 0:SEQ]).then_inc(s_onT, 1)
                exps(1)
                if a and causal:
                    project_out(s + 1, 0)
                exps(2)
                if a and causal:
                    project_out(s + 1, 1)
                exps(3)
                if d:
                    route.act_T(act, s - 2, u, psD)
                exps(6)
                if a and causal:
                    values_out(s + 1, 1 - u)

            pairs_of_steps(act, -1, 2, 14, 17, step)
            route.act_end(act)

        @block.tensor
        def _(pe):
            pe.wait_ge(s_ready, 1)
            pe.wait_ge(route.s_w, 16)

            def tiles(b, u):
                pe.wait_ge(norm.s_out, b + 1)
                wait(pe, s_QK, 4 * b)
                for t in range(TPB):
                    last = nc.tensor.transpose(psA[:, t * P:(t + 1) * P], norm.out[:, u, t, :], keep.ident[:, :])
                last.then_inc(s_xaT_ps, 1)

            def project(b, t):
                if t == 0:
                    pe.wait_ge(s_xaT, b + 1)
                else:
                    pe.wait_ge(s_pr, TPB * b + t)
                nc.tensor.matmul(psA[:, 0:QKV], xaT[:, t * P:(t + 1) * P], wqkv[:, :],
                                 start=True, stop=True).then_inc(s_proj, 1)

            def operands(b, u, n):
                t, w = n // 2, n % 2
                if n == 0:
                    pe.wait_ge(s_pr, TPB * (b + 1))
                    pe.wait_ge(s_ext, b + 1)
                else:
                    pe.wait_ge(s_QK, 4 * b + n)
                src = ext[u][:, t, w, :, :].rearrange("p h r -> p (h r)")
                dst = psA[:, :].bitcast(BF16)
                for k in range(8):
                    last = nc.tensor.transpose(dst[:, k * P:(k + 1) * P], src[:, k * P:(k + 1) * P], identb[:, :])
                last.then_inc(s_X, 1)

            def unit_scores(b, u, c):
                t, g, r = unit_b(c)
                cols = P if causal and t == 0 else SEQ
                if c == 0:
                    pe.wait_ge(s_QK, 4 * (b + 1))
                wait(pe, s_max, UNITS * b + c - 1)
                if causal:
                    nc.tensor.matmul(psS[c % 2][:, :, t * P:(t + 1) * P], identb[:, :],
                                     masks[:, 0, :].unsqueeze(1).to_broadcast([P, 2, P]), start=True, stop=False,
                                     skip_group_check=True)
                for hh in range(2):
                    k = 2 * g + hh
                    last = nc.tensor.matmul(
                        psS[c % 2][:, hh, 0:cols], QT[u][64 * r:64 * r + MAXR, k, t * P:(t + 1) * P],
                        KT[u][64 * r:64 * r + MAXR, k, 0:cols], start=not causal, stop=True, skip_group_check=True)
                last.then_inc(s_S, 1)

            def queries(b, u, t):
                if t == 0:
                    pe.wait_ge(s_m, b + 1)
                    wait(pe, route.s_A, b - 1)
                else:
                    pe.wait_ge(s_QM, TPB * b + 1)
                src = ext[u][:, t, 0, :, :].rearrange("p h r -> p (h r)")
                dst = psD[:, :].bitcast(BF16)
                for k in range(8):
                    last = nc.tensor.transpose(dst[:, k * P:(k + 1) * P], src[:, k * P:(k + 1) * P], identb[:, :])
                last.then_inc(s_Xm, 1)

            def unit_e(b, u, c):
                g, r, kt = unit_c(c)
                q0 = P if causal and kt else 0
                if c == 0:
                    pe.wait_ge(s_QM, TPB * (b + 1))
                wait(pe, s_e, UNITS * b + c - 1)
                if causal:
                    nc.tensor.matmul(psE[c % 2][:, :, kt * P:(kt + 1) * P], identb[:, :],
                                     masks[:, 1, :].unsqueeze(1).to_broadcast([P, 2, P]), start=True, stop=False,
                                     skip_group_check=True)
                for hh in range(2):
                    k = 2 * g + hh
                    last = nc.tensor.matmul(
                        psE[c % 2][:, hh, q0:SEQ], KT[u][64 * r:64 * r + MAXR + 2, k, kt * P:(kt + 1) * P],
                        QM[64 * r:64 * r + MAXR + 2, k, q0:SEQ], start=not causal, stop=True, skip_group_check=True)
                last.then_inc(s_E, 1)

            def unit_v(b, u, c):
                g, r, kt = unit_c(c)
                q0 = P if causal and kt else 0
                pe.wait_ge(s_e, UNITS * b + c + 1)
                if c == 0:
                    pe.wait_ge(s_v, b + 1)
                if c % 8 == 0:
                    wait(pe, s_oT, 2 * b - 1 + c // 8)
                for hh in range(2):
                    head, quad = 4 * g + 2 * hh + r, 2 * hh + r
                    last = nc.tensor.matmul(
                        psV[g // 2][32 * quad:32 * quad + 32, g % 2, q0:SEQ], vx[u][:, kt, head, :],
                        PT[:, c % 4, hh, q0:SEQ], start=(kt == 0), stop=(kt == 1), skip_group_check=True,
                        tile_position=(0, 32 * quad))
                last.then_inc(s_V, 1)

            def back(b, u, t):
                if t == 0:
                    pe.wait_ge(s_oT, 2 * (b + 1))
                    if has(b + 1):
                        pe.wait_ge(s_QM, TPB * (b + 2))
                else:
                    pe.wait_ge(s_o, TPB * b + 1)
                for g in range(G):
                    last = nc.tensor.transpose(psD[:, g * P:(g + 1) * P], oT[u][:, g, t * P:(t + 1) * P], keep.ident[:, :])
                last.then_inc(s_O, 1)

            def divided(b):
                pe.wait_ge(s_o, TPB * (b + 1))
                for t in range(TPB):
                    last = nc.tensor.transpose(psD[:, t * P:(t + 1) * P], o[:, t, :], keep.ident[:, :])
                last.then_inc(s_OT, 1)

            def output(b):
                pe.wait_ge(s_onT, b + 1)
                for t in range(TPB):
                    last = nc.tensor.matmul(psD[:, t * P:(t + 1) * P], onT[:, t * P:(t + 1) * P],
                                            par[:, WO0:WO0 + D], start=True, stop=causal)
                    if not causal:
                        last = nc.tensor.matmul(psD[:, t * P:(t + 1) * P], par[0:1, ONE0:ONE0 + P],
                                                par[0:1, BO0:BO0 + D], start=False, stop=True)
                last.then_inc(s_Y, 1)

            def step(s, u):
                v = 1 - u
                a, bb, c, d = has(s + 1), has(s), has(s - 1), has(s - 2)
                if c:
                    queries(s - 1, v, 0)
                if bb:
                    unit_scores(s, u, 0)
                    unit_scores(s, u, 1)
                if c:
                    queries(s - 1, v, 1)
                for n in range(UNITS):
                    if c:
                        unit_e(s - 1, v, n)
                        if n >= 1:
                            unit_v(s - 1, v, n - 1)
                    if n == 0 and d:
                        back(s - 2, u, 0)
                    if n == 1 and d:
                        back(s - 2, u, 1)
                    if n == 2 and a:
                        tiles(s + 1, v)
                    if n == 3 and d:
                        divided(s - 2)
                    if n == 4 and a:
                        project(s + 1, 0)
                    if n == 6 and a:
                        project(s + 1, 1)
                    if n == 5 and d:
                        output(s - 2)
                    if n == 9 and d:
                        route.pe_T(pe, s - 2, u, psD)
                    if n == 11 and d:
                        route.pe_L(pe, s - 2, u, psD)
                    if n == 13 and d:
                        route.pe_P(pe, s - 2, u, psD)
                    if bb and n < 14:
                        unit_scores(s, u, n + 2)
                if c:
                    unit_v(s - 1, v, 15)
                if a:
                    for n in range(4):
                        operands(s + 1, v, n)

            pairs_of_steps(pe, -1, 2, 14, 17, step)


def expert_stage(nc, keep, tag, slots_in, slots_out, packed, gated):
    HID = 2 if gated else 4
    WCOLS = packed.shape[2]
    DOWN0 = UP
    B1 = UP + HID * D
    B2 = B1 + UP // P
    with ExitStack() as ctx:
        def sb(name, shape, dt):
            return ctx.enter_context(nc.sbuf_tensor(f"{tag}_{name}", shape, dt))

        def pb(name, shape, dt):
            return ctx.enter_context(nc.psum_tensor(f"{tag}_{name}", shape, dt))

        sem = stage_semaphores(nc, ctx, tag)

        U = 2
        S = ROWS // P
        w = sb("w", [P, U, WCOLS], F32)
        rows = sb("rows", [P, U, S, D], F32)
        rowsT = sb("rowsT", [P, U, ROWS], F32)
        hT = sb("hT", [P, U, HID, ROWS], F32)
        sg = sb("sg", [P, U, HID, ROWS], F32)
        y = sb("y", [P, U, S, D], F32)
        psT = pb("psT", [P, U, 256], F32)
        psH = [pb(f"psH{u}", [P, 4, ROWS], F32) for u in range(U)]
        psY = [pb(f"psY{u}", [P, 512], F32) for u in range(U)]
        s_w = [sem(f"w{u}") for u in range(U)]
        s_rows = [sem(f"rows{u}") for u in range(U)]
        s_T = sem("T")
        s_rT = sem("rT")
        s_H = sem("H")
        s_sg = sem("sg")
        s_h = sem("h")
        s_Y = sem("Y")
        s_y = sem("y")
        s_st = [sem(f"st{u}") for u in range(U)]
        block = ctx.enter_context(nc.Block())
        turns = MOE_TILES // U

        def row_view(dram, r):
            return dram[bass.ds(r, ROWS), :].rearrange("(p s) d -> p (s d)", p=P)

        @block.sync
        def _(sp):
            def load(i, first):
                for u in range(U):
                    j = i * U + u
                    e = sp.value_load(keep.table[0:1, bass.ds(j, 1), 0], min_val=0, max_val=E - 1)
                    r = sp.value_load(keep.table[0:1, bass.ds(j, 1), 1], min_val=0, max_val=SPARE)
                    if not first:
                        sp.wait_ge(s_y, j - 1)
                    sp.dma_start(w[:, u, :], packed[bass.ds(e, 1), :, :].rearrange("a p n -> (a p) n")).then_inc(s_w[u], 16)
                    sp.dma_start(rows[:, u, :, :].rearrange("p s d -> p (s d)"), row_view(slots_in, r)).then_inc(s_rows[u], 16)

            load(0, True)
            with sp.Fori(1, turns) as i:
                load(i, False)

        @block.tensor
        def _(pe):
            with pe.Fori(0, turns) as i:
                for u in range(U):
                    j = i * U + u
                    pe.wait_ge(s_rows[u], 16 * (i + 1))
                    for s in range(S):
                        last = nc.tensor.transpose(psT[:, u, s * P:(s + 1) * P], rows[:, u, s, :], keep.ident[:, :])
                    last.then_inc(s_T, 1)
                    pe.wait_ge(s_w[u], 16 * (i + 1))
                    pe.wait_ge(s_rT, j + 1)
                    for c in range(4):
                        last = nc.tensor.matmul(psH[u][:, c, :], w[:, u, c * P:(c + 1) * P], rowsT[:, u, :],
                                                start=True, stop=True)
                    last.then_inc(s_H, 1)
                    pe.wait_ge(s_h, j + 1)
                    for s in range(S):
                        for c in range(HID):
                            last = nc.tensor.matmul(
                                psY[u][:, s * D:(s + 1) * D], hT[:, u, c, s * P:(s + 1) * P],
                                w[:, u, DOWN0 + c * D:DOWN0 + (c + 1) * D], start=(c == 0), stop=(c == HID - 1))
                    last.then_inc(s_Y, 1)

        @block.scalar
        def _(act):
            with act.Fori(0, turns) as i:
                for u in range(U):
                    j = i * U + u
                    act.wait_ge(s_H, j + 1)
                    if gated:
                        for c in range(HID):
                            ins = nc.scalar.activation(sg[:, u, c, :], psH[u][:, c, :], ACT.Silu,
                                                       bias=w[:, u, B1 + c:B1 + c + 1])
                        ins.then_inc(s_sg, 1)
                    else:
                        nc.scalar.activation(hT[:, u, :, :], psH[u][:, :, :], ACT.Gelu).then_inc(s_h, 1)

        @block.vector
        def _(dve):
            with dve.Fori(0, turns) as i:
                for u in range(U):
                    j = i * U + u
                    dve.wait_ge(s_T, j + 1)
                    nc.vector.tensor_copy(rowsT[:, u, :], psT[:, u, :]).then_inc(s_rT, 1)
                    if gated:
                        dve.wait_ge(s_sg, j + 1)
                        for c in range(HID):
                            ins = nc.vector.scalar_tensor_tensor(
                                out=hT[:, u, c, :], in0=psH[u][:, HID + c, :],
                                scalar=w[:, u, B1 + HID + c:B1 + HID + c + 1], in1=sg[:, u, c, :],
                                op0=ALU.add, op1=ALU.mult)
                        ins.then_inc(s_h, 1)
                    dve.wait_ge(s_Y, j + 1)
                    dve.wait_ge(s_st[u], 16 * i)
                    if gated:
                        nc.vector.tensor_tensor(
                            y[:, u, :, :], psY[u][:, 0:S * D].rearrange("p (s d) -> p s d", s=S),
                            w[:, u, B2:B2 + D].unsqueeze(1).to_broadcast([P, S, D]), ALU.add).then_inc(s_y, 1)
                    else:
                        nc.vector.tensor_copy(
                            y[:, u, :, :], psY[u][:, 0:S * D].rearrange("p (s d) -> p s d", s=S)).then_inc(s_y, 1)

        @block.gpsimd
        def _(pool):
            with pool.Fori(0, turns) as i:
                for u in range(U):
                    j = i * U + u
                    pool.wait_ge(s_y, j + 1)
                    pool.dma_start(row_view(slots_out, j * ROWS), y[:, u, :, :].rearrange("p s d -> p (s d)")).then_inc(s_st[u], 16)
            for u in range(U):
                pool.wait_ge(s_st[u], 16 * turns)


def program(nc, a, out):
    with ExitStack() as ctx:
        keep = Persistent(nc, ctx)
        slots_x = nc.dram_tensor("slots_x", (SLOT_ROWS, D), F32, kind="Internal").ap()
        slots_y = nc.dram_tensor("slots_y", (MOE_TILES * ROWS, D), F32, kind="Internal").ap()
        setup_stage(nc, keep, a["x"], a["consts"])
        token_stage(nc, keep, "t0", None, slots_x, a["wg"], False, capacity=True)
        expert_stage(nc, keep, "e0", slots_x, slots_y, a["pack0"], False)
        attention_stage(nc, keep, "a0", slots_y, slots_x, True, a["par0"], a["wg"], False, True)
        expert_stage(nc, keep, "e1", slots_x, slots_y, a["pack0"], False)
        token_stage(nc, keep, "t1", slots_y, slots_x, a["wr"], True)
        expert_stage(nc, keep, "e2", slots_x, slots_y, a["pack1"], True)
        attention_stage(nc, keep, "a1", slots_y, slots_x, False, a["par1"], a["wr"], True, False)
        expert_stage(nc, keep, "e3", slots_x, slots_y, a["pack1"], True)
        token_stage(nc, keep, "t2", slots_y, None, out=out)


def shape_constants():
    import numpy as np
    p = np.arange(P)[:, None]
    cols = [
        np.eye(P), (p < np.arange(P)[None, :]) * 1.0,
        np.broadcast_to(np.arange(E), (P, E)), np.broadcast_to(np.arange(E) * REGION, (P, E)),
        np.broadcast_to(np.arange(TOKENS // ROWS) * ROWS, (P, TOKENS // ROWS)),
        np.broadcast_to(np.arange(MOE_TILES), (P, MOE_TILES)),
    ]
    return np.concatenate(cols, 1).astype(np.float32)


def causal_constants():
    import math
    import numpy as np
    pos = (np.arange(P)[:, None] + P * np.arange(TPB)[None, :]).astype(np.float32)
    freq = np.float32(math.pi) ** (np.float32(1.0) - np.arange(0, DH, 2, dtype=np.float32) / np.float32(DH))
    ang = (pos[:, :, None] * freq.astype(np.float32)).reshape(P, -1)
    above = np.arange(P)[:, None] < np.arange(P)[None, :]
    return np.concatenate([ang, pos, above * MASKED, above.T * MASKED], 1).astype(np.float32)


def kernel(**inputs):
    import numpy as np
    import concourse.bacc as bacc
    from concourse.bass_utils import run_bass_kernel_spmd as run

    f = {k: np.asarray(v) for k, v in inputs.items()}

    def down(w):
        return w.reshape(E, -1, P, D).transpose(0, 2, 1, 3).reshape(E, P, -1)

    def rep(v):
        return np.broadcast_to(v.reshape(1, -1), (P, v.size))

    def per_head(name):
        return np.concatenate([np.tile(f[f"L1_attn_{n}_{name}"], HEADS) for n in "qkv"])

    arrays = {
        "x": f["L0_attn_x"].reshape(TOKENS, D),
        "consts": shape_constants(),
        "wg": np.tile(f["L0_ffn_wg"], (1, 2)),
        "wr": np.concatenate([f["L1_ffn_Wr"], rep(f["L1_ffn_br"])], 1),
        "pack0": np.concatenate([f["L0_ffn_w_gate"], down(f["L0_ffn_w_down"])], 2),
        "pack1": np.concatenate([
            f["L1_ffn_W1"], down(f["L1_ffn_W2"]), f["L1_ffn_b1"].reshape(E, UP // P, P).transpose(0, 2, 1),
            np.broadcast_to(f["L1_ffn_b2"][:, None, :], (E, P, D))], 2),
        "par0": np.concatenate([
            f["L0_attn_Wqkv"].T, f["L0_attn_Wo"].T, rep(f["L0_attn_pi_gate_logit"]), rep(f["L0_attn_e_gate_logit"]),
            rep(f["L0_attn_log_xi"]), causal_constants()], 1),
        "par1": np.concatenate([
            f["L1_attn_Wq"], f["L1_attn_Wk"], f["L1_attn_Wv"], f["L1_attn_Wo"],
            rep(np.concatenate([f["L1_attn_bq"], f["L1_attn_bk"], f["L1_attn_bv"]])),
            rep(per_head("scale")), rep(per_head("bias")), rep(f["L1_attn_bo"]),
            np.ones((P, P), np.float32)], 1),
    }
    nc = bacc.Bacc("TRN2", target_bir_lowering=False, num_devices=1)
    feeds, aps = {}, {}
    for name, v in arrays.items():
        v = np.ascontiguousarray(v)
        feeds[f"in_{name}"] = v
        aps[name] = nc.dram_tensor(f"in_{name}", v.shape, mybir.dt.from_np(v.dtype), kind="ExternalInput").ap()
    out = nc.dram_tensor("out_x", (TOKENS, D), F32, kind="ExternalOutput").ap()
    program(nc, aps, out)
    r = run(nc, [feeds], core_ids=[0])
    return r.results[0]["out_x"].reshape(BATCHES, SEQ, D)
```

```python
import concourse.bass as bass
from concourse import mybir
from concourse.alu_op_type import AluOpType as ALU
from contextlib import ExitStack

F32 = mybir.dt.float32
BF16 = mybir.dt.bfloat16
I32 = mybir.dt.int32
U32 = mybir.dt.uint32
ACT = mybir.ActivationFunctionType
AX = mybir.AxisListType.X

P = 128
D = 128
SEQ = 256
BATCHES = 16
TOKENS = BATCHES * SEQ
TILES = TOKENS // P
TPB = SEQ // P
E = 8
TOPK = 2
CAP = TOPK * TOKENS // E
ROWS = 256
REGION = TOKENS + ROWS
SPARE = E * REGION
SLOT_ROWS = SPARE + ROWS
MOE_TILES = (TOPK * TOKENS + E * (ROWS - 1)) // ROWS
MOE_TILES += MOE_TILES % 2
UP = 512
LN_EPS = 1e-5
HEADS = 16
DH = 8
XR = 64
PROD, DECAY, MAXR = 0, 48, 54
XQ = 2 * HEADS * XR
MASKED = -1e30
QK_EPS = 1e-6
WO0 = 3 * D
BI0 = WO0 + D
SC0 = BI0 + 3 * D
SB0 = SC0 + 3 * D
BO0 = SB0 + 3 * D
ONE0 = BO0 + D
GATE0 = WO0 + D
XI0 = GATE0 + 2 * HEADS
ANG0 = XI0 + HEADS
POS0 = ANG0 + 4 * TPB
MASK0 = POS0 + TPB
TWO_PI = 6.283185307179586
TWO_PI_HI = 6.28125
TWO_PI_LO = TWO_PI - TWO_PI_HI
HALF_PI = TWO_PI / 4
LN2 = 0.6931471805599453
PI_BELOW = 3.1415925
ROUNDER = 1.5 * 2 ** 23


class Persistent:

    def __init__(self, nc, ctx):
        def sb(name, shape, dt):
            return ctx.enter_context(nc.sbuf_tensor(name, shape, dt))

        self.x = sb("x_res", [P, TILES, D], F32)
        self.ident = sb("ident", [P, P], F32)
        self.upper = sb("upper", [P, P], BF16)
        self.ones = sb("ones", [P, P], BF16)
        self.iota_e = sb("iota_e", [P, E], F32)
        self.base = sb("base", [P, E], F32)
        self.iota_rows = sb("iota_rows", [P, TOKENS // ROWS], F32)
        self.iota_tiles = sb("iota_tiles", [P, MOE_TILES], F32)
        self.neg_half = sb("neg_half", [P, 96], F32)
        self.no_rows = sb("no_rows", [P, TPB * TOPK], I32)
        self.zeros = sb("zeros", [P, ROWS // P * D], F32)
        self.rows_all = sb("rows_all", [P, TILES, TOPK], I32)
        self.gates = sb("gates", [P, TILES, TOPK], F32)
        self.table = sb("table", [P, MOE_TILES, 2], I32)
        self.counts = sb("counts", [P, E], I32)


def stage_semaphores(nc, ctx, tag):
    held = []

    def clear():
        nc.clear_and_free_semaphores(held)
        nc.all_engine_barrier()

    ctx.callback(clear)

    def sem(name):
        held.append(nc.alloc_semaphore(f"{tag}_{name}"))
        return held[-1]

    return sem


def setup_stage(nc, keep, x_in, consts):
    with ExitStack() as ctx:
        s_load = stage_semaphores(nc, ctx, "setup")("load")
        f = ctx.enter_context(nc.sbuf_tensor("const_f", [P, consts.shape[1]], F32))
        block = ctx.enter_context(nc.Block())

        @block.sync
        def _(sp):
            sp.dma_start(f[:, :], consts).then_inc(s_load, 16)
            sp.dma_start(keep.x[:, :, :], x_in.rearrange("(n p) d -> p n d", p=P)).then_inc(s_load, 16)
            sp.wait_ge(s_load, 32)

        @block.vector
        def _(dve):
            dve.wait_ge(s_load, 32)
            o = 0
            for dst in (keep.ident, keep.upper, keep.iota_e, keep.base, keep.iota_rows, keep.iota_tiles):
                n = dst.shape[1]
                nc.vector.tensor_copy(dst[:, :], f[:, o:o + n])
                o += n
            nc.vector.memset(keep.ones[:, :], 1.0)
            nc.vector.memset(keep.zeros[:, :], 0.0)
            nc.vector.memset(keep.no_rows[:, :], 0)
            nc.vector.memset(keep.neg_half[:, :], -0.5)


def wait(eng, sem, value):
    if isinstance(value, int) and value <= 0:
        return
    eng.wait_ge(sem, value)


class Chain:

    def __init__(self, eng, sem):
        self.eng, self.sem, self.n = eng, sem, 0

    def __call__(self, ins):
        ins.then_inc(self.sem, 1)
        self.n += 1
        self.eng.wait_ge(self.sem, self.n)

    def with_next(self, ins):
        ins.then_inc(self.sem, 1)
        self.n += 1

    def restart(self):
        self.eng.sem_clear(self.sem)
        self.n = 0


class Combine:

    def __init__(self, nc, keep, sb, sem, slots):
        self.nc, self.keep, self.slots = nc, keep, slots
        K4 = TPB * TOPK
        self.idx0 = sb("idx0", [P, 2, K4], I32)
        self.idx = sb("idx", [P, 2, K4], I32)
        self.got = sb("got", [P, 2, K4, D], F32)
        self.gate = sb("gate_b", [P, 2, K4], F32)
        self.used = sb("used", [P, 2], F32)
        self.s_got = [sem(f"got{u}") for u in range(2)]
        self.s_added = sem("added")

    def pool_gather(self, pool, chain, b, u):
        nc, keep = self.nc, self.keep
        chain(nc.gpsimd.tensor_copy(self.idx0[:, u, :].rearrange("p (t k) -> p t k", t=TPB),
                                    keep.rows_all[:, bass.ds(b * TPB, TPB), :]))
        wait(pool, self.s_added, b - 1)
        chain(nc.gpsimd.tensor_tensor(self.idx[:, u, :], self.idx0[:, u, :], keep.no_rows[:, :], ALU.add))
        for k in range(TPB * TOPK):
            pool.indirect_dma_start(
                self.got[:, u, k, :], None, self.slots,
                bass.IndirectOffsetOnAxis(ap=self.idx[:, u, k:k + 1].bitcast(U32), axis=0),
            ).then_inc(self.s_got[u], 16)

    def dve_add(self, dve, link, b, u):
        nc, keep = self.nc, self.keep
        link(nc.vector.tensor_copy(self.gate[:, u, :].rearrange("p (t k) -> p t k", t=TPB),
                                   keep.gates[:, bass.ds(b * TPB, TPB), :]))
        wait(dve, self.s_got[u], (b - u) * 8 * TPB * TOPK + 16 * TPB * TOPK)
        for k in range(TOPK):
            for t in range(TPB):
                ins = nc.vector.scalar_tensor_tensor(
                    out=keep.x[:, bass.ds(b * TPB + t, 1), :],
                    in0=self.got[:, u, t * TOPK + k, :].unsqueeze(1),
                    scalar=self.gate[:, u, t * TOPK + k:t * TOPK + k + 1],
                    in1=keep.x[:, bass.ds(b * TPB + t, 1), :],
                    op0=ALU.mult, op1=ALU.add)
                (link if t == TPB - 1 else link.with_next)(ins)
        nc.vector.tensor_copy(self.used[:, u:u + 1], self.gate[:, u, 0:1]).then_inc(self.s_added, 1)


class Norm:

    def __init__(self, nc, keep, sb, sem, name, buffers=2):
        self.nc, self.keep, self.n = nc, keep, buffers
        self.stats = sb(f"{name}_stats", [P, 2, TPB, 6], F32)
        self.mv = sb(f"{name}_mv", [P, 2, TPB, 2], F32)
        self.vare = sb(f"{name}_vare", [P, 2, TPB], F32)
        self.rstd = sb(f"{name}_rstd", [P, 2, TPB], F32)
        self.out = sb(f"{name}_out", [P, 2, TPB, D], F32)
        self.s_var = sem(f"{name}_var")
        self.s_rstd = sem(f"{name}_rstd")
        self.s_out = sem(f"{name}_out")

    def dve_stats(self, dve, link, b, u):
        nc = self.nc
        for t in range(TPB):
            (link if t == TPB - 1 else link.with_next)(nc.vector.bn_stats(self.stats[:, u, t, :], self.keep.x[:, bass.ds(b * TPB + t, 1), :]))
        for t in range(TPB):
            (link if t == TPB - 1 else link.with_next)(nc.vector.bn_aggr(self.mv[:, u, t, :], self.stats[:, u, t, :]))
        nc.vector.tensor_scalar(self.vare[:, u, :], self.mv[:, u, :, 1], LN_EPS, None,
                                ALU.add).then_inc(self.s_var, 1)

    def pool_rstd(self, pool, b, u):
        wait(pool, self.s_var, b + 1)
        self.nc.gpsimd.tensor_tensor(self.rstd[:, u, :], self.vare[:, u, :], self.keep.neg_half[:, 0:TPB],
                                     ALU.pow).then_inc(self.s_rstd, 1)

    def dve_apply(self, dve, b, u):
        wait(dve, self.s_rstd, b + 1)
        for t in range(TPB):
            ins = self.nc.vector.tensor_scalar(
                self.out[:, u, t, :].unsqueeze(1), self.keep.x[:, bass.ds(b * TPB + t, 1), :],
                self.mv[:, u, t, 0:1], self.rstd[:, u, t:t + 1], ALU.subtract, ALU.mult)
        ins.then_inc(self.s_out, 1)


class Route:

    def __init__(self, nc, keep, sb, sem, slots, has_bias, capacity):
        self.nc, self.keep, self.slots, self.has_bias, self.capacity = nc, keep, slots, has_bias, capacity
        U = 2
        self.norm = Norm(nc, keep, sb, sem, "route")
        self.xnT = sb("xnT", [P, U, SEQ], F32)
        self.wr = sb("wr", [P, 2 * E], F32)
        self.lg = sb("lg", [P, U, TPB, E], F32)
        self.mx = sb("top", [P, U, TPB, 8], F32)
        self.mi = sb("top_i", [P, U, TPB, 8], U32)
        self.mif = sb("top_f", [P, U, TPB, TOPK], F32)
        self.M = sb("choice", [P, U, TPB, TOPK, E], BF16)
        self.M_all = sb("choice_all", [P, TILES, TOPK, E], BF16)
        self.R = sb("running", [P, TOPK, E], F32)
        self.A = sb("before", [P, U, TPB, TOPK, E], F32)
        self.B = sb("before_sum", [P, U, 2, TPB, E], F32)
        self.prod = sb("picked", [P, U, 2, TPB * TOPK, E], F32)
        self.rows_f = sb("rows_f", [P, U, TPB * TOPK], F32)
        self.rows0 = sb("rows0", [P, U, TPB * TOPK], I32)
        self.rows = sb("rows", [P, U, TPB * TOPK], I32)
        self.loc = sb("loc", [P, TILES, TOPK], F32)
        self.rowx = sb("rowx", [P, TILES, TOPK], F32)
        self.dl = sb("dl", [P, TILES], F32)
        many = TILES * TOPK
        self.shift = sb("shift", [P, 2, many, E], F32)
        self.rowy = sb("rowy", [P, 2, many], F32)
        self.g = sb("g", [P, 6, TILES], F32)
        self.ahead = sb("ahead", [P, TILES, E], F32)
        self.cnt = sb("cnt", [P, 6, E], F32)
        self.cmp = sb("cmp", [P, E, TOKENS // ROWS], F32)
        self.tt = sb("tt", [P, 3, MOE_TILES, E], F32)
        self.tr = sb("tr", [P, 6, MOE_TILES], F32)
        self.s_w = sem("router_w")
        self.s_T = sem("route_T")
        self.s_xnT = sem("route_xnT")
        self.s_L = sem("logits")
        self.s_M = sem("choices")
        self.s_P = sem("prefix")
        self.s_A = sem("prefix_used")
        self.s_rows = sem("row_numbers")
        self.s_scat = [sem(f"scattered{u}") for u in range(U)]
        self.s_dl = sem("logit_gap")
        self.s_exp = sem("gap_exp")
        self.s_counts = sem("counts")
        self.s_zero = sem("tails")

    def sp_load(self, sp, router):
        sp.dma_start(self.wr[:, :], router).then_inc(self.s_w, 16)

    def dve_start(self, dve, link):
        link(self.nc.vector.memset(self.R[:, :, :], 0.0))
        dve.wait_ge(self.s_w, 16)

    def dve_norm(self, dve, b, u):
        wait(dve, self.s_scat[u], (b - u) * 8 * TPB * TOPK)
        self.norm.dve_apply(dve, b, u)

    def pe_T(self, pe, b, u, ps):
        wait(pe, self.norm.s_out, b + 1)
        for t in range(TPB):
            last = self.nc.tensor.transpose(ps[:, t * P:(t + 1) * P], self.norm.out[:, u, t, :], self.keep.ident[:, :])
        last.then_inc(self.s_T, 1)

    def act_T(self, act, b, u, ps):
        act.wait_ge(self.s_T, b + 1)
        self.nc.scalar.copy(self.xnT[:, u, :], ps[:, 0:SEQ]).then_inc(self.s_xnT, 1)

    def pe_L(self, pe, b, u, ps):
        pe.wait_ge(self.s_xnT, b + 1)
        for t in range(TPB):
            last = self.nc.tensor.matmul(ps[:, t * E:(t + 1) * E], self.xnT[:, u, t * P:(t + 1) * P],
                                         self.wr[:, 0:E], start=True, stop=True)
        last.then_inc(self.s_L, 1)

    def dve_choose(self, dve, link, b, u, ps):
        nc, keep = self.nc, self.keep
        dve.wait_ge(self.s_L, b + 1)
        lg = self.lg[:, u, :, :]
        src = ps[:, 0:TPB * E].rearrange("p (t e) -> p t e", t=TPB)
        if self.has_bias:
            link(nc.vector.tensor_tensor(lg, src, self.wr[:, E:2 * E].unsqueeze(1).to_broadcast([P, TPB, E]), ALU.add))
        else:
            link(nc.vector.tensor_copy(lg, src))
        for t in range(TPB):
            (link if t == TPB - 1 else link.with_next)(nc.vector.max(self.mx[:, u, t, :], self.lg[:, u, t, :]))
        for t in range(TPB):
            (link if t == TPB - 1 else link.with_next)(nc.vector.max_index(self.mi[:, u, t, :], self.mx[:, u, t, :], self.lg[:, u, t, :]))
        nc.vector.tensor_tensor(self.dl[:, bass.ds(b * TPB, TPB)], self.mx[:, u, :, 1], self.mx[:, u, :, 0],
                                ALU.subtract).then_inc(self.s_dl, 1)
        link(nc.vector.tensor_copy(self.mif[:, u, :, :], self.mi[:, u, :, 0:TOPK]))
        nc.vector.tensor_tensor(
            self.M[:, u, :, :, :].rearrange("p t k e -> p (t k) e"),
            self.mif[:, u, :, :].rearrange("p t k -> p (t k)").unsqueeze(2).to_broadcast([P, TPB * TOPK, E]),
            keep.iota_e[:, :].unsqueeze(1).to_broadcast([P, TPB * TOPK, E]),
            ALU.is_equal).then_inc(self.s_M, 1)

    def pe_P(self, pe, b, u, ps):
        nc, keep = self.nc, self.keep
        pe.wait_ge(self.s_M, b + 1)
        m = [self.M[:, u, t, :, :].rearrange("p k e -> p (k e)") for t in range(TPB)]
        nc.tensor.matmul(ps[:, 0:16], keep.upper[:, :], m[0], start=True, stop=True)
        nc.tensor.matmul(ps[:, 16:32], keep.upper[:, :], m[1], start=True, stop=False)
        nc.tensor.matmul(ps[:, 16:32], keep.ones[:, :], m[0], start=False, stop=True)
        nc.tensor.matmul(ps[:, 32:48], keep.ones[:, :], m[0], start=True, stop=False)
        nc.tensor.matmul(ps[:, 32:48], keep.ones[:, :], m[1], start=False, stop=True).then_inc(self.s_P, 1)

    def dve_rows(self, dve, link, b, u, ps):
        nc, keep = self.nc, self.keep
        dve.wait_ge(self.s_M, b + 1)
        nc.vector.tensor_copy(self.M_all[:, bass.ds(b * TPB, TPB), :, :], self.M[:, u, :, :, :])
        dve.wait_ge(self.s_P, b + 1)
        link(nc.vector.tensor_tensor(
            self.A[:, u, :, :, :].rearrange("p t k e -> p t (k e)"),
            ps[:, 0:32].rearrange("p (t m) -> p t m", t=TPB),
            self.R[:, :, :].rearrange("p k e -> p (k e)").unsqueeze(1).to_broadcast([P, TPB, TOPK * E]), ALU.add))
        nc.vector.tensor_tensor(
            self.R[:, :, :], ps[:, 32:48].rearrange("p (k e) -> p k e", k=TOPK), self.R[:, :, :],
            ALU.add).then_inc(self.s_A, 1)
        link(nc.vector.tensor_tensor(self.B[:, u, 0, :, :], self.A[:, u, :, 0, :], self.A[:, u, :, 1, :], ALU.add))
        link(nc.vector.tensor_tensor(self.B[:, u, 1, :, :], self.B[:, u, 0, :, :],
                                     keep.base[:, :].unsqueeze(1).to_broadcast([P, TPB, E]), ALU.add))
        m = self.M[:, u, :, :, :]
        nc.vector.tensor_tensor(
            self.prod[:, u, 0, :, :], m.rearrange("p t k e -> p (t k) e"),
            self.A[:, u, :, :, :].rearrange("p t k e -> p (t k) e"), ALU.mult)
        link(nc.vector.tensor_tensor(
            self.prod[:, u, 1, :, :].rearrange("p (t k) e -> p t k e", t=TPB), m,
            self.B[:, u, 1, :, :].unsqueeze(2).to_broadcast([P, TPB, TOPK, E]), ALU.mult))
        nc.vector.tensor_reduce(
            self.loc[:, bass.ds(b * TPB, TPB), :],
            self.prod[:, u, 0, :, :].rearrange("p (t k) e -> p t k e", t=TPB), AX, ALU.add)
        link(nc.vector.tensor_reduce(self.rows_f[:, u, :], self.prod[:, u, 1, :, :], AX, ALU.add))
        nc.vector.tensor_copy(self.rowx[:, bass.ds(b * TPB, TPB), :],
                              self.rows_f[:, u, :].rearrange("p (t k) -> p t k", t=TPB))
        nc.vector.tensor_copy(self.rows0[:, u, :], self.rows_f[:, u, :]).then_inc(self.s_rows, 1)

    def pool_scatter(self, pool, chain, b, u):
        wait(pool, self.s_rows, b + 1)
        chain(self.nc.gpsimd.tensor_tensor(self.rows[:, u, :], self.rows0[:, u, :], self.keep.no_rows[:, :], ALU.add))
        for k in range(TPB * TOPK):
            pool.indirect_dma_start(
                self.slots, bass.IndirectOffsetOnAxis(ap=self.rows[:, u, k:k + 1].bitcast(U32), axis=0),
                self.norm.out[:, u, k // TOPK, :], None).then_inc(self.s_scat[u], 16)

    def pool_end(self, pool):
        for u in range(2):
            pool.wait_ge(self.s_scat[u], 8 * TPB * TOPK * BATCHES)

    def act_end(self, act):
        act.wait_ge(self.s_dl, BATCHES)
        self.nc.scalar.activation(self.g[:, 0, :], self.dl[:, :], ACT.Exp).then_inc(self.s_exp, 1)
        self.clear_tails(act, range(E // 2, E), False)

    def dve_end(self, dve, link):
        nc, keep, g, cnt, tt, tr = self.nc, self.keep, self.g, self.cnt, self.tt, self.tr
        dve.wait_ge(self.s_A, BATCHES)
        nr = TOKENS // ROWS
        link(nc.vector.tensor_tensor(cnt[:, 0, :], self.R[:, 0, :], self.R[:, 1, :], ALU.add))
        nc.vector.tensor_copy(keep.counts[:, :], cnt[:, 0, :]).then_inc(self.s_counts, 1)
        link(nc.vector.tensor_tensor(
            self.cmp[:, :, :], cnt[:, 0, :].unsqueeze(2).to_broadcast([P, E, nr]),
            keep.iota_rows[:, :].unsqueeze(1).to_broadcast([P, E, nr]), ALU.is_gt))
        link(nc.vector.tensor_reduce(cnt[:, 1, :], self.cmp[:, :, :], AX, ALU.add))
        link(nc.vector.memset(cnt[:, 5, :], 1.0))
        link(nc.vector.tensor_tensor_scan(cnt[:, 2, :], cnt[:, 5, :], cnt[:, 1, :], 0.0, ALU.mult, ALU.add))
        link(nc.vector.tensor_tensor(cnt[:, 3, :], cnt[:, 2, :], cnt[:, 1, :], ALU.subtract))
        link(nc.vector.scalar_tensor_tensor(
            out=cnt[:, 4, :], in0=cnt[:, 3, :], scalar=-float(ROWS), in1=keep.base[:, :],
            op0=ALU.mult, op1=ALU.add))
        jt = keep.iota_tiles[:, :].unsqueeze(2).to_broadcast([P, MOE_TILES, E])

        def per_e(row):
            return row.unsqueeze(1).to_broadcast([P, MOE_TILES, E])

        nc.vector.tensor_tensor(tt[:, 0, :, :], per_e(cnt[:, 2, :]), jt, ALU.is_gt)
        link(nc.vector.tensor_tensor(tt[:, 1, :, :], per_e(cnt[:, 3, :]), jt, ALU.is_le))
        link(nc.vector.tensor_tensor(tt[:, 2, :, :], tt[:, 0, :, :], tt[:, 1, :, :], ALU.mult))
        nc.vector.tensor_tensor(tt[:, 0, :, :], tt[:, 2, :, :], per_e(cnt[:, 4, :]), ALU.mult)
        link(nc.vector.tensor_tensor(tt[:, 1, :, :], tt[:, 2, :, :], per_e(keep.iota_e[:, :]), ALU.mult))
        link(nc.vector.tensor_reduce(tr[:, 0:3, :], tt[:, :, :, :], AX, ALU.add))
        nc.vector.tensor_scalar(tr[:, 5, :], tr[:, 2, :], -float(SPARE), float(SPARE), ALU.mult, ALU.add)
        link(nc.vector.scalar_tensor_tensor(
            out=tr[:, 3, :], in0=keep.iota_tiles[:, :], scalar=float(ROWS), in1=tr[:, 2, :],
            op0=ALU.mult, op1=ALU.mult))
        link(nc.vector.tensor_tensor(tr[:, 4, :], tr[:, 3, :], tr[:, 0, :], ALU.add))
        link(nc.vector.tensor_tensor(tr[:, 3, :], tr[:, 4, :], tr[:, 5, :], ALU.add))
        nc.vector.tensor_copy(keep.table[:, :, 0], tr[:, 1, :])
        nc.vector.tensor_copy(keep.table[:, :, 1], tr[:, 3, :])
        many = TILES * TOPK
        link(nc.vector.tensor_tensor(
            self.shift[:, 0, :, :], self.M_all[:, :, :, :].rearrange("p n k e -> p (n k) e"),
            cnt[:, 4, :].unsqueeze(1).to_broadcast([P, many, E]), ALU.mult))
        link(nc.vector.tensor_reduce(self.rowy[:, 0, :], self.shift[:, 0, :, :], AX, ALU.add))
        nc.vector.tensor_tensor(
            keep.rows_all[:, :, :].rearrange("p n k -> p (n k)"),
            self.rowx[:, :, :].rearrange("p n k -> p (n k)"), self.rowy[:, 0, :], ALU.subtract)
        dve.wait_ge(self.s_exp, 1)
        link(nc.vector.tensor_scalar(g[:, 1, :], g[:, 0, :], 1.0, 2.0, ALU.add, ALU.mult))
        link(nc.vector.reciprocal(g[:, 2, :], g[:, 1, :]))
        link(nc.vector.tensor_tensor(g[:, 3, :], g[:, 0, :], g[:, 2, :], ALU.mult))
        if self.capacity:
            link(nc.vector.tensor_tensor(
                self.ahead[:, :, :], self.M_all[:, :, 1, :],
                self.R[:, 0, :].unsqueeze(1).to_broadcast([P, TILES, E]), ALU.mult))
            link(nc.vector.tensor_reduce(g[:, 4, :], self.ahead[:, :, :], AX, ALU.add))
            link(nc.vector.tensor_tensor(g[:, 5, :], g[:, 4, :], self.loc[:, :, 1], ALU.add))
            nc.vector.scalar_tensor_tensor(
                out=keep.gates[:, :, 0], in0=self.loc[:, :, 0], scalar=float(CAP), in1=g[:, 2, :],
                op0=ALU.is_lt, op1=ALU.mult)
            nc.vector.scalar_tensor_tensor(
                out=keep.gates[:, :, 1], in0=g[:, 5, :], scalar=float(CAP), in1=g[:, 3, :],
                op0=ALU.is_lt, op1=ALU.mult)
        else:
            nc.vector.tensor_copy(keep.gates[:, :, 0], g[:, 2, :])
            nc.vector.tensor_copy(keep.gates[:, :, 1], g[:, 3, :])

    def clear_tails(self, eng, experts, spare):
        eng.wait_ge(self.s_counts, 1)
        for e in experts:
            c = eng.value_load(self.keep.counts[0:1, e:e + 1], min_val=0, max_val=TOKENS)
            eng.dma_start(self.slots[bass.ds(c + e * REGION, ROWS), :].rearrange("(p s) d -> p (s d)", p=P),
                          self.keep.zeros[:, :]).then_inc(self.s_zero, 16)
        if spare:
            eng.dma_start(self.slots[SPARE:SPARE + ROWS, :].rearrange("(p s) d -> p (s d)", p=P),
                          self.keep.zeros[:, :]).then_inc(self.s_zero, 16)
        eng.wait_ge(self.s_zero, 16 * (E + 1))

    def sp_end(self, sp):
        self.clear_tails(sp, range(E // 2), True)


def looped_steps(eng, first, lo, hi, last, step, per=2):
    for s in range(first, lo):
        step(s, s % per)
    if hi > lo:
        with eng.Fori(0, (hi - lo) // per) as i:
            for n in range(per):
                step(i * per + (lo + n), (lo + n) % per)
    for s in range(hi, last + 1):
        step(s, s % per)


def has(b, count=BATCHES):
    return not isinstance(b, int) or 0 <= b < count


def token_stage(nc, keep, tag, slots_in, slots_out, router=None, router_bias=False, capacity=False, out=None):
    with ExitStack() as ctx:
        def sb(name, shape, dt):
            return ctx.enter_context(nc.sbuf_tensor(f"{tag}_{name}", shape, dt))

        def pb(name, shape, dt):
            return ctx.enter_context(nc.psum_tensor(f"{tag}_{name}", shape, dt))

        sem = stage_semaphores(nc, ctx, tag)

        comb = Combine(nc, keep, sb, sem, slots_in) if slots_in is not None else None
        route = Route(nc, keep, sb, sem, slots_out, router_bias, capacity) if slots_out is not None else None
        psT = [pb(f"psT{u}", [P, 512], F32) for u in range(2)]
        psL = [pb(f"psL{u}", [P, 512], F32) for u in range(2)]
        psP = [pb(f"psP{u}", [P, 512], F32) for u in range(2)]
        s_dve = sem("dve_chain")
        s_pool = sem("pool_chain")
        s_out = sem("out")
        block = ctx.enter_context(nc.Block())

        @block.gpsimd
        def _(pool):
            chain = Chain(pool, s_pool)

            def step(s, u):
                v = 1 - u
                if route and has(s - 1):
                    route.norm.pool_rstd(pool, s - 1, v)
                if comb and has(s + 1):
                    comb.pool_gather(pool, chain, s + 1, v)
                if route and has(s - 2):
                    route.pool_scatter(pool, chain, s - 2, u)
                chain.restart()

            looped_steps(pool, -1, 3, 15, 17, step)
            if route:
                route.pool_end(pool)

        @block.vector
        def _(dve):
            link = Chain(dve, s_dve)
            if route:
                route.dve_start(dve, link)
                link.restart()

            def step(s, u):
                v = 1 - u
                if comb and has(s):
                    comb.dve_add(dve, link, s, u)
                if route and has(s):
                    route.norm.dve_stats(dve, link, s, u)
                if route and has(s - 2):
                    route.dve_choose(dve, link, s - 2, u, psL[u])
                if route and has(s - 2):
                    route.dve_rows(dve, link, s - 2, u, psP[u])
                if route and has(s - 1):
                    route.dve_norm(dve, s - 1, v)
                link.restart()

            looped_steps(dve, -1, 3, 15, 17, step)
            if route:
                route.dve_end(dve, link)

        @block.tensor
        def _(pe):
            if not route:
                return
            pe.wait_ge(route.s_w, 16)

            def step(s, u):
                v = 1 - u
                if has(s - 2):
                    route.pe_P(pe, s - 2, u, psP[u])
                if has(s - 1):
                    route.pe_T(pe, s - 1, v, psT[v])
                    route.pe_L(pe, s - 1, v, psL[v])

            looped_steps(pe, 1, 3, 15, 17, step)

        @block.scalar
        def _(act):
            if not route:
                return

            def step(s, u):
                route.act_T(act, s, u, psT[u])

            looped_steps(act, 0, 0, BATCHES, BATCHES - 1, step)
            route.act_end(act)

        @block.sync
        def _(sp):
            if route:
                route.sp_load(sp, router)
                route.sp_end(sp)
            if out is not None:
                with sp.Fori(0, BATCHES) as b:
                    sp.wait_ge(comb.s_added, b + 1)
                    sp.dma_start(out[bass.ds(b * SEQ, SEQ), :].rearrange("(t p) d -> p t d", p=P),
                                 keep.x[:, bass.ds(b * TPB, TPB), :]).then_inc(s_out, 16)
                sp.wait_ge(s_out, 16 * BATCHES)


def attention_stage(nc, keep, tag, slots_in, slots_out, causal, params, router, router_bias, capacity):
    with ExitStack() as ctx:
        def sb(name, shape, dt):
            return ctx.enter_context(nc.sbuf_tensor(f"{tag}_{name}", shape, dt))

        def pb(name, shape, dt):
            return ctx.enter_context(nc.psum_tensor(f"{tag}_{name}", shape, dt))

        sem = stage_semaphores(nc, ctx, tag)

        QKV = 3 * D
        G = HEADS // 4
        UNITS = 16
        OPERANDS = ((0, 0), (1, 0), (0, 1), (1, 1))
        comb = Combine(nc, keep, sb, sem, slots_in)
        route = Route(nc, keep, sb, sem, slots_out, router_bias, capacity)
        norm = Norm(nc, keep, sb, sem, "attn")
        par = sb("par", [P, params.shape[1]], F32)
        wqkv = sb("wqkv", [P, QKV], F32)
        xaT = sb("xaT", [P, SEQ], F32)
        pr = sb("pr", [P, 2, TPB, QKV], F32)
        pt = sb("pt", [P, 2, TPB, QKV], F32)
        pt2 = sb("pt2", [P, TPB, QKV], F32)
        qk = sb("qk", [P, TPB, 2 * D], F32)
        left = sb("left", [P, TPB, 2 * D], F32)
        left2 = sb("left2", [P, TPB, 2 * D], F32)
        hv = sb("hv", [P, 8, TPB * 3 * HEADS], F32)
        ext = [sb(f"ext{u}", [P, TPB, 2, HEADS, XR], BF16) for u in range(2)]
        vx = [sb(f"vx{u}", [P, TPB, HEADS, 32], F32) for u in range(2)]
        QT = [sb(f"QT{u}", [P, HEADS // 2, SEQ], BF16) for u in range(2)]
        KT = [sb(f"KT{u}", [P, HEADS // 2, SEQ], BF16) for u in range(2)]
        QM = sb("QM", [P, HEADS // 2, SEQ], BF16)
        mx = [sb(f"mx{u}", [P, TPB, HEADS], F32) for u in range(2)]
        mleft = sb("mleft", [P, TPB, HEADS], F32)
        PT = sb("PT", [P, 4, 2, SEQ], F32)
        oT = [sb(f"oT{u}", [P, G, SEQ], F32) for u in range(2)]
        den = sb("den", [P, TPB, HEADS], F32)
        o = sb("o", [P, TPB, D], F32)
        onT = sb("onT", [P, SEQ], F32)
        identb = sb("identb", [P, P], BF16)
        psS = [pb(f"psS{n}", [P, 2, SEQ], F32) for n in range(2)]
        psE = [pb(f"psE{n}", [P, 2, SEQ], F32) for n in range(2)]
        psV = [pb(f"psV{n}", [P, 2, SEQ], F32) for n in range(2)]
        psA = pb("psA", [P, 512], F32)
        psD = pb("psD", [P, 512], F32)
        back_bank, first_bank = (psV[n][:, :, :].rearrange("p a q -> p (a q)") for n in (1, 0))
        bank_of = (first_bank, psA, psD, first_bank)
        if causal:
            masks = sb("masks", [P, 2, P], BF16)
            cosn = sb("cosn", [P, 2, TPB, 2, 64], F32)
            ang = sb("ang", [P, 6, TPB * 64], F32)
            dec = sb("dec", [P, 6, HEADS], F32)
        s_par = sem("par")
        s_ready = sem("ready")
        s_gpi = sem("sigmoids")
        s_sin = sem("sines")
        s_dve = sem("dve_chain")
        s_pool = sem("pool_chain")
        s_act = sem("act_chain")
        s_xaT_ps = sem("xaT_ps")
        s_xaT = sem("xaT")
        s_proj = sem("proj")
        s_pr = sem("pr")
        s_sq = sem("sq")
        s_hv = sem("hv")
        s_xb = sem("output_bias")
        s_hn = sem("hn")
        s_hr = sem("hr")
        s_qk = sem("qk")
        s_v = sem("v")
        s_a = sem("part_a")
        s_l1 = sem("left1")
        s_b = sem("part_b")
        s_l2 = sem("left2")
        s_ext = sem("ext")
        s_X = sem("X")
        s_QK = [sem(f"QK{n}") for n in range(4)]
        s_S = sem("S")
        s_max = sem("max")
        s_m = sem("m")
        s_Xm = sem("Xm")
        s_QM = [sem(f"QM{t}") for t in range(TPB)]
        s_E = sem("E")
        s_e = sem("e")
        s_V = sem("V")
        s_oT = [sem(f"oT{n}") for n in range(2)]
        s_O = sem("O")
        s_o = sem("o")
        s_OT = sem("OT")
        s_onT = sem("onT")
        s_Y = sem("Y")
        block = ctx.enter_context(nc.Block())

        def parts(u, w, g):
            return ext[u][:, :, w, :, g * DH:(g + 1) * DH]

        def both(u, g):
            return ext[u][:, :, :, :, g * DH:(g + 1) * DH].rearrange("p t w h d -> p (t w h) d")

        def flat(buf):
            return buf[:, :, :].rearrange("p t (g d) -> p (t g) d", d=DH)

        def one(buf, w):
            return buf[:, :, w * D:(w + 1) * D].rearrange("p t (h d) -> p t h d", d=DH)

        def unit_b(c):
            return c // 8, (c % 8) // 2, c % 2

        def unit_c(c):
            return c // 4, (c // 2) % 2, c % 2

        @block.sync
        def _(sp):
            sp.dma_start(par[:, :], params).then_inc(s_par, 16)
            route.sp_load(sp, router)
            route.sp_end(sp)

        @block.gpsimd
        def _(pool):
            chain = Chain(pool, s_pool)

            def rotate(b, u):
                pool.wait_ge(s_pr, TPB * (b + 1))
                wait(pool, s_a, b)
                pairs = pr[:, u, :, 0:2 * D].rearrange("p t (f two) -> p t f two", two=2)
                even, odd = pairs[:, :, :, 0], pairs[:, :, :, 1]
                c, s = (cosn[:, n, :, :, :].rearrange("p t w f -> p t (w f)") for n in range(2))
                w = [pt[:, 0, :, n * D:(n + 1) * D] for n in range(3)] + [pt2[:, :, 0:D]]
                dst = qk[:, :, :].rearrange("p t (f two) -> p t f two", two=2)
                nc.gpsimd.tensor_tensor(w[0], even, c, ALU.mult).then_inc(s_pool, 1)
                nc.gpsimd.tensor_tensor(w[1], odd, s, ALU.mult).then_inc(s_pool, 1)
                nc.gpsimd.tensor_tensor(w[2], even, s, ALU.mult).then_inc(s_pool, 1)
                chain.n += 3
                chain(nc.gpsimd.tensor_tensor(w[3], odd, c, ALU.mult))
                nc.gpsimd.tensor_tensor(dst[:, :, :, 0], w[0], w[1], ALU.subtract).then_inc(s_qk, 1)
                nc.gpsimd.tensor_tensor(dst[:, :, :, 1], w[2], w[3], ALU.add).then_inc(s_qk, 1)

            def squares(b, u):
                pool.wait_ge(s_pr, TPB * (b + 1))
                nc.gpsimd.tensor_tensor(pt[:, u, :, :], pr[:, u, :, :], pr[:, u, :, :], ALU.mult).then_inc(s_sq, 1)

            def refine(b):
                pool.wait_ge(s_hr, b + 1)
                for n in range(3):
                    chain(nc.gpsimd.tensor_tensor(hv[:, 4, :], hv[:, 3, :], hv[:, 3, :], ALU.mult))
                    chain(nc.gpsimd.tensor_tensor(hv[:, 5, :], hv[:, 4, :], hv[:, 1, :], ALU.mult))
                    chain(nc.gpsimd.tensor_scalar(hv[:, 6, :], hv[:, 5, :], -0.5, 1.5, ALU.mult, ALU.add))
                    if n < 2:
                        chain(nc.gpsimd.tensor_tensor(hv[:, 3, :], hv[:, 6, :], hv[:, 3, :], ALU.mult))
                    else:
                        nc.gpsimd.tensor_tensor(hv[:, 7, :], hv[:, 6, :], hv[:, 3, :], ALU.mult).then_inc(s_hn, 1)

            def scale_heads(b, u):
                pool.wait_ge(s_hn, b + 1)
                chain(nc.gpsimd.tensor_tensor(
                    pt2[:, :, :].rearrange("p t (h d) -> p (t h) d", d=DH),
                    pr[:, u, :, :].rearrange("p t (h d) -> p (t h) d", d=DH),
                    hv[:, 7, :].unsqueeze(2).to_broadcast([P, TPB * 3 * HEADS, DH]), ALU.mult))
                chain(nc.gpsimd.tensor_tensor(
                    pt[:, u, :, :], pt2[:, :, :],
                    par[:, SC0:SC0 + QKV].unsqueeze(1).to_broadcast([P, TPB, QKV]), ALU.mult))
                wait(pool, s_a, b)
                nc.gpsimd.tensor_tensor(
                    qk[:, :, :], pt[:, u, :, 0:2 * D],
                    par[:, SB0:SB0 + 2 * D].unsqueeze(1).to_broadcast([P, TPB, 2 * D]), ALU.add).then_inc(s_qk, 2)

            def output_bias(b):
                nc.gpsimd.tensor_tensor(
                    keep.x[:, bass.ds(b * TPB, TPB), :], keep.x[:, bass.ds(b * TPB, TPB), :],
                    par[:, BO0:BO0 + D].unsqueeze(1).to_broadcast([P, TPB, D]), ALU.add).then_inc(s_xb, 1)

            def left_of_a(b, u):
                pool.wait_ge(s_a, b + 1)
                nc.gpsimd.tensor_tensor(flat(left), flat(qk), both(u, 0), ALU.subtract).then_inc(s_l1, 1)

            def left_of_b(b, u):
                pool.wait_ge(s_b, b + 1)
                nc.gpsimd.tensor_tensor(flat(left2), flat(left), both(u, 4), ALU.subtract).then_inc(s_l2, 1)

            def step(s, u):
                v = 1 - u
                if has(s + 1) and not causal:
                    scale_heads(s + 1, v)
                if has(s + 1):
                    left_of_a(s + 1, v)
                if has(s + 1):
                    left_of_b(s + 1, v)
                if has(s + 3):
                    norm.pool_rstd(pool, s + 3, v)
                if has(s + 4):
                    comb.pool_gather(pool, chain, s + 4, u)
                if has(s + 2) and not causal:
                    squares(s + 2, u)
                if has(s - 3):
                    route.pool_scatter(pool, chain, s - 3, v)
                if has(s - 2):
                    route.norm.pool_rstd(pool, s - 2, u)
                if has(s + 2) and causal:
                    rotate(s + 2, u)
                if has(s + 2) and not causal:
                    refine(s + 2)
                if has(s) and not causal:
                    output_bias(s)
                chain.restart()

            pool.wait_ge(s_ready, 1)
            looped_steps(pool, -4, 4, 12, 18, step)
            route.pool_end(pool)

        @block.vector
        def _(dve):
            link = Chain(dve, s_dve)

            route.dve_start(dve, link)
            for u in range(2):
                nc.vector.memset(ext[u][:, :, :, :, :], 0.0).then_inc(s_dve, 1)
                nc.vector.memset(vx[u][:, :, :, :], 0.0).then_inc(s_dve, 1)
            link.n += 4
            link(nc.vector.tensor_copy(identb[:, :], keep.ident[:, :]))
            for u in range(2):
                nc.vector.memset(ext[u][:, :, 1, :, MAXR:MAXR + 2], 1.0)
                nc.vector.memset(vx[u][:, :, :, DH:DH + 1], 1.0)
            dve.wait_ge(s_par, 16)
            if causal:
                dve.wait_ge(s_gpi, 2)
                link(nc.vector.tensor_scalar(dec[:, 1:3, :], dec[:, 3:5, :], 1.0, None, ALU.add))
                link(nc.vector.reciprocal(dec[:, 3:5, :], dec[:, 1:3, :]))
                link(nc.vector.tensor_tensor(dec[:, 1, :], dec[:, 4, :], dec[:, 0, :], ALU.mult))
                for part in range(3):
                    for u in range(2):
                        for t in range(TPB):
                            ins = nc.vector.tensor_copy(ext[u][:, t, 0, :, DECAY + part], dec[:, 1 + part % 2, :])
                            nc.vector.tensor_copy(ext[u][:, t, 1, :, DECAY + 3 + part], dec[:, 1 + part % 2, :])
                            nc.vector.tensor_copy(ext[u][:, t, 1, :, DECAY + part],
                                                  par[:, POS0 + t:POS0 + t + 1].to_broadcast([P, HEADS]))
                            nc.vector.tensor_scalar(ext[u][:, t, 0, :, DECAY + 3 + part],
                                                    par[:, POS0 + t:POS0 + t + 1].to_broadcast([P, HEADS]),
                                                    -1.0, None, ALU.mult)
                    link(ins)
                    if part < 2:
                        link(nc.vector.tensor_tensor(dec[:, 1 + (part + 1) % 2, :], dec[:, 1 + part % 2, :],
                                                     ext[0][:, 0, 0, :, DECAY + part], ALU.subtract))
                for t in range(TPB):
                    ins = nc.vector.tensor_tensor(
                        ang[:, 0, t * 64:(t + 1) * 64].rearrange("p (h f) -> p h f", f=4),
                        par[:, ANG0 + 4 * t:ANG0 + 4 * t + 4].unsqueeze(1).to_broadcast([P, HEADS, 4]),
                        dec[:, 3, :].unsqueeze(2).to_broadcast([P, HEADS, 4]), ALU.mult)
                link(ins)
                link(nc.vector.tensor_scalar(ang[:, 1, :], ang[:, 0, :], 1 / TWO_PI, ROUNDER, ALU.mult, ALU.add))
                link(nc.vector.tensor_scalar(ang[:, 2, :], ang[:, 1, :], ROUNDER, None, ALU.subtract))
                link(nc.vector.scalar_tensor_tensor(out=ang[:, 1, :], in0=ang[:, 2, :], scalar=-TWO_PI_HI,
                                                    in1=ang[:, 0, :], op0=ALU.mult, op1=ALU.add))
                link(nc.vector.scalar_tensor_tensor(out=ang[:, 3, :], in0=ang[:, 2, :], scalar=-TWO_PI_LO,
                                                    in1=ang[:, 1, :], op0=ALU.mult, op1=ALU.add))
                link(nc.vector.tensor_scalar(ang[:, 0, :], ang[:, 3, :], PI_BELOW, -PI_BELOW, ALU.min, ALU.max))
                link(nc.vector.scalar_tensor_tensor(out=ang[:, 1, :], in0=ang[:, 0, :], scalar=-1.0,
                                                    in1=ang[:, 0, :], op0=ALU.mult, op1=ALU.max))
                nc.vector.tensor_scalar(ang[:, 2, :], ang[:, 1, :], -1.0, HALF_PI, ALU.mult,
                                        ALU.add).then_inc(s_sin, 1)
                dve.wait_ge(s_sin, 3)
                for n in range(2):
                    src = ang[:, 4 + n, :].rearrange("p (t f) -> p t f", t=TPB)
                    nc.vector.tensor_scalar(cosn[:, n, :, 0, :], src, DH ** -0.5, None, ALU.mult)
                    nc.vector.tensor_copy(cosn[:, n, :, 1, :], src)
                nc.vector.tensor_copy(masks[:, :, :].rearrange("p a b -> p (a b)"), par[:, MASK0:MASK0 + 2 * P])
                nc.vector.tensor_copy(wqkv[:, :], par[:, 0:QKV]).then_inc(s_ready, 1)
            else:
                mean = hv[:, :, 0:3 * HEADS]
                for n, col in enumerate((0, BI0)):
                    src = par[:, col:col + QKV].rearrange("p (h d) -> p h d", d=DH)
                    dst = (wqkv[:, :] if n == 0 else par[:, col:col + QKV]).rearrange("p (h d) -> p h d", d=DH)
                    link(nc.vector.tensor_reduce(mean[:, 0, :], src, AX, ALU.add))
                    link(nc.vector.tensor_scalar(mean[:, 1, :], mean[:, 0, :], 1.0 / DH, None, ALU.mult))
                    link(nc.vector.tensor_tensor(
                        dst, src, mean[:, 1, :].unsqueeze(2).to_broadcast([P, 3 * HEADS, DH]), ALU.subtract))
                link(nc.vector.tensor_scalar(par[:, SC0:SC0 + D], par[:, SC0:SC0 + D], DH ** -0.5, None, ALU.mult))
                nc.vector.tensor_scalar(par[:, SB0:SB0 + D], par[:, SB0:SB0 + D], DH ** -0.5, None,
                                        ALU.mult).then_inc(s_ready, 1)
            dve.wait_ge(s_ready, 1)
            link.restart()

            def project_out(b, u, t):
                dve.wait_ge(s_proj, TPB * b + t + 1)
                if t == 0:
                    wait(dve, s_v, b - 1)
                nc.vector.tensor_tensor(pr[:, u, t, :], psA[:, 0:QKV], par[:, BI0:BI0 + QKV], ALU.add).then_inc(s_pr, 1)

            def head_var(b, u):
                dve.wait_ge(s_sq, b + 1)
                wait(dve, s_hn, b)
                link(nc.vector.tensor_reduce(
                    hv[:, 0, :], pt[:, u, :, :].rearrange("p t (h d) -> p (t h) d", d=DH), AX, ALU.add))
                link(nc.vector.tensor_scalar(hv[:, 1, :], hv[:, 0, :], 1.0 / DH, QK_EPS, ALU.mult, ALU.add))
                nc.vector.tensor_scalar(hv[:, 2, :], hv[:, 1, :].bitcast(I32), -0.5 * LN2 / 2 ** 23,
                                        0.5 * LN2 * (127 - 0.043), ALU.mult, ALU.add).then_inc(s_hv, 1)

            def values_out(b, u):
                wait(dve, s_V, UNITS * (b - 1))
                dve.wait_ge(s_qk, 2 * (b + 1))
                nc.vector.tensor_tensor(
                    vx[u][:, :, :, 0:DH], pt[:, u, :, 2 * D:QKV].rearrange("p t (h d) -> p t h d", d=DH),
                    par[:, SB0 + 2 * D:SB0 + QKV].rearrange("p (h d) -> p h d", d=DH).unsqueeze(1)
                    .to_broadcast([P, TPB, HEADS, DH]), ALU.add).then_inc(s_v, 1)

            def split_a(b, u):
                dve.wait_ge(s_qk, 2 * (b + 1))
                wait(dve, s_Xm, TPB * (b - 1))
                nc.vector.tensor_copy(both(u, 0), flat(qk)).then_inc(s_a, 1)
                dve.wait_ge(s_a, b + 1)
                nc.vector.tensor_copy(parts(u, 1, 1), parts(u, 1, 0))
                nc.vector.tensor_copy(parts(u, 1, 2), parts(u, 1, 0))
                nc.vector.tensor_copy(parts(u, 0, 3), parts(u, 0, 0))
                nc.vector.tensor_copy(parts(u, 0, 5), parts(u, 0, 0))

            def split_b(b, u):
                dve.wait_ge(s_l1, b + 1)
                nc.vector.tensor_copy(both(u, 4), flat(left)).then_inc(s_b, 1)
                dve.wait_ge(s_b, b + 1)
                nc.vector.tensor_copy(parts(u, 0, 1), parts(u, 0, 4))
                nc.vector.tensor_copy(parts(u, 1, 3), parts(u, 1, 4))

            def split_c(b, u):
                dve.wait_ge(s_l2, b + 1)
                nc.vector.tensor_copy(parts(u, 0, 2), one(left2, 0))
                nc.vector.tensor_copy(parts(u, 1, 5), one(left2, 1)).then_inc(s_ext, 1)

            def unit_max(b, u, c):
                t, g, r = unit_b(c)
                cols = P if causal and t == 0 else SEQ
                dve.wait_ge(s_S, UNITS * b + c + 1)
                nc.vector.tensor_reduce(mx[u][:, t, 4 * g + r:4 * g + r + 3:2], psS[c % 2][:, :, 0:cols],
                                        AX, ALU.max).then_inc(s_max, 1)

            def max_rows(b, u):
                dve.wait_ge(s_max, UNITS * (b + 1))
                dst = [ext[u][:, :, 0, :, MAXR + n] for n in range(2)]
                link(nc.vector.tensor_scalar(dst[0], mx[u][:, :, :], -1.0, None, ALU.mult))
                link(nc.vector.scalar_tensor_tensor(out=mleft[:, :, :], in0=mx[u][:, :, :], scalar=-1.0,
                                                    in1=dst[0], op0=ALU.mult, op1=ALU.subtract))
                nc.vector.tensor_copy(dst[1], mleft[:, :, :]).then_inc(s_m, 1)

            def queries_out(b):
                dve.wait_ge(s_Xm, TPB * b + 1)
                wait(dve, s_E, UNITS * b)
                nc.vector.tensor_copy(QM[:, :, 0:P].bitcast(U32),
                                      psA[:, :].bitcast(U32).rearrange("p (k q) -> p k q", k=8)).then_inc(s_QM[0], 1)

            def last_operand_out(b, u):
                dve.wait_ge(s_X, 4 * (b + 1))
                wait(dve, s_E, UNITS * (b - 1))
                nc.vector.tensor_copy(KT[u][:, :, P:2 * P].bitcast(U32),
                                      bank_of[3][:, :].bitcast(U32).rearrange("p (k q) -> p k q", k=8)).then_inc(s_QK[3], 1)

            def weighted_out(b, u):
                dve.wait_ge(s_V, UNITS * (b + 1))
                nc.vector.tensor_copy(oT[u][:, 2:4, :], psV[1][:, :, :]).then_inc(s_oT[1], 1)

            def divide(b, t):
                dve.wait_ge(s_O, TPB * b + t + 1)
                heads = back_bank.rearrange("p (h d) -> p h d", d=32)
                if t == 0:
                    wait(dve, s_OT, b)
                link(nc.vector.reciprocal(den[:, t, :].unsqueeze(2), heads[:, :, DH:DH + 1]))
                nc.vector.tensor_tensor(
                    o[:, t, :].rearrange("p (h d) -> p h d", d=DH), heads[:, :, 0:DH],
                    den[:, t, :].unsqueeze(2).to_broadcast([P, HEADS, DH]), ALU.mult).then_inc(s_o, 1)

            def residual(b):
                dve.wait_ge(s_Y, b + 1)
                if not causal:
                    dve.wait_ge(s_xb, b + 1)
                link(nc.vector.tensor_tensor(
                    keep.x[:, bass.ds(b * TPB, TPB), :], psD[:, 0:SEQ].rearrange("p (t d) -> p t d", t=TPB),
                    keep.x[:, bass.ds(b * TPB, TPB), :], ALU.add))

            def step(s, u):
                v = 1 - u
                if has(s - 1):
                    queries_out(s - 1)

                def maxima(lo, hi):
                    for c in range(lo, hi):
                        if has(s):
                            unit_max(s, u, c)

                maxima(0, 1)
                if has(s + 3) and not causal:
                    comb.dve_add(dve, link, s + 3, v)
                maxima(1, 2)
                if has(s + 1) and causal:
                    split_a(s + 1, v)
                if has(s) and not causal:
                    values_out(s, u)
                maxima(2, 3)
                if has(s - 2):
                    divide(s - 2, 0)
                maxima(3, 4)
                if has(s + 3) and causal:
                    comb.dve_add(dve, link, s + 3, v)
                if has(s + 1) and not causal:
                    split_a(s + 1, v)
                maxima(4, 5)
                if has(s - 3):
                    route.dve_choose(dve, link, s - 3, v, psD)
                maxima(5, 6)
                if has(s + 1) and causal:
                    split_b(s + 1, v)
                if has(s + 2) and not causal:
                    project_out(s + 2, u, 0)
                if has(s - 2):
                    divide(s - 2, 1)
                maxima(6, 7)
                if has(s + 3) and causal:
                    norm.dve_stats(dve, link, s + 3, v)
                if has(s + 1) and not causal:
                    split_b(s + 1, v)
                maxima(7, 8)
                if has(s + 3) and not causal:
                    norm.dve_stats(dve, link, s + 3, v)
                maxima(8, 9)
                if has(s + 2) and not causal:
                    project_out(s + 2, u, 1)
                if has(s - 3):
                    route.dve_rows(dve, link, s - 3, v, psD)
                maxima(9, 10)
                if has(s + 1):
                    split_c(s + 1, v)
                maxima(10, 12)
                if has(s - 2):
                    residual(s - 2)
                    route.norm.dve_stats(dve, link, s - 2, u)
                maxima(12, 13)
                if has(s + 2) and not causal:
                    head_var(s + 2, u)
                maxima(13, 16)
                if has(s):
                    max_rows(s, u)
                if has(s + 3):
                    norm.dve_apply(dve, s + 3, v)
                if has(s - 1):
                    weighted_out(s - 1, v)
                if has(s + 1):
                    last_operand_out(s + 1, v)
                if has(s - 2):
                    route.dve_norm(dve, s - 2, u)
                link.restart()

            looped_steps(dve, -4, 4, 12, 18, step)
            route.dve_end(dve, link)

        @block.scalar
        def _(act):
            if causal:
                act.wait_ge(s_par, 16)
                nc.scalar.activation(dec[:, 3:5, :], par[:, GATE0:GATE0 + 2 * HEADS].rearrange("p (a h) -> p a h", a=2),
                                     ACT.Exp, scale=-1.0).then_inc(s_gpi, 1)
                nc.scalar.activation(dec[:, 0, :], par[:, XI0:XI0 + HEADS], ACT.Exp, scale=-1.0).then_inc(s_gpi, 1)
                act.wait_ge(s_sin, 1)
                nc.scalar.activation(ang[:, 5, :], ang[:, 0, :], ACT.Sin).then_inc(s_sin, 1)
                nc.scalar.activation(ang[:, 4, :], ang[:, 2, :], ACT.Sin).then_inc(s_sin, 1)

            def tiles_out(b):
                act.wait_ge(s_xaT_ps, b + 1)
                nc.scalar.copy(xaT[:, :], psA[:, 0:SEQ]).then_inc(s_xaT, 1)

            def project_out(b, u, t):
                act.wait_ge(s_proj, TPB * b + t + 1)
                if t == 0:
                    wait(act, s_qk, 2 * (b - 1))
                    wait(act, s_v, b - 1)
                nc.scalar.copy(pr[:, u, t, :], psA[:, 0:QKV]).then_inc(s_pr, 1)

            def heads_rsqrt(b):
                act.wait_ge(s_hv, b + 1)
                nc.scalar.activation(hv[:, 3, :], hv[:, 2, :], ACT.Exp).then_inc(s_hr, 1)

            def values_out(b, u):
                act.wait_ge(s_pr, TPB * (b + 1))
                wait(act, s_V, UNITS * (b - 1))
                nc.scalar.copy(vx[u][:, :, :, 0:DH],
                               pr[:, u, :, 2 * D:QKV].rearrange("p t (h d) -> p t h d", d=DH)).then_inc(s_v, 1)

            def operands_out(b, u, n):
                t, w = OPERANDS[n]
                act.wait_ge(s_X, 4 * b + n + 1)
                if n == 2:
                    wait(act, s_E, UNITS * (b - 1))
                nc.scalar.copy((QT, KT)[w][u][:, :, t * P:(t + 1) * P],
                               bank_of[n][:, :].bitcast(BF16).rearrange("p (k q) -> p k q", k=8)).then_inc(s_QK[n], 1)

            def queries_out(b):
                act.wait_ge(s_Xm, TPB * (b + 1))
                wait(act, s_E, UNITS * b)
                nc.scalar.copy(QM[:, :, P:2 * P],
                               psD[:, :].bitcast(BF16).rearrange("p (k q) -> p k q", k=8)).then_inc(s_QM[1], 1)

            def weighted_out(b, u):
                act.wait_ge(s_V, UNITS * b + 8)
                nc.scalar.copy(oT[u][:, 0:2, :], psV[0][:, :, :]).then_inc(s_oT[0], 1)

            def divided_out(b):
                act.wait_ge(s_OT, b + 1)
                nc.scalar.copy(onT[:, :], back_bank[:, 0:SEQ]).then_inc(s_onT, 1)

            def unit_exp(b, c):
                g, r, kt = unit_c(c)
                q0 = P if causal and kt else 0
                act.wait_ge(s_E, UNITS * b + c + 1)
                wait(act, s_V, UNITS * b + c - 3)
                nc.scalar.activation(PT[:, c % 4, :, q0:SEQ], psE[c % 2][:, :, q0:SEQ], ACT.Exp).then_inc(s_e, 1)

            def step(s, u):
                v = 1 - u
                if has(s - 1):
                    queries_out(s - 1)

                def exps(lo, hi):
                    for c in range(lo, hi):
                        if has(s - 1):
                            unit_exp(s - 1, c)

                exps(0, 1)
                if has(s - 3):
                    route.act_T(act, s - 3, v, psA)
                exps(1, 3)
                if has(s) and causal:
                    values_out(s, u)
                exps(3, 4)
                if has(s + 2):
                    tiles_out(s + 2)
                exps(4, 6)
                if has(s + 2) and causal:
                    project_out(s + 2, u, 0)
                exps(6, 9)
                if has(s - 2):
                    divided_out(s - 2)
                if has(s + 2) and causal:
                    project_out(s + 2, u, 1)
                exps(9, 10)
                if has(s - 1):
                    weighted_out(s - 1, v)
                exps(10, 13)
                if has(s + 2) and not causal:
                    heads_rsqrt(s + 2)
                exps(13, 14)
                if has(s + 1):
                    operands_out(s + 1, v, 0)
                exps(14, 15)
                exps(15, 16)
                if has(s + 1):
                    operands_out(s + 1, v, 1)
                    operands_out(s + 1, v, 2)

            looped_steps(act, -4, 4, 12, 18, step)
            route.act_end(act)

        @block.tensor
        def _(pe):
            pe.wait_ge(s_ready, 1)
            pe.wait_ge(route.s_w, 16)

            def tiles(b, u):
                pe.wait_ge(norm.s_out, b + 1)
                if has(b - 5):
                    pe.wait_ge(route.s_xnT, b - 4)
                elif has(b - 3):
                    pe.wait_ge(s_QM[0], b - 2)
                elif has(b - 2):
                    pe.wait_ge(s_QK[1], b - 1)
                elif has(b - 1):
                    pe.wait_ge(s_pr, TPB * b)
                for t in range(TPB):
                    last = nc.tensor.transpose(psA[:, t * P:(t + 1) * P], norm.out[:, u, t, :], keep.ident[:, :])
                last.then_inc(s_xaT_ps, 1)

            def project(b, t):
                if t == 0:
                    pe.wait_ge(s_xaT, b + 1)
                else:
                    pe.wait_ge(s_pr, TPB * b + t)
                nc.tensor.matmul(psA[:, 0:QKV], xaT[:, t * P:(t + 1) * P], wqkv[:, :],
                                 start=True, stop=True).then_inc(s_proj, 1)

            def operands(b, u, n):
                t, w = OPERANDS[n]
                if n == 0:
                    if has(b - 2):
                        pe.wait_ge(s_oT[0], b - 1)
                    elif has(b - 1):
                        pe.wait_ge(s_QK[3], b)
                    pe.wait_ge(s_ext, b + 1)
                if n == 1:
                    if has(b + 1):
                        pe.wait_ge(s_pr, TPB * (b + 2))
                    else:
                        pe.wait_ge(route.s_xnT, b - 3)
                if n == 2:
                    if has(b - 3):
                        pe.wait_ge(route.norm.s_var, b - 2)
                    elif has(b - 2):
                        pe.wait_ge(s_QM[1], b - 1)
                    elif has(b - 1):
                        pe.wait_ge(s_QK[2], b)
                if n == 3:
                    pe.wait_ge(s_QK[0], b + 1)
                src = ext[u][:, t, w, :, :].rearrange("p h r -> p (h r)")
                dst = bank_of[n][:, :].bitcast(BF16)
                for k in range(8):
                    last = nc.tensor.transpose(dst[:, k * P:(k + 1) * P], src[:, k * P:(k + 1) * P], identb[:, :])
                last.then_inc(s_X, 1)

            def unit_scores(b, u, c):
                t, g, r = unit_b(c)
                cols = P if causal and t == 0 else SEQ
                if c == 0:
                    for n in (0, 2) if causal else (0, 2, 3):
                        pe.wait_ge(s_QK[n], b + 1)
                if c == 8:
                    for n in (1, 3) if causal else (1,):
                        pe.wait_ge(s_QK[n], b + 1)
                wait(pe, s_max, UNITS * b + c - 1)
                if causal:
                    nc.tensor.matmul(psS[c % 2][:, :, t * P:(t + 1) * P], identb[:, :],
                                     masks[:, 0, :].unsqueeze(1).to_broadcast([P, 2, P]), start=True, stop=False,
                                     skip_group_check=True)
                for hh in range(2):
                    k = 2 * g + hh
                    last = nc.tensor.matmul(
                        psS[c % 2][:, hh, 0:cols], QT[u][64 * r:64 * r + MAXR, k, t * P:(t + 1) * P],
                        KT[u][64 * r:64 * r + MAXR, k, 0:cols], start=not causal, stop=True, skip_group_check=True)
                last.then_inc(s_S, 1)

            def queries(b, u, t):
                if t == 0:
                    pe.wait_ge(s_m, b + 1)
                if has(b + 1):
                    pe.wait_ge(s_QK[1 + t], b + 2)
                elif t == 0:
                    pe.wait_ge(route.s_xnT, b - 2)
                else:
                    pe.wait_ge(route.norm.s_var, b - 1)
                src = ext[u][:, t, 0, :, :].rearrange("p h r -> p (h r)")
                dst = (psA, psD)[t][:, :].bitcast(BF16)
                for k in range(8):
                    last = nc.tensor.transpose(dst[:, k * P:(k + 1) * P], src[:, k * P:(k + 1) * P], identb[:, :])
                last.then_inc(s_Xm, 1)

            def unit_e(b, u, c):
                g, r, kt = unit_c(c)
                q0 = P if causal and kt else 0
                if c == 0:
                    for t in range(TPB):
                        pe.wait_ge(s_QM[t], b + 1)
                wait(pe, s_e, UNITS * b + c - 1)
                if causal:
                    nc.tensor.matmul(psE[c % 2][:, :, kt * P:(kt + 1) * P], identb[:, :],
                                     masks[:, 1, :].unsqueeze(1).to_broadcast([P, 2, P]), start=True, stop=False,
                                     skip_group_check=True)
                for hh in range(2):
                    k = 2 * g + hh
                    last = nc.tensor.matmul(
                        psE[c % 2][:, hh, q0:SEQ], KT[u][64 * r:64 * r + MAXR + 2, k, kt * P:(kt + 1) * P],
                        QM[64 * r:64 * r + MAXR + 2, k, q0:SEQ], start=not causal, stop=True, skip_group_check=True)
                last.then_inc(s_E, 1)

            def unit_v(b, u, c):
                g, r, kt = unit_c(c)
                q0 = P if causal and kt else 0
                pe.wait_ge(s_e, UNITS * b + c + 1)
                if c == 0:
                    pe.wait_ge(s_v, b + 1)
                if c == 0:
                    if has(b + 1):
                        pe.wait_ge(s_QK[3], b + 2)
                    else:
                        pe.wait_ge(s_oT[0], b)
                if c == 8 and has(b - 1):
                    pe.wait_ge(s_onT, b)
                for hh in range(2):
                    head, quad = 4 * g + 2 * hh + r, 2 * hh + r
                    last = nc.tensor.matmul(
                        psV[g // 2][32 * quad:32 * quad + 32, g % 2, q0:SEQ], vx[u][:, kt, head, :],
                        PT[:, c % 4, hh, q0:SEQ], start=(kt == 0), stop=(kt == 1), skip_group_check=True,
                        tile_position=(0, 32 * quad))
                last.then_inc(s_V, 1)

            def back(b, u, t):
                if t == 0:
                    for n in range(2):
                        pe.wait_ge(s_oT[n], b + 1)
                else:
                    pe.wait_ge(s_o, TPB * b + 1)
                for g in range(G):
                    last = nc.tensor.transpose(back_bank[:, g * P:(g + 1) * P], oT[u][:, g, t * P:(t + 1) * P], keep.ident[:, :])
                last.then_inc(s_O, 1)

            def divided(b):
                pe.wait_ge(s_o, TPB * (b + 1))
                for t in range(TPB):
                    last = nc.tensor.transpose(back_bank[:, t * P:(t + 1) * P], o[:, t, :], keep.ident[:, :])
                last.then_inc(s_OT, 1)

            def output(b):
                if has(b - 1):
                    pe.wait_ge(route.s_A, b)
                elif has(b + 1):
                    pe.wait_ge(s_QM[1], b + 2)
                pe.wait_ge(s_onT, b + 1)
                for t in range(TPB):
                    dst = psD[:, t * P:(t + 1) * P]
                    last = nc.tensor.matmul(dst, onT[:, t * P:(t + 1) * P],
                                            par[:, WO0:WO0 + D], start=True, stop=True)
                last.then_inc(s_Y, 1)

            def routed_tiles(b, u):
                if has(b + 2):
                    pe.wait_ge(s_QM[0], b + 3)
                else:
                    pe.wait_ge(route.s_xnT, b)
                route.pe_T(pe, b, u, psA)

            def logits(b, u):
                if has(b + 2):
                    pe.wait_ge(s_QM[1], b + 3)
                else:
                    pe.wait_ge(route.norm.s_var, b + 1)
                route.pe_L(pe, b, u, psD)

            def step(s, u):
                v = 1 - u
                if has(s - 1):
                    queries(s - 1, v, 0)
                    queries(s - 1, v, 1)
                if has(s):
                    unit_scores(s, u, 0)
                    unit_scores(s, u, 1)
                if has(s - 3):
                    routed_tiles(s - 3, v)
                for n in range(UNITS):
                    if has(s - 1):
                        unit_e(s - 1, v, n)
                        if n >= 1:
                            unit_v(s - 1, v, n - 1)
                    if n == 0 and has(s - 2):
                        back(s - 2, u, 0)
                    if n == 2 and has(s + 2):
                        tiles(s + 2, u)
                    if n == 3 and has(s - 3):
                        logits(s - 3, v)
                    if n == 4 and has(s - 2):
                        back(s - 2, u, 1)
                    if n == 4 and has(s + 2):
                        project(s + 2, 0)
                    if n == 6 and has(s - 3):
                        route.pe_P(pe, s - 3, v, psD)
                    if n == 7 and has(s - 2):
                        divided(s - 2)
                    if n == 7 and has(s + 2):
                        project(s + 2, 1)
                    if n == 10 and has(s - 2):
                        output(s - 2)
                    if n == 12 and has(s + 1):
                        operands(s + 1, v, 0)
                    if n == 13 and has(s + 1):
                        operands(s + 1, v, 1)
                    if n == 14 and has(s + 1):
                        operands(s + 1, v, 2)
                    if has(s) and n < 14:
                        unit_scores(s, u, n + 2)
                if has(s - 1):
                    unit_v(s - 1, v, 15)
                if has(s + 1):
                    operands(s + 1, v, 3)

            looped_steps(pe, -4, 4, 12, 18, step)


def expert_stage(nc, keep, tag, slots_in, slots_out, packed, gated):
    HID = 2 if gated else 4
    WCOLS = packed.shape[2]
    DOWN0 = UP
    B1 = UP + HID * D
    B2 = B1 + UP // P
    U = 4
    S = ROWS // P
    with ExitStack() as ctx:
        def sb(name, shape, dt):
            return ctx.enter_context(nc.sbuf_tensor(f"{tag}_{name}", shape, dt))

        def pb(name, shape, dt):
            return ctx.enter_context(nc.psum_tensor(f"{tag}_{name}", shape, dt))

        sem = stage_semaphores(nc, ctx, tag)
        w = sb("w", [P, U, WCOLS], F32)
        rows = sb("rows", [P, U, S, D], F32)
        rowsT = sb("rowsT", [P, 2, ROWS], F32)
        hT = sb("hT", [P, 2, HID, ROWS], F32)
        sg = sb("sg", [P, 2, HID, ROWS], F32)
        y = sb("y", [P, U, S, D], F32)
        psT = pb("psT", [P, 2, 256], F32)
        psH = [pb(f"psH{u}", [P, 4, ROWS], F32) for u in range(2)]
        psY = [pb(f"psY{u}", [P, 512], F32) for u in range(2)]
        s_w = [sem(f"w{u}") for u in range(U)]
        s_rows = [sem(f"rows{u}") for u in range(U)]
        s_T = sem("rows_T")
        s_rT = sem("rows_T_sbuf")
        s_H = sem("hidden")
        s_sg = sem("silu")
        s_h = sem("hidden_sbuf")
        s_Y = sem("result")
        s_y = sem("result_sbuf")
        s_st = [sem(f"stored{u}") for u in range(U)]
        block = ctx.enter_context(nc.Block())

        def row_view(dram, r):
            return dram[bass.ds(r, ROWS), :].rearrange("(p s) d -> p (s d)", p=P)

        @block.sync
        def _(sp):
            def load(j, u, first):
                e = sp.value_load(keep.table[0:1, bass.ds(j, 1), 0], min_val=0, max_val=E - 1)
                r = sp.value_load(keep.table[0:1, bass.ds(j, 1), 1], min_val=0, max_val=SPARE)
                if not first:
                    sp.wait_ge(s_y, j - U + 1)
                sp.dma_start(rows[:, u, :, :].rearrange("p s d -> p (s d)"),
                             row_view(slots_in, r)).then_inc(s_rows[u], 16)
                sp.dma_start(w[:, u, :], packed[bass.ds(e, 1), :, :].rearrange("a p n -> (a p) n")).then_inc(s_w[u], 16)

            for u in range(U):
                load(u, u, True)
            with sp.Fori(1, MOE_TILES // U) as i:
                for u in range(U):
                    load(i * U + u, u, False)

        @block.tensor
        def _(pe):
            def transpose_rows(j, u):
                pe.wait_ge(s_rows[u], (j - u) * (16 // U) + 16)
                for s in range(S):
                    last = nc.tensor.transpose(psT[:, u % 2, s * P:(s + 1) * P], rows[:, u, s, :], keep.ident[:, :])
                last.then_inc(s_T, 1)

            def up(j, u):
                pe.wait_ge(s_w[u], (j - u) * (16 // U) + 16)
                pe.wait_ge(s_rT, j + 1)
                for c in range(4):
                    last = nc.tensor.matmul(psH[u % 2][:, c, :], w[:, u, c * P:(c + 1) * P], rowsT[:, u % 2, :],
                                            start=True, stop=True)
                last.then_inc(s_H, 1)

            def down(j, u):
                pe.wait_ge(s_h, j + 1)
                wait(pe, s_y, j - 1)
                for s in range(S):
                    for c in range(HID):
                        last = nc.tensor.matmul(
                            psY[u % 2][:, s * D:(s + 1) * D], hT[:, u % 2, c, s * P:(s + 1) * P],
                            w[:, u, DOWN0 + c * D:DOWN0 + (c + 1) * D], start=(c == 0), stop=(c == HID - 1))
                last.then_inc(s_Y, 1)

            def step(s, u):
                if has(s + 1, MOE_TILES):
                    up(s + 1, (u + 1) % U)
                if has(s + 2, MOE_TILES):
                    transpose_rows(s + 2, (u + 2) % U)
                if has(s, MOE_TILES):
                    down(s, u)

            looped_steps(pe, -2, 4, 36, 39, step, U)

        @block.scalar
        def _(act):
            with act.Fori(0, MOE_TILES // U) as i:
                for u in range(U):
                    act.wait_ge(s_H, i * U + u + 1)
                    if gated:
                        for c in range(HID):
                            ins = nc.scalar.activation(sg[:, u % 2, c, :], psH[u % 2][:, c, :], ACT.Silu,
                                                       bias=w[:, u, B1 + c:B1 + c + 1])
                        ins.then_inc(s_sg, 1)
                    else:
                        nc.scalar.activation(hT[:, u % 2, :, :], psH[u % 2][:, :, :], ACT.Gelu).then_inc(s_h, 1)

        @block.vector
        def _(dve):
            def step(s, u):
                if has(s + 2, MOE_TILES):
                    dve.wait_ge(s_T, s + 3)
                    nc.vector.tensor_copy(rowsT[:, u % 2, :], psT[:, u % 2, :]).then_inc(s_rT, 1)
                if gated and has(s + 1, MOE_TILES):
                    dve.wait_ge(s_sg, s + 2)
                    v = (u + 1) % U
                    for c in range(HID):
                        ins = nc.vector.scalar_tensor_tensor(
                            out=hT[:, v % 2, c, :], in0=psH[v % 2][:, HID + c, :],
                            scalar=w[:, v, B1 + HID + c:B1 + HID + c + 1], in1=sg[:, v % 2, c, :],
                            op0=ALU.add, op1=ALU.mult)
                    ins.then_inc(s_h, 1)
                if has(s, MOE_TILES):
                    wait(dve, s_st[u], (s - u) * (16 // U))
                    dve.wait_ge(s_Y, s + 1)
                    src = psY[u % 2][:, 0:S * D].rearrange("p (s d) -> p s d", s=S)
                    if gated:
                        nc.vector.tensor_tensor(
                            y[:, u, :, :], src, w[:, u, B2:B2 + D].unsqueeze(1).to_broadcast([P, S, D]),
                            ALU.add).then_inc(s_y, 1)
                    else:
                        nc.vector.tensor_copy(y[:, u, :, :], src).then_inc(s_y, 1)

            looped_steps(dve, -2, 4, 36, 39, step, U)

        @block.gpsimd
        def _(pool):
            with pool.Fori(0, MOE_TILES // U) as i:
                for u in range(U):
                    j = i * U + u
                    pool.wait_ge(s_y, j + 1)
                    pool.dma_start(row_view(slots_out, j * ROWS),
                                   y[:, u, :, :].rearrange("p s d -> p (s d)")).then_inc(s_st[u], 16)
            for u in range(U):
                pool.wait_ge(s_st[u], 16 * (MOE_TILES // U))


def program(nc, a, out):
    with ExitStack() as ctx:
        keep = Persistent(nc, ctx)
        slots_x = nc.dram_tensor("slots_x", (SLOT_ROWS, D), F32, kind="Internal").ap()
        slots_y = nc.dram_tensor("slots_y", (MOE_TILES * ROWS, D), F32, kind="Internal").ap()
        setup_stage(nc, keep, a["x"], a["consts"])
        token_stage(nc, keep, "t0", None, slots_x, a["wg"], False, capacity=True)
        expert_stage(nc, keep, "e0", slots_x, slots_y, a["pack0"], False)
        attention_stage(nc, keep, "a0", slots_y, slots_x, True, a["par0"], a["wg"], False, True)
        expert_stage(nc, keep, "e1", slots_x, slots_y, a["pack0"], False)
        token_stage(nc, keep, "t1", slots_y, slots_x, a["wr"], True)
        expert_stage(nc, keep, "e2", slots_x, slots_y, a["pack1"], True)
        attention_stage(nc, keep, "a1", slots_y, slots_x, False, a["par1"], a["wr"], True, False)
        expert_stage(nc, keep, "e3", slots_x, slots_y, a["pack1"], True)
        token_stage(nc, keep, "t2", slots_y, None, out=out)


def shape_constants():
    import numpy as np
    p = np.arange(P)[:, None]
    cols = [
        np.eye(P), (p < np.arange(P)[None, :]) * 1.0,
        np.broadcast_to(np.arange(E), (P, E)), np.broadcast_to(np.arange(E) * REGION, (P, E)),
        np.broadcast_to(np.arange(TOKENS // ROWS) * ROWS, (P, TOKENS // ROWS)),
        np.broadcast_to(np.arange(MOE_TILES), (P, MOE_TILES)),
    ]
    return np.concatenate(cols, 1).astype(np.float32)


def causal_constants():
    import math
    import numpy as np
    pos = (np.arange(P)[:, None] + P * np.arange(TPB)[None, :]).astype(np.float32)
    freq = np.float32(math.pi) ** (np.float32(1.0) - np.arange(0, DH, 2, dtype=np.float32) / np.float32(DH))
    ang = (pos[:, :, None] * freq.astype(np.float32)).reshape(P, -1)
    above = np.arange(P)[:, None] < np.arange(P)[None, :]
    return np.concatenate([ang, pos, above * MASKED, above.T * MASKED], 1).astype(np.float32)


def kernel(**inputs):
    import numpy as np
    import concourse.bacc as bacc
    from concourse.bass_utils import run_bass_kernel_spmd as run

    f = {k: np.asarray(v) for k, v in inputs.items()}

    def down(w):
        return w.reshape(E, -1, P, D).transpose(0, 2, 1, 3).reshape(E, P, -1)

    def rep(v):
        return np.broadcast_to(v.reshape(1, -1), (P, v.size))

    def per_head(name):
        return np.concatenate([np.tile(f[f"L1_attn_{n}_{name}"], HEADS) for n in "qkv"])

    arrays = {
        "x": f["L0_attn_x"].reshape(TOKENS, D),
        "consts": shape_constants(),
        "wg": np.tile(f["L0_ffn_wg"], (1, 2)),
        "wr": np.concatenate([f["L1_ffn_Wr"], rep(f["L1_ffn_br"])], 1),
        "pack0": np.concatenate([f["L0_ffn_w_gate"], down(f["L0_ffn_w_down"])], 2),
        "pack1": np.concatenate([
            f["L1_ffn_W1"], down(f["L1_ffn_W2"]), f["L1_ffn_b1"].reshape(E, UP // P, P).transpose(0, 2, 1),
            np.broadcast_to(f["L1_ffn_b2"][:, None, :], (E, P, D))], 2),
        "par0": np.concatenate([
            f["L0_attn_Wqkv"].T, f["L0_attn_Wo"].T, rep(f["L0_attn_pi_gate_logit"]), rep(f["L0_attn_e_gate_logit"]),
            rep(f["L0_attn_log_xi"]), causal_constants()], 1),
        "par1": np.concatenate([
            f["L1_attn_Wq"], f["L1_attn_Wk"], f["L1_attn_Wv"], f["L1_attn_Wo"],
            rep(np.concatenate([f["L1_attn_bq"], f["L1_attn_bk"], f["L1_attn_bv"]])),
            rep(per_head("scale")), rep(per_head("bias")), rep(f["L1_attn_bo"]),
            np.ones((P, P), np.float32)], 1),
    }
    nc = bacc.Bacc("TRN2", target_bir_lowering=False, num_devices=1)
    feeds, aps = {}, {}
    for name, v in arrays.items():
        v = np.ascontiguousarray(v)
        feeds[f"in_{name}"] = v
        aps[name] = nc.dram_tensor(f"in_{name}", v.shape, mybir.dt.from_np(v.dtype), kind="ExternalInput").ap()
    out = nc.dram_tensor("out_x", (TOKENS, D), F32, kind="ExternalOutput").ap()
    program(nc, aps, out)
    r = run(nc, [feeds], core_ids=[0])
    return r.results[0]["out_x"].reshape(BATCHES, SEQ, D)
```

```python
import concourse.bass as bass
from concourse import mybir
from concourse.alu_op_type import AluOpType as ALU
from contextlib import ExitStack

F32 = mybir.dt.float32
BF16 = mybir.dt.bfloat16
I32 = mybir.dt.int32
U32 = mybir.dt.uint32
ACT = mybir.ActivationFunctionType
AX = mybir.AxisListType.X

P = 128
D = 128
SEQ = 256
BATCHES = 16
TOKENS = BATCHES * SEQ
TILES = TOKENS // P
TPB = SEQ // P
E = 8
TOPK = 2
CAP = TOPK * TOKENS // E
ROWS = 256
REGION = TOKENS + ROWS
SPARE = E * REGION
SLOT_ROWS = SPARE + ROWS
TILES_HELD = 4
MOE_TILES = (TOPK * TOKENS + E * (ROWS - 1)) // ROWS
MOE_TILES += -MOE_TILES % TILES_HELD
RESULT_ROWS = TOKENS * TOPK + TILES_HELD * ROWS
UP = 512
LN_EPS = 1e-5
HEADS = 16
DH = 8
XR = 64
PROD, DECAY, MAXR = 0, 48, 54
MASKED = -1e30
QK_EPS = 1e-6
WO0 = 3 * D
BI0 = WO0 + D
SC0 = BI0 + 3 * D
SB0 = SC0 + 3 * D
BO0 = SB0 + 3 * D
ONE0 = BO0 + D
GATE0 = WO0 + D
XI0 = GATE0 + 2 * HEADS
ANG0 = XI0 + HEADS
POS0 = ANG0 + 4 * TPB
MASK0 = POS0 + TPB
TWO_PI = 6.283185307179586
TWO_PI_HI = 6.28125
TWO_PI_LO = TWO_PI - TWO_PI_HI
HALF_PI = TWO_PI / 4
LN2 = 0.6931471805599453
PI_BELOW = 3.1415925
ROUNDER = 1.5 * 2 ** 23


class Persistent:

    def __init__(self, nc, ctx):
        def sb(name, shape, dt):
            return ctx.enter_context(nc.sbuf_tensor(name, shape, dt))

        self.x = sb("x_res", [P, TILES, D], F32)
        self.ident = sb("ident", [P, P], F32)
        self.upper = sb("upper", [P, P], BF16)
        self.ones = sb("ones", [P, P], BF16)
        self.iota_e = sb("iota_e", [P, E], F32)
        self.base = sb("base", [P, E], F32)
        self.iota_rows = sb("iota_rows", [P, TOKENS // ROWS], F32)
        self.iota_tiles = sb("iota_tiles", [P, MOE_TILES], F32)
        self.neg_half = sb("neg_half", [P, 96], F32)
        self.no_rows = sb("no_rows", [P, TPB * TOPK], I32)
        self.ids = sb("ids", [P, TILES, TOPK], I32)
        self.pad_ids = sb("pad_ids", [P, TILES_HELD, ROWS // P], I32)
        self.tail = sb("tail", [P, ROWS // P, D + 1], F32)
        self.gates = sb("gates", [P, TILES, TOPK], F32)
        self.table = sb("table", [P, MOE_TILES, 2], I32)
        self.counts = sb("counts", [P, E], I32)


def stage_semaphores(nc, ctx, tag):
    held = []

    def clear():
        nc.clear_and_free_semaphores(held)
        nc.all_engine_barrier()

    ctx.callback(clear)

    def sem(name):
        held.append(nc.alloc_semaphore(f"{tag}_{name}"))
        return held[-1]

    return sem


def setup_stage(nc, keep, x_in, consts):
    with ExitStack() as ctx:
        s_load = stage_semaphores(nc, ctx, "setup")("load")
        f = ctx.enter_context(nc.sbuf_tensor("const_f", [P, consts.shape[1]], F32))
        block = ctx.enter_context(nc.Block())

        @block.sync
        def _(sp):
            sp.dma_start(f[:, :], consts).then_inc(s_load, 16)
            sp.dma_start(keep.x[:, :, :], x_in.rearrange("(n p) d -> p n d", p=P)).then_inc(s_load, 16)
            sp.wait_ge(s_load, 32)

        @block.vector
        def _(dve):
            dve.wait_ge(s_load, 32)
            o = 0
            for dst in (keep.ident, keep.upper, keep.iota_e, keep.base, keep.iota_rows, keep.iota_tiles,
                        keep.ids[:, :, :].rearrange("p n k -> p (n k)"),
                        keep.pad_ids[:, :, :].rearrange("p u s -> p (u s)")):
                n = dst.shape[1]
                nc.vector.tensor_copy(dst[:, 0:n], f[:, o:o + n])
                o += n
            nc.vector.memset(keep.ones[:, :], 1.0)
            nc.vector.memset(keep.tail[:, :, 0:D], 0.0)
            nc.vector.tensor_copy(keep.tail[:, :, D].bitcast(I32), f[:, o:o + ROWS // P])
            nc.vector.memset(keep.no_rows[:, :], 0)
            nc.vector.memset(keep.neg_half[:, :], -0.5)


def wait(eng, sem, value):
    if isinstance(value, int) and value <= 0:
        return
    eng.wait_ge(sem, value)


class Chain:

    def __init__(self, eng, sem):
        self.eng, self.sem, self.n = eng, sem, 0

    def __call__(self, ins):
        ins.then_inc(self.sem, 1)
        self.n += 1
        self.eng.wait_ge(self.sem, self.n)

    def later(self, ins):
        ins.then_inc(self.sem, 1)
        self.n += 1

    def sync(self):
        if self.n:
            self.eng.wait_ge(self.sem, self.n)

    def restart(self):
        self.eng.sem_clear(self.sem)
        self.n = 0


class Combine:

    def __init__(self, nc, keep, sb, sem, slots, held=2):
        self.held = held
        self.nc, self.keep, self.slots = nc, keep, slots
        K4 = TPB * TOPK
        self.got = sb("got", [P, held, K4, D], F32)
        self.gate = sb("gate_b", [P, 2, K4], F32)
        self.used = sb("used", [P, 2], F32)
        self.s_got = [sem(f"got{u}") for u in range(held)]
        self.s_added = sem("added")

    def load(self, sp, b, w):
        wait(sp, self.s_added, b - self.held + 1)
        sp.dma_start(
            self.got[:, w, :, :].rearrange("p (t k) d -> p t k d", t=TPB),
            self.slots[bass.ds(b * (SEQ * TOPK), SEQ * TOPK), :].rearrange("(t p k) d -> p t k d", p=P, k=TOPK),
        ).then_inc(self.s_got[w], 16)

    def sp_loads(self, sp, done=None):
        n = self.held
        for b in range(n):
            self.load(sp, b, b)
        with sp.Fori(0, BATCHES // n - 1) as i:
            for w in range(n):
                if done:
                    done(i * n + w)
                self.load(sp, i * n + (w + n), w)
        if done:
            for b in range(BATCHES - n, BATCHES):
                done(b)

    def dve_add(self, dve, link, b, u, w=None):
        w = u if w is None else w
        nc, keep = self.nc, self.keep
        link(nc.vector.tensor_copy(self.gate[:, u, :].rearrange("p (t k) -> p t k", t=TPB),
                                   keep.gates[:, bass.ds(b * TPB, TPB), :]))
        wait(dve, self.s_got[w], (b - w) * (16 // self.held) + 16)
        for k in range(TOPK):
            for t in range(TPB):
                ins = nc.vector.scalar_tensor_tensor(
                    out=keep.x[:, bass.ds(b * TPB + t, 1), :],
                    in0=self.got[:, w, t * TOPK + k, :].unsqueeze(1),
                    scalar=self.gate[:, u, t * TOPK + k:t * TOPK + k + 1],
                    in1=keep.x[:, bass.ds(b * TPB + t, 1), :],
                    op0=ALU.mult, op1=ALU.add)
                (link if t == TPB - 1 else link.later)(ins)
        nc.vector.tensor_copy(self.used[:, u:u + 1], self.gate[:, u, 0:1]).then_inc(self.s_added, 1)


class Norm:

    def __init__(self, nc, keep, sb, sem, name, to_scatter=False, held=2):
        self.nc, self.keep, self.to_scatter = nc, keep, to_scatter
        self.stats = sb(f"{name}_stats", [P, 2, TPB, 6], F32)
        self.mv = sb(f"{name}_mv", [P, 2, TPB, 2], F32)
        self.vare = sb(f"{name}_vare", [P, 2, TPB], F32)
        self.rstd = sb(f"{name}_rstd", [P, 2, TPB], F32)
        self.out = sb(f"{name}_out", [P, held, TPB, TOPK, D + 1] if to_scatter else [P, held, TPB, 1, D], F32)
        self.s_var = sem(f"{name}_var")
        self.s_rstd = sem(f"{name}_rstd")
        self.s_out = sem(f"{name}_out")

    def stats_pieces(self, dve, link, b, u):
        nc = self.nc

        def sums():
            link.sync()
            for t in range(TPB):
                link.later(nc.vector.bn_stats(self.stats[:, u, t, :], self.keep.x[:, bass.ds(b * TPB + t, 1), :]))

        def aggregate():
            link.sync()
            for t in range(TPB):
                link.later(nc.vector.bn_aggr(self.mv[:, u, t, :], self.stats[:, u, t, :]))

        def with_eps():
            link.sync()
            nc.vector.tensor_scalar(self.vare[:, u, :], self.mv[:, u, :, 1], LN_EPS, None,
                                    ALU.add).then_inc(self.s_var, 1)

        return sums, aggregate, with_eps

    def dve_stats(self, dve, link, b, u):
        for piece in self.stats_pieces(dve, link, b, u):
            piece()

    def pool_rstd(self, pool, b, u):
        wait(pool, self.s_var, b + 1)
        self.nc.gpsimd.tensor_tensor(self.rstd[:, u, :], self.vare[:, u, :], self.keep.neg_half[:, 0:TPB],
                                     ALU.pow).then_inc(self.s_rstd, 1)

    def dve_apply(self, dve, b, u, w=None):
        w = u if w is None else w
        wait(dve, self.s_rstd, b + 1)
        if self.to_scatter:
            self.nc.vector.tensor_copy(self.out[:, w, :, :, D].bitcast(I32), self.keep.ids[:, bass.ds(b * TPB, TPB), :])
        for t in range(TPB):
            x = self.keep.x[:, bass.ds(b * TPB + t, 1), :]
            ins = self.nc.vector.tensor_scalar(
                self.out[:, w, t, :, 0:D], x.to_broadcast([P, TOPK, D]) if self.to_scatter else x,
                self.mv[:, u, t, 0:1], self.rstd[:, u, t:t + 1], ALU.subtract, ALU.mult)
        ins.then_inc(self.s_out, 1)


class Route:

    def __init__(self, nc, keep, sb, sem, slots, has_bias, capacity, held=2):
        self.held = held
        self.nc, self.keep, self.slots, self.has_bias, self.capacity = nc, keep, slots, has_bias, capacity
        U = 2
        self.norm = Norm(nc, keep, sb, sem, "route", to_scatter=True, held=held)
        self.xnT = sb("xnT", [P, U, SEQ], F32)
        self.wr = sb("wr", [P, 2 * E], F32)
        self.lg = sb("lg", [P, U, TPB, E], F32)
        self.mx = sb("top", [P, U, TPB, 8], F32)
        self.mi = sb("top_i", [P, U, TPB, 8], U32)
        self.mif = sb("top_f", [P, U, TPB, TOPK], F32)
        self.M = sb("choice", [P, U, TPB, TOPK, E], BF16)
        self.M_all = sb("choice_all", [P, TILES, TOPK, E], BF16)
        self.R = sb("running", [P, TOPK, E], F32)
        self.A = sb("before", [P, U, TPB, TOPK, E], F32)
        self.B = sb("before_sum", [P, U, 2, TPB, E], F32)
        self.prod = sb("picked", [P, U, 2, TPB * TOPK, E], F32)
        self.rows_f = sb("rows_f", [P, U, TPB * TOPK], F32)
        self.rows0 = sb("rows0", [P, held, TPB * TOPK], I32)
        self.rows = sb("rows", [P, held, TPB * TOPK], I32)
        self.loc = sb("loc", [P, TILES, TOPK], F32)
        self.dl = sb("dl", [P, TILES], F32)
        self.g = sb("g", [P, 6, TILES], F32)
        self.ahead = sb("ahead", [P, TILES, E], F32)
        self.cnt = sb("cnt", [P, 6, E], F32)
        self.cmp = sb("cmp", [P, E, TOKENS // ROWS], F32)
        self.tt = sb("tt", [P, 3, MOE_TILES, E], F32)
        self.tr = sb("tr", [P, 6, MOE_TILES], F32)
        self.s_w = sem("router_w")
        self.s_T = sem("route_T")
        self.s_xnT = sem("route_xnT")
        self.s_L = sem("logits")
        self.s_M = sem("choices")
        self.s_P = sem("prefix")
        self.s_A = sem("prefix_used")
        self.s_rows = sem("row_numbers")
        self.s_scat = [sem(f"scattered{u}") for u in range(held)]
        self.s_dl = sem("logit_gap")
        self.s_exp = sem("gap_exp")
        self.s_counts = sem("counts")
        self.s_zero = sem("tails")

    def sp_load(self, sp, router):
        sp.dma_start(self.wr[:, :], router).then_inc(self.s_w, 16)

    def dve_start(self, dve, link):
        link(self.nc.vector.memset(self.R[:, :, :], 0.0))
        dve.wait_ge(self.s_w, 16)

    def dve_norm(self, dve, b, u, w):
        wait(dve, self.s_scat[w], (b - w) * (16 * TPB * TOPK // self.held))
        self.norm.dve_apply(dve, b, u, w)

    def pe_T(self, pe, b, w, ps):
        wait(pe, self.norm.s_out, b + 1)
        for t in range(TPB):
            last = self.nc.tensor.transpose(ps[:, t * P:(t + 1) * P], self.norm.out[:, w, t, 0, 0:D], self.keep.ident[:, :])
        last.then_inc(self.s_T, 1)

    def act_T(self, act, b, u, ps):
        act.wait_ge(self.s_T, b + 1)
        self.nc.scalar.copy(self.xnT[:, u, :], ps[:, 0:SEQ]).then_inc(self.s_xnT, 1)

    def pe_L(self, pe, b, u, ps):
        pe.wait_ge(self.s_xnT, b + 1)
        for t in range(TPB):
            last = self.nc.tensor.matmul(ps[:, t * E:(t + 1) * E], self.xnT[:, u, t * P:(t + 1) * P],
                                         self.wr[:, 0:E], start=True, stop=True)
        last.then_inc(self.s_L, 1)

    def choose(self, dve, link, b, u, ps):
        nc, keep = self.nc, self.keep
        lg = self.lg[:, u, :, :]

        def logits_out():
            dve.wait_ge(self.s_L, b + 1)
            src = ps[:, 0:TPB * E].rearrange("p (t e) -> p t e", t=TPB)
            if self.has_bias:
                link.later(nc.vector.tensor_tensor(
                    lg, src, self.wr[:, E:2 * E].unsqueeze(1).to_broadcast([P, TPB, E]), ALU.add))
            else:
                link.later(nc.vector.tensor_copy(lg, src))

        def largest():
            link.sync()
            for t in range(TPB):
                link.later(nc.vector.max(self.mx[:, u, t, :], self.lg[:, u, t, :]))

        def places():
            link.sync()
            for t in range(TPB):
                link.later(nc.vector.max_index(self.mi[:, u, t, :], self.mx[:, u, t, :], self.lg[:, u, t, :]))

        def as_floats():
            link.sync()
            link.later(nc.vector.tensor_copy(self.mif[:, u, :, :], self.mi[:, u, :, 0:TOPK]))
            nc.vector.tensor_tensor(self.dl[:, bass.ds(b * TPB, TPB)], self.mx[:, u, :, 1], self.mx[:, u, :, 0],
                                    ALU.subtract).then_inc(self.s_dl, 1)

        def one_hot():
            link.sync()
            nc.vector.tensor_tensor(
                self.M[:, u, :, :, :].rearrange("p t k e -> p (t k) e"),
                self.mif[:, u, :, :].rearrange("p t k -> p (t k)").unsqueeze(2).to_broadcast([P, TPB * TOPK, E]),
                keep.iota_e[:, :].unsqueeze(1).to_broadcast([P, TPB * TOPK, E]),
                ALU.is_equal).then_inc(self.s_M, 1)

        return logits_out, largest, places, as_floats, one_hot

    def pe_P(self, pe, b, u, ps):
        nc, keep = self.nc, self.keep
        pe.wait_ge(self.s_M, b + 1)
        m = [self.M[:, u, t, :, :].rearrange("p k e -> p (k e)") for t in range(TPB)]
        nc.tensor.matmul(ps[:, 0:16], keep.upper[:, :], m[0], start=True, stop=True)
        nc.tensor.matmul(ps[:, 16:32], keep.upper[:, :], m[1], start=True, stop=False)
        nc.tensor.matmul(ps[:, 16:32], keep.ones[:, :], m[0], start=False, stop=True)
        nc.tensor.matmul(ps[:, 32:48], keep.ones[:, :], m[0], start=True, stop=False)
        nc.tensor.matmul(ps[:, 32:48], keep.ones[:, :], m[1], start=False, stop=True).then_inc(self.s_P, 1)

    def number(self, dve, link, b, u, w, ps):
        nc, keep = self.nc, self.keep
        m = self.M[:, u, :, :, :]

        def counts_out():
            dve.wait_ge(self.s_P, b + 1)
            link.later(nc.vector.tensor_tensor(
                self.A[:, u, :, :, :].rearrange("p t k e -> p t (k e)"),
                ps[:, 0:32].rearrange("p (t m) -> p t m", t=TPB),
                self.R[:, :, :].rearrange("p k e -> p (k e)").unsqueeze(1).to_broadcast([P, TPB, TOPK * E]), ALU.add))
            nc.vector.tensor_copy(self.M_all[:, bass.ds(b * TPB, TPB), :, :], m)

        def both_choices():
            link.sync()
            link.later(nc.vector.tensor_tensor(
                self.B[:, u, 0, :, :], self.A[:, u, :, 0, :], self.A[:, u, :, 1, :], ALU.add))
            nc.vector.tensor_tensor(
                self.R[:, :, :], ps[:, 32:48].rearrange("p (k e) -> p k e", k=TOPK), self.R[:, :, :],
                ALU.add).then_inc(self.s_A, 1)

        def plus_base():
            link.sync()
            link.later(nc.vector.tensor_tensor(self.B[:, u, 1, :, :], self.B[:, u, 0, :, :],
                                               keep.base[:, :].unsqueeze(1).to_broadcast([P, TPB, E]), ALU.add))
            link.later(nc.vector.tensor_tensor(
                self.prod[:, u, 0, :, :], m.rearrange("p t k e -> p (t k) e"),
                self.A[:, u, :, :, :].rearrange("p t k e -> p (t k) e"), ALU.mult))

        def picked():
            link.sync()
            link.later(nc.vector.tensor_tensor(
                self.prod[:, u, 1, :, :].rearrange("p (t k) e -> p t k e", t=TPB), m,
                self.B[:, u, 1, :, :].unsqueeze(2).to_broadcast([P, TPB, TOPK, E]), ALU.mult))
            nc.vector.tensor_reduce(
                self.loc[:, bass.ds(b * TPB, TPB), :],
                self.prod[:, u, 0, :, :].rearrange("p (t k) e -> p t k e", t=TPB), AX, ALU.add)

        def rows_out():
            link.sync()
            link(nc.vector.tensor_reduce(self.rows_f[:, u, :], self.prod[:, u, 1, :, :], AX, ALU.add))
            nc.vector.tensor_copy(self.rows0[:, w, :], self.rows_f[:, u, :]).then_inc(self.s_rows, 1)

        return counts_out, both_choices, plus_base, picked, rows_out

    def pool_scatter(self, pool, chain, b, w):
        wait(pool, self.s_rows, b + 1)
        chain(self.nc.gpsimd.tensor_tensor(self.rows[:, w, :], self.rows0[:, w, :], self.keep.no_rows[:, :], ALU.add))
        for k in range(TPB * TOPK):
            pool.indirect_dma_start(
                self.slots, bass.IndirectOffsetOnAxis(ap=self.rows[:, w, k:k + 1].bitcast(U32), axis=0),
                self.norm.out[:, w, k // TOPK, k % TOPK, :], None).then_inc(self.s_scat[w], 16)

    def pool_end(self, pool):
        for w in range(self.held):
            pool.wait_ge(self.s_scat[w], 16 * TPB * TOPK // self.held * BATCHES)

    def act_end(self, act):
        act.wait_ge(self.s_dl, BATCHES)
        self.nc.scalar.activation(self.g[:, 0, :], self.dl[:, :], ACT.Exp).then_inc(self.s_exp, 1)
        self.clear_tails(act, range(E // 2, E), False)

    def dve_end(self, dve, link):
        nc, keep, g, cnt, tt, tr = self.nc, self.keep, self.g, self.cnt, self.tt, self.tr
        dve.wait_ge(self.s_A, BATCHES)
        nr = TOKENS // ROWS
        link(nc.vector.tensor_tensor(cnt[:, 0, :], self.R[:, 0, :], self.R[:, 1, :], ALU.add))
        nc.vector.tensor_copy(keep.counts[:, :], cnt[:, 0, :]).then_inc(self.s_counts, 1)
        link(nc.vector.tensor_tensor(
            self.cmp[:, :, :], cnt[:, 0, :].unsqueeze(2).to_broadcast([P, E, nr]),
            keep.iota_rows[:, :].unsqueeze(1).to_broadcast([P, E, nr]), ALU.is_gt))
        link(nc.vector.tensor_reduce(cnt[:, 1, :], self.cmp[:, :, :], AX, ALU.add))
        link(nc.vector.memset(cnt[:, 5, :], 1.0))
        link(nc.vector.tensor_tensor_scan(cnt[:, 2, :], cnt[:, 5, :], cnt[:, 1, :], 0.0, ALU.mult, ALU.add))
        link(nc.vector.tensor_tensor(cnt[:, 3, :], cnt[:, 2, :], cnt[:, 1, :], ALU.subtract))
        link(nc.vector.scalar_tensor_tensor(
            out=cnt[:, 4, :], in0=cnt[:, 3, :], scalar=-float(ROWS), in1=keep.base[:, :],
            op0=ALU.mult, op1=ALU.add))
        jt = keep.iota_tiles[:, :].unsqueeze(2).to_broadcast([P, MOE_TILES, E])

        def per_e(row):
            return row.unsqueeze(1).to_broadcast([P, MOE_TILES, E])

        nc.vector.tensor_tensor(tt[:, 0, :, :], per_e(cnt[:, 2, :]), jt, ALU.is_gt)
        link(nc.vector.tensor_tensor(tt[:, 1, :, :], per_e(cnt[:, 3, :]), jt, ALU.is_le))
        link(nc.vector.tensor_tensor(tt[:, 2, :, :], tt[:, 0, :, :], tt[:, 1, :, :], ALU.mult))
        nc.vector.tensor_tensor(tt[:, 0, :, :], tt[:, 2, :, :], per_e(cnt[:, 4, :]), ALU.mult)
        link(nc.vector.tensor_tensor(tt[:, 1, :, :], tt[:, 2, :, :], per_e(keep.iota_e[:, :]), ALU.mult))
        link(nc.vector.tensor_reduce(tr[:, 0:3, :], tt[:, :, :, :], AX, ALU.add))
        nc.vector.tensor_scalar(tr[:, 5, :], tr[:, 2, :], -float(SPARE), float(SPARE), ALU.mult, ALU.add)
        link(nc.vector.scalar_tensor_tensor(
            out=tr[:, 3, :], in0=keep.iota_tiles[:, :], scalar=float(ROWS), in1=tr[:, 2, :],
            op0=ALU.mult, op1=ALU.mult))
        link(nc.vector.tensor_tensor(tr[:, 4, :], tr[:, 3, :], tr[:, 0, :], ALU.add))
        link(nc.vector.tensor_tensor(tr[:, 3, :], tr[:, 4, :], tr[:, 5, :], ALU.add))
        nc.vector.tensor_copy(keep.table[:, :, 0], tr[:, 1, :])
        nc.vector.tensor_copy(keep.table[:, :, 1], tr[:, 3, :])
        dve.wait_ge(self.s_exp, 1)
        link(nc.vector.tensor_scalar(g[:, 1, :], g[:, 0, :], 1.0, 2.0, ALU.add, ALU.mult))
        link(nc.vector.reciprocal(g[:, 2, :], g[:, 1, :]))
        link(nc.vector.tensor_tensor(g[:, 3, :], g[:, 0, :], g[:, 2, :], ALU.mult))
        if self.capacity:
            link(nc.vector.tensor_tensor(
                self.ahead[:, :, :], self.M_all[:, :, 1, :],
                self.R[:, 0, :].unsqueeze(1).to_broadcast([P, TILES, E]), ALU.mult))
            link(nc.vector.tensor_reduce(g[:, 4, :], self.ahead[:, :, :], AX, ALU.add))
            link(nc.vector.tensor_tensor(g[:, 5, :], g[:, 4, :], self.loc[:, :, 1], ALU.add))
            nc.vector.scalar_tensor_tensor(
                out=keep.gates[:, :, 0], in0=self.loc[:, :, 0], scalar=float(CAP), in1=g[:, 2, :],
                op0=ALU.is_lt, op1=ALU.mult)
            nc.vector.scalar_tensor_tensor(
                out=keep.gates[:, :, 1], in0=g[:, 5, :], scalar=float(CAP), in1=g[:, 3, :],
                op0=ALU.is_lt, op1=ALU.mult)
        else:
            nc.vector.tensor_copy(keep.gates[:, :, 0], g[:, 2, :])
            nc.vector.tensor_copy(keep.gates[:, :, 1], g[:, 3, :])

    def clear_tails(self, eng, experts, spare):
        eng.wait_ge(self.s_counts, 1)
        for e in experts:
            c = eng.value_load(self.keep.counts[0:1, e:e + 1], min_val=0, max_val=TOKENS)
            eng.dma_start(self.slots[bass.ds(c + e * REGION, ROWS), :].rearrange("(p s) d -> p (s d)", p=P),
                          self.keep.tail[:, :, :].rearrange("p s d -> p (s d)")).then_inc(self.s_zero, 16)
        if spare:
            eng.dma_start(self.slots[SPARE:SPARE + ROWS, :].rearrange("(p s) d -> p (s d)", p=P),
                          self.keep.tail[:, :, :].rearrange("p s d -> p (s d)")).then_inc(self.s_zero, 16)
        eng.wait_ge(self.s_zero, 16 * (E + 1))

    def sp_end(self, sp):
        self.clear_tails(sp, range(E // 2), True)


def looped_steps(eng, first, lo, hi, last, step, per=2):
    for s in range(first, lo):
        step(s, s % per)
    if hi > lo:
        with eng.Fori(0, (hi - lo) // per) as i:
            for n in range(per):
                step(i * per + (lo + n), (lo + n) % per)
    for s in range(hi, last + 1):
        step(s, s % per)


def is_first(b):
    return isinstance(b, int) and b == 0


def has(b, count=BATCHES):
    return not isinstance(b, int) or 0 <= b < count


def token_stage(nc, keep, tag, slots_in, slots_out, router=None, router_bias=False, capacity=False, out=None):
    with ExitStack() as ctx:
        def sb(name, shape, dt):
            return ctx.enter_context(nc.sbuf_tensor(f"{tag}_{name}", shape, dt))

        def pb(name, shape, dt):
            return ctx.enter_context(nc.psum_tensor(f"{tag}_{name}", shape, dt))

        sem = stage_semaphores(nc, ctx, tag)

        comb = Combine(nc, keep, sb, sem, slots_in, 4) if slots_in is not None else None
        route = Route(nc, keep, sb, sem, slots_out, router_bias, capacity, 4) if slots_out is not None else None
        psT = [pb(f"psT{u}", [P, 512], F32) for u in range(2)]
        psL = [pb(f"psL{u}", [P, 512], F32) for u in range(2)]
        psP = [pb(f"psP{u}", [P, 512], F32) for u in range(2)]
        s_dve = sem("dve_chain")
        s_pool = sem("pool_chain")
        s_out = sem("out")
        block = ctx.enter_context(nc.Block())

        @block.gpsimd
        def _(pool):
            chain = Chain(pool, s_pool)

            def step(s, w):
                if route and has(s):
                    route.norm.pool_rstd(pool, s, w % 2)
                if route and has(s - 2):
                    route.pool_scatter(pool, chain, s - 2, (w + 2) % 4)
                chain.restart()

            looped_steps(pool, -1, 5, 13, 17, step, 4)
            if route:
                route.pool_end(pool)

        @block.vector
        def _(dve):
            link = Chain(dve, s_dve)
            if route:
                route.dve_start(dve, link)
                link.restart()

            def step(s, w):
                u = w % 2
                if comb and has(s):
                    comb.dve_add(dve, link, s, u, w)
                if route:
                    stats = route.norm.stats_pieces(dve, link, s, u) if has(s) else ()
                    choose = route.choose(dve, link, s - 2, u, psL[u]) if has(s - 2) else ()
                    for n in range(5):
                        for piece in stats[n:n + 1] + choose[n:n + 1]:
                            piece()
                    if has(s - 1):
                        route.dve_norm(dve, s - 1, 1 - u, (w + 3) % 4)
                    if has(s - 2):
                        for piece in route.number(dve, link, s - 2, u, (w + 2) % 4, psP[u]):
                            piece()
                link.restart()

            looped_steps(dve, -1, 5, 13, 17, step, 4)
            if route:
                route.dve_end(dve, link)

        @block.tensor
        def _(pe):
            if not route:
                return
            pe.wait_ge(route.s_w, 16)

            def step(s, w):
                u, v = w % 2, (w + 1) % 2
                if has(s - 2):
                    route.pe_P(pe, s - 2, u, psP[u])
                if has(s - 1):
                    route.pe_T(pe, s - 1, (w + 3) % 4, psT[v])
                    route.pe_L(pe, s - 1, v, psL[v])

            looped_steps(pe, 1, 5, 13, 17, step, 4)

        @block.scalar
        def _(act):
            if not route:
                return

            def step(s, u):
                route.act_T(act, s, u, psT[u])

            looped_steps(act, 0, 0, BATCHES, BATCHES - 1, step)
            route.act_end(act)

        @block.sync
        def _(sp):
            def store(b):
                sp.wait_ge(comb.s_added, b + 1)
                sp.dma_start(out[bass.ds(b * SEQ, SEQ), :].rearrange("(t p) d -> p t d", p=P),
                             keep.x[:, bass.ds(b * TPB, TPB), :]).then_inc(s_out, 16)

            if route:
                route.sp_load(sp, router)
            if comb:
                comb.sp_loads(sp, store if out is not None else None)
            if route:
                route.sp_end(sp)
            if out is not None:
                sp.wait_ge(s_out, 16 * BATCHES)


def attention_stage(nc, keep, tag, slots_in, slots_out, causal, params, router, router_bias, capacity):
    with ExitStack() as ctx:
        def sb(name, shape, dt):
            return ctx.enter_context(nc.sbuf_tensor(f"{tag}_{name}", shape, dt))

        def pb(name, shape, dt):
            return ctx.enter_context(nc.psum_tensor(f"{tag}_{name}", shape, dt))

        sem = stage_semaphores(nc, ctx, tag)

        QKV = 3 * D
        G = HEADS // 4
        UNITS = 16
        OPERANDS = ((0, 0), (1, 0), (0, 1), (1, 1))
        comb = Combine(nc, keep, sb, sem, slots_in)
        route = Route(nc, keep, sb, sem, slots_out, router_bias, capacity)
        norm = Norm(nc, keep, sb, sem, "attn")
        par = sb("par", [P, params.shape[1]], F32)
        wqkv = sb("wqkv", [P, QKV], F32)
        xaT = sb("xaT", [P, SEQ], F32)
        pr = sb("pr", [P, 2, TPB, QKV], F32)
        pt = sb("pt", [P, 2, TPB, QKV], F32)
        pt2 = sb("pt2", [P, TPB, QKV], F32)
        qk = sb("qk", [P, TPB, 2 * D], F32)
        left = sb("left", [P, TPB, 2 * D], F32)
        left2 = sb("left2", [P, TPB, 2 * D], F32)
        hv = sb("hv", [P, 8, TPB * 3 * HEADS], F32)
        ext = [sb(f"ext{u}", [P, TPB, 2, HEADS, XR], BF16) for u in range(2)]
        vx = [sb(f"vx{u}", [P, TPB, HEADS, 32], F32) for u in range(2)]
        QT = [sb(f"QT{u}", [P, HEADS // 2, SEQ], BF16) for u in range(2)]
        KT = [sb(f"KT{u}", [P, HEADS // 2, SEQ], BF16) for u in range(2)]
        QM = sb("QM", [P, HEADS // 2, SEQ], BF16)
        mx = [sb(f"mx{u}", [P, TPB, HEADS], F32) for u in range(2)]
        mleft = sb("mleft", [P, TPB, HEADS], F32)
        PT = sb("PT", [P, 4, 2, SEQ], F32)
        oT = [sb(f"oT{u}", [P, G, SEQ], F32) for u in range(2)]
        den = sb("den", [P, TPB, HEADS], F32)
        o = sb("o", [P, TPB, D], F32)
        onT = sb("onT", [P, SEQ], F32)
        identb = sb("identb", [P, P], BF16)
        psS = [pb(f"psS{n}", [P, 2, SEQ], F32) for n in range(2)]
        psE = [pb(f"psE{n}", [P, 2, SEQ], F32) for n in range(2)]
        psV = [pb(f"psV{n}", [P, 2, SEQ], F32) for n in range(2)]
        psA = pb("psA", [P, 512], F32)
        psD = pb("psD", [P, 512], F32)
        back_bank, first_bank = (psV[n][:, :, :].rearrange("p a q -> p (a q)") for n in (1, 0))
        bank_of = (first_bank, psA, psD, first_bank)
        if causal:
            masks = sb("masks", [P, 2, P], BF16)
            cosn = sb("cosn", [P, 2, TPB, 2, 64], F32)
            ang = sb("ang", [P, 6, TPB * 64], F32)
            dec = sb("dec", [P, 6, HEADS], F32)
        s_par = sem("par")
        s_ones = sem("ones")
        s_ready = sem("ready")
        s_gpi = sem("sigmoids")
        s_sin = sem("sines")
        s_dve = sem("dve_chain")
        s_pool = sem("pool_chain")
        s_act = sem("act_chain")
        s_xaT_ps = sem("xaT_ps")
        s_xaT = sem("xaT")
        s_proj = sem("proj")
        s_pr = sem("pr")
        s_sq = sem("sq")
        s_hv = sem("hv")
        s_xb = sem("output_bias")
        s_hn = sem("hn")
        s_hr = sem("hr")
        s_qk = sem("qk")
        s_v = sem("v")
        s_a = sem("part_a")
        s_l1 = sem("left1")
        s_b = sem("part_b")
        s_l2 = sem("left2")
        s_copies = sem("copies")
        s_ext = sem("ext")
        s_X = sem("X")
        s_QK = [sem(f"QK{n}") for n in range(4)]
        s_S = sem("S")
        s_max = sem("max")
        s_m = sem("m")
        s_Xm = sem("Xm")
        s_QM = [sem(f"QM{t}") for t in range(TPB)]
        s_E = sem("E")
        s_e = sem("e")
        s_V = sem("V")
        s_oT = [sem(f"oT{n}") for n in range(2)]
        s_O = sem("O")
        s_o = sem("o")
        s_OT = sem("OT")
        s_onT = sem("onT")
        s_Y = sem("Y")
        block = ctx.enter_context(nc.Block())

        def parts(u, w, g):
            return ext[u][:, :, w, :, g * DH:(g + 1) * DH]

        def both(u, g):
            return ext[u][:, :, :, :, g * DH:(g + 1) * DH].rearrange("p t w h d -> p (t w h) d")

        def flat(buf):
            return buf[:, :, :].rearrange("p t (g d) -> p (t g) d", d=DH)

        def one(buf, w):
            return buf[:, :, w * D:(w + 1) * D].rearrange("p t (h d) -> p t h d", d=DH)

        def unit_b(c):
            return c // 8, (c % 8) // 2, c % 2

        def unit_c(c):
            return c // 4, (c // 2) % 2, c % 2

        @block.sync
        def _(sp):
            sp.dma_start(par[:, :], params).then_inc(s_par, 16)
            route.sp_load(sp, router)
            comb.sp_loads(sp)
            route.sp_end(sp)

        @block.gpsimd
        def _(pool):
            chain = Chain(pool, s_pool)

            def rotate(b, u):
                if is_first(b):
                    pool.wait_ge(s_ready, 1)
                pool.wait_ge(s_pr, TPB * (b + 1))
                wait(pool, s_a, b)
                pairs = pr[:, u, :, 0:2 * D].rearrange("p t (f two) -> p t f two", two=2)
                even, odd = pairs[:, :, :, 0], pairs[:, :, :, 1]
                c, s = (cosn[:, n, :, :, :].rearrange("p t w f -> p t (w f)") for n in range(2))
                w = [pt[:, 0, :, n * D:(n + 1) * D] for n in range(3)] + [pt2[:, :, 0:D]]
                dst = qk[:, :, :].rearrange("p t (f two) -> p t f two", two=2)
                nc.gpsimd.tensor_tensor(w[0], even, c, ALU.mult).then_inc(s_pool, 1)
                nc.gpsimd.tensor_tensor(w[1], odd, s, ALU.mult).then_inc(s_pool, 1)
                nc.gpsimd.tensor_tensor(w[2], even, s, ALU.mult).then_inc(s_pool, 1)
                chain.n += 3
                chain(nc.gpsimd.tensor_tensor(w[3], odd, c, ALU.mult))
                nc.gpsimd.tensor_tensor(dst[:, :, :, 0], w[0], w[1], ALU.subtract).then_inc(s_qk, 1)
                nc.gpsimd.tensor_tensor(dst[:, :, :, 1], w[2], w[3], ALU.add).then_inc(s_qk, 1)

            def refine(b):
                pool.wait_ge(s_hr, b + 1)
                for n in range(3):
                    chain(nc.gpsimd.tensor_tensor(hv[:, 4, :], hv[:, 3, :], hv[:, 3, :], ALU.mult))
                    chain(nc.gpsimd.tensor_tensor(hv[:, 5, :], hv[:, 4, :], hv[:, 1, :], ALU.mult))
                    chain(nc.gpsimd.tensor_scalar(hv[:, 6, :], hv[:, 5, :], -0.5, 1.5, ALU.mult, ALU.add))
                    if n < 2:
                        chain(nc.gpsimd.tensor_tensor(hv[:, 3, :], hv[:, 6, :], hv[:, 3, :], ALU.mult))
                    else:
                        nc.gpsimd.tensor_tensor(hv[:, 7, :], hv[:, 6, :], hv[:, 3, :], ALU.mult).then_inc(s_hn, 1)

            def scale_heads(b, u):
                if is_first(b):
                    pool.wait_ge(s_ready, 1)
                pool.wait_ge(s_hn, b + 1)
                chain(nc.gpsimd.tensor_tensor(
                    pt2[:, :, :].rearrange("p t (h d) -> p (t h) d", d=DH),
                    pr[:, u, :, :].rearrange("p t (h d) -> p (t h) d", d=DH),
                    hv[:, 7, :].unsqueeze(2).to_broadcast([P, TPB * 3 * HEADS, DH]), ALU.mult))
                chain(nc.gpsimd.tensor_tensor(
                    pt[:, u, :, :], pt2[:, :, :],
                    par[:, SC0:SC0 + QKV].unsqueeze(1).to_broadcast([P, TPB, QKV]), ALU.mult))
                wait(pool, s_a, b)
                nc.gpsimd.tensor_tensor(
                    qk[:, :, :], pt[:, u, :, 0:2 * D],
                    par[:, SB0:SB0 + 2 * D].unsqueeze(1).to_broadcast([P, TPB, 2 * D]), ALU.add).then_inc(s_qk, 2)

            def output_bias(b):
                nc.gpsimd.tensor_tensor(
                    keep.x[:, bass.ds(b * TPB, TPB), :], keep.x[:, bass.ds(b * TPB, TPB), :],
                    par[:, BO0:BO0 + D].unsqueeze(1).to_broadcast([P, TPB, D]), ALU.add).then_inc(s_xb, 1)

            def left_of_a(b, u):
                pool.wait_ge(s_a, b + 1)
                nc.gpsimd.tensor_tensor(flat(left), flat(qk), both(u, 0), ALU.subtract).then_inc(s_l1, 1)

            def left_of_b(b, u):
                pool.wait_ge(s_b, b + 1)
                nc.gpsimd.tensor_tensor(flat(left2), flat(left), both(u, 4), ALU.subtract).then_inc(s_l2, 1)

            def step(s, u):
                v = 1 - u
                if has(s + 1) and not causal:
                    scale_heads(s + 1, v)
                if has(s + 1):
                    left_of_a(s + 1, v)
                if has(s) and not causal:
                    output_bias(s)
                if has(s + 1):
                    left_of_b(s + 1, v)
                if has(s + 3):
                    norm.pool_rstd(pool, s + 3, v)
                if has(s - 3):
                    route.pool_scatter(pool, chain, s - 3, v)
                if has(s - 2):
                    route.norm.pool_rstd(pool, s - 2, u)
                if has(s + 2) and causal:
                    rotate(s + 2, u)
                if has(s + 2) and not causal:
                    refine(s + 2)
                chain.restart()

            for u in range(2):
                chain.later(nc.gpsimd.memset(vx[u][:, :, :, :], 0.0))
            chain.sync()
            for u in range(2):
                nc.gpsimd.memset(vx[u][:, :, :, DH:DH + 1], 1.0).then_inc(s_ones, 1)
            looped_steps(pool, -3, 4, 12, 18, step)
            route.pool_end(pool)

        @block.vector
        def _(dve):
            link = Chain(dve, s_dve)

            def project_out(b, u, t):
                dve.wait_ge(s_proj, TPB * b + t + 1)
                if t == 0:
                    wait(dve, s_v, b - 1)
                nc.vector.tensor_tensor(pr[:, u, t, :], psA[:, 0:QKV], par[:, BI0:BI0 + QKV], ALU.add).then_inc(s_pr, 1)

            def head_var(b, u):
                dve.wait_ge(s_sq, b + 1)
                wait(dve, s_hn, b)
                link(nc.vector.tensor_reduce(
                    hv[:, 0, :], pt[:, u, :, :].rearrange("p t (h d) -> p (t h) d", d=DH), AX, ALU.add))
                link(nc.vector.tensor_scalar(hv[:, 1, :], hv[:, 0, :], 1.0 / DH, QK_EPS, ALU.mult, ALU.add))
                nc.vector.tensor_scalar(hv[:, 2, :], hv[:, 1, :].bitcast(I32), -0.5 * LN2 / 2 ** 23,
                                        0.5 * LN2 * (127 - 0.043), ALU.mult, ALU.add).then_inc(s_hv, 1)

            def values_out(b, u):
                wait(dve, s_V, UNITS * (b - 1))
                dve.wait_ge(s_qk, 2 * (b + 1))
                nc.vector.tensor_tensor(
                    vx[u][:, :, :, 0:DH], pt[:, u, :, 2 * D:QKV].rearrange("p t (h d) -> p t h d", d=DH),
                    par[:, SB0 + 2 * D:SB0 + QKV].rearrange("p (h d) -> p h d", d=DH).unsqueeze(1)
                    .to_broadcast([P, TPB, HEADS, DH]), ALU.add).then_inc(s_v, 1)

            def split_a(b, u):
                dve.wait_ge(s_qk, 2 * (b + 1))
                wait(dve, s_Xm, TPB * (b - 1))
                nc.vector.tensor_copy(both(u, 0), flat(qk)).then_inc(s_a, 1)

            def split_b(b, u):
                dve.wait_ge(s_l1, b + 1)
                nc.vector.tensor_copy(both(u, 4), flat(left)).then_inc(s_b, 1)

            def split_c(b, u):
                dve.wait_ge(s_l2, b + 1)
                nc.vector.tensor_copy(parts(u, 0, 2), one(left2, 0))
                nc.vector.tensor_copy(parts(u, 1, 5), one(left2, 1)).then_inc(s_ext, 1)

            def unit_max(b, u, c):
                t, g, r = unit_b(c)
                cols = P if causal and t == 0 else SEQ
                dve.wait_ge(s_S, UNITS * b + c + 1)
                nc.vector.tensor_reduce(mx[u][:, t, 4 * g + r:4 * g + r + 3:2], psS[c % 2][:, :, 0:cols],
                                        AX, ALU.max).then_inc(s_max, 1)

            def max_rows(b, u):
                dve.wait_ge(s_max, UNITS * (b + 1))
                dst = [ext[u][:, :, 0, :, MAXR + n] for n in range(2)]
                link(nc.vector.tensor_scalar(dst[0], mx[u][:, :, :], -1.0, None, ALU.mult))
                link(nc.vector.scalar_tensor_tensor(out=mleft[:, :, :], in0=mx[u][:, :, :], scalar=-1.0,
                                                    in1=dst[0], op0=ALU.mult, op1=ALU.subtract))
                nc.vector.tensor_copy(dst[1], mleft[:, :, :]).then_inc(s_m, 1)

            def queries_out(b):
                dve.wait_ge(s_Xm, TPB * b + 1)
                wait(dve, s_E, UNITS * b)
                nc.vector.tensor_copy(QM[:, :, 0:P].bitcast(U32),
                                      psA[:, :].bitcast(U32).rearrange("p (k q) -> p k q", k=8)).then_inc(s_QM[0], 1)

            def last_operand_out(b, u):
                dve.wait_ge(s_X, 4 * (b + 1))
                wait(dve, s_E, UNITS * (b - 1))
                nc.vector.tensor_copy(KT[u][:, :, P:2 * P].bitcast(U32),
                                      bank_of[3][:, :].bitcast(U32).rearrange("p (k q) -> p k q", k=8)).then_inc(s_QK[3], 1)

            def weighted_out(b, u):
                dve.wait_ge(s_V, UNITS * (b + 1))
                nc.vector.tensor_copy(oT[u][:, 2:4, :], psV[1][:, :, :]).then_inc(s_oT[1], 1)

            def divide(b, t):
                dve.wait_ge(s_O, TPB * b + t + 1)
                heads = back_bank.rearrange("p (h d) -> p h d", d=32)
                if t == 0:
                    wait(dve, s_OT, b)
                link(nc.vector.reciprocal(den[:, t, :].unsqueeze(2), heads[:, :, DH:DH + 1]))
                nc.vector.tensor_tensor(
                    o[:, t, :].rearrange("p (h d) -> p h d", d=DH), heads[:, :, 0:DH],
                    den[:, t, :].unsqueeze(2).to_broadcast([P, HEADS, DH]), ALU.mult).then_inc(s_o, 1)

            def residual(b):
                dve.wait_ge(s_Y, b + 1)
                if not causal:
                    dve.wait_ge(s_xb, b + 1)
                link(nc.vector.tensor_tensor(
                    keep.x[:, bass.ds(b * TPB, TPB), :], psD[:, 0:SEQ].rearrange("p (t d) -> p t d", t=TPB),
                    keep.x[:, bass.ds(b * TPB, TPB), :], ALU.add))

            def step(s, u):
                v = 1 - u
                if has(s - 1):
                    queries_out(s - 1)

                def maxima(lo, hi):
                    for c in range(lo, hi):
                        if has(s):
                            unit_max(s, u, c)

                choose = route.choose(dve, link, s - 3, v, psD) if has(s - 3) else ()
                number = route.number(dve, link, s - 3, v, v, psD) if has(s - 3) else ()
                stats = norm.stats_pieces(dve, link, s + 3, v) if has(s + 3) else ()

                def do(pieces, n):
                    for piece in pieces[n:n + 1]:
                        piece()

                maxima(0, 1)
                if has(s + 3) and not causal:
                    comb.dve_add(dve, link, s + 3, v)
                maxima(1, 2)
                if has(s + 1) and causal:
                    split_a(s + 1, v)
                if has(s) and not causal:
                    values_out(s, u)
                maxima(2, 3)
                if has(s - 2):
                    divide(s - 2, 0)
                maxima(3, 4)
                if has(s + 3) and causal:
                    comb.dve_add(dve, link, s + 3, v)
                if has(s + 1) and not causal:
                    split_a(s + 1, v)
                do(choose, 0)
                maxima(4, 5)
                do(choose, 1)
                if has(s + 2) and not causal:
                    project_out(s + 2, u, 0)
                if has(s + 1) and causal:
                    split_b(s + 1, v)
                do(choose, 2)
                maxima(5, 6)
                do(choose, 3)
                if has(s - 2):
                    divide(s - 2, 1)
                do(choose, 4)
                maxima(6, 7)
                do(stats, 0)
                if has(s + 1) and not causal:
                    split_b(s + 1, v)
                maxima(7, 8)
                do(stats, 1)
                if has(s + 2) and not causal:
                    project_out(s + 2, u, 1)
                do(number, 0)
                do(stats, 2)
                maxima(8, 9)
                do(number, 1)
                maxima(9, 10)
                do(number, 2)
                if has(s + 1):
                    split_c(s + 1, v)
                do(number, 3)
                maxima(10, 11)
                do(number, 4)
                maxima(11, 12)
                maxima(12, 13)
                if has(s - 2):
                    residual(s - 2)
                    route.norm.dve_stats(dve, link, s - 2, u)
                if has(s + 2) and not causal:
                    head_var(s + 2, u)
                maxima(13, 16)
                if has(s):
                    max_rows(s, u)
                if has(s + 3):
                    norm.dve_apply(dve, s + 3, v)
                if has(s - 1):
                    weighted_out(s - 1, v)
                if has(s + 1):
                    last_operand_out(s + 1, v)
                if has(s - 2):
                    route.dve_norm(dve, s - 2, u, u)
                link.restart()

            def setup():
                route.dve_start(dve, link)
                for u in range(2):
                    link.later(nc.vector.memset(
                        ext[u][:, :, :, :, :].rearrange("p t w h r -> p (t w h r)").bitcast(U32), 0))
                link(nc.vector.tensor_copy(identb[:, :], keep.ident[:, :]))
                for u in range(2):
                    nc.vector.memset(ext[u][:, :, 1, :, MAXR:MAXR + 2], 1.0)
                dve.wait_ge(s_par, 16)
                if causal:
                    dve.wait_ge(s_gpi, 2)
                    link(nc.vector.tensor_scalar(dec[:, 1:3, :], dec[:, 3:5, :], 1.0, None, ALU.add))
                    link(nc.vector.reciprocal(dec[:, 3:5, :], dec[:, 1:3, :]))
                    link(nc.vector.tensor_tensor(dec[:, 1, :], dec[:, 4, :], dec[:, 0, :], ALU.mult))
                    for part in range(3):
                        for u in range(2):
                            for t in range(TPB):
                                ins = nc.vector.tensor_copy(ext[u][:, t, 0, :, DECAY + part], dec[:, 1 + part % 2, :])
                                nc.vector.tensor_copy(ext[u][:, t, 1, :, DECAY + 3 + part], dec[:, 1 + part % 2, :])
                                nc.vector.tensor_copy(ext[u][:, t, 1, :, DECAY + part],
                                                      par[:, POS0 + t:POS0 + t + 1].to_broadcast([P, HEADS]))
                                nc.vector.tensor_scalar(ext[u][:, t, 0, :, DECAY + 3 + part],
                                                        par[:, POS0 + t:POS0 + t + 1].to_broadcast([P, HEADS]),
                                                        -1.0, None, ALU.mult)
                        link(ins)
                        if part < 2:
                            link(nc.vector.tensor_tensor(dec[:, 1 + (part + 1) % 2, :], dec[:, 1 + part % 2, :],
                                                         ext[0][:, 0, 0, :, DECAY + part], ALU.subtract))
                    for t in range(TPB):
                        ins = nc.vector.tensor_tensor(
                            ang[:, 0, t * 64:(t + 1) * 64].rearrange("p (h f) -> p h f", f=4),
                            par[:, ANG0 + 4 * t:ANG0 + 4 * t + 4].unsqueeze(1).to_broadcast([P, HEADS, 4]),
                            dec[:, 3, :].unsqueeze(2).to_broadcast([P, HEADS, 4]), ALU.mult)
                    link(ins)
                    link(nc.vector.tensor_scalar(ang[:, 1, :], ang[:, 0, :], 1 / TWO_PI, ROUNDER, ALU.mult, ALU.add))
                    link(nc.vector.tensor_scalar(ang[:, 2, :], ang[:, 1, :], ROUNDER, None, ALU.subtract))
                    link(nc.vector.scalar_tensor_tensor(out=ang[:, 1, :], in0=ang[:, 2, :], scalar=-TWO_PI_HI,
                                                        in1=ang[:, 0, :], op0=ALU.mult, op1=ALU.add))
                    link(nc.vector.scalar_tensor_tensor(out=ang[:, 3, :], in0=ang[:, 2, :], scalar=-TWO_PI_LO,
                                                        in1=ang[:, 1, :], op0=ALU.mult, op1=ALU.add))
                    link(nc.vector.tensor_scalar(ang[:, 0, :], ang[:, 3, :], PI_BELOW, -PI_BELOW, ALU.min, ALU.max))
                    link(nc.vector.scalar_tensor_tensor(out=ang[:, 1, :], in0=ang[:, 0, :], scalar=-1.0,
                                                        in1=ang[:, 0, :], op0=ALU.mult, op1=ALU.max))
                    nc.vector.tensor_scalar(ang[:, 2, :], ang[:, 1, :], -1.0, HALF_PI, ALU.mult,
                                            ALU.add).then_inc(s_sin, 1)
                    dve.wait_ge(s_sin, 3)
                    for n in range(2):
                        src = ang[:, 4 + n, :].rearrange("p (t f) -> p t f", t=TPB)
                        nc.vector.tensor_scalar(cosn[:, n, :, 0, :], src, DH ** -0.5, None, ALU.mult)
                        nc.vector.tensor_copy(cosn[:, n, :, 1, :], src)
                    nc.vector.tensor_copy(masks[:, :, :].rearrange("p a b -> p (a b)"), par[:, MASK0:MASK0 + 2 * P])
                    nc.vector.tensor_copy(wqkv[:, :], par[:, 0:QKV]).then_inc(s_ready, 1)
                else:
                    mean = hv[:, :, 0:3 * HEADS]
                    for n, col in enumerate((0, BI0)):
                        src = par[:, col:col + QKV].rearrange("p (h d) -> p h d", d=DH)
                        dst = (wqkv[:, :] if n == 0 else par[:, col:col + QKV]).rearrange("p (h d) -> p h d", d=DH)
                        link(nc.vector.tensor_reduce(mean[:, 0, :], src, AX, ALU.add))
                        link(nc.vector.tensor_scalar(mean[:, 1, :], mean[:, 0, :], 1.0 / DH, None, ALU.mult))
                        link(nc.vector.tensor_tensor(
                            dst, src, mean[:, 1, :].unsqueeze(2).to_broadcast([P, 3 * HEADS, DH]), ALU.subtract))
                    link(nc.vector.tensor_scalar(par[:, SC0:SC0 + D], par[:, SC0:SC0 + D], DH ** -0.5, None, ALU.mult))
                    nc.vector.tensor_scalar(par[:, SB0:SB0 + D], par[:, SB0:SB0 + D], DH ** -0.5, None,
                                            ALU.mult).then_inc(s_ready, 1)
                dve.wait_ge(s_ready, 1)
                link.restart()

            step(-3, 1)
            setup()
            looped_steps(dve, -2, 4, 12, 18, step)
            route.dve_end(dve, link)

        @block.scalar
        def _(act):
            if causal:
                act.wait_ge(s_par, 16)
                nc.scalar.activation(dec[:, 3:5, :], par[:, GATE0:GATE0 + 2 * HEADS].rearrange("p (a h) -> p a h", a=2),
                                     ACT.Exp, scale=-1.0).then_inc(s_gpi, 1)
                nc.scalar.activation(dec[:, 0, :], par[:, XI0:XI0 + HEADS], ACT.Exp, scale=-1.0).then_inc(s_gpi, 1)
                act.wait_ge(s_sin, 1)
                nc.scalar.activation(ang[:, 5, :], ang[:, 0, :], ACT.Sin).then_inc(s_sin, 1)
                nc.scalar.activation(ang[:, 4, :], ang[:, 2, :], ACT.Sin).then_inc(s_sin, 1)

            def tiles_out(b):
                act.wait_ge(s_xaT_ps, b + 1)
                nc.scalar.copy(xaT[:, :], psA[:, 0:SEQ]).then_inc(s_xaT, 1)

            def project_out(b, u, t):
                act.wait_ge(s_proj, TPB * b + t + 1)
                if t == 0:
                    wait(act, s_qk, 2 * (b - 1))
                    wait(act, s_v, b - 1)
                nc.scalar.copy(pr[:, u, t, :], psA[:, 0:QKV]).then_inc(s_pr, 1)

            def copies_of_a(b, u):
                act.wait_ge(s_a, b + 1)
                for g in (1, 2):
                    nc.scalar.copy(parts(u, 1, g), parts(u, 1, 0))
                for g in (3, 5):
                    nc.scalar.copy(parts(u, 0, g), parts(u, 0, 0))

            def copies_of_b(b, u):
                act.wait_ge(s_b, b + 1)
                nc.scalar.copy(parts(u, 0, 1), parts(u, 0, 4))
                nc.scalar.copy(parts(u, 1, 3), parts(u, 1, 4)).then_inc(s_copies, 1)

            def squares(b, u):
                act.wait_ge(s_pr, TPB * (b + 1))
                nc.scalar.activation(pt[:, u, :, :], pr[:, u, :, :], ACT.Square).then_inc(s_sq, 1)

            def heads_rsqrt(b):
                act.wait_ge(s_hv, b + 1)
                nc.scalar.activation(hv[:, 3, :], hv[:, 2, :], ACT.Exp).then_inc(s_hr, 1)

            def values_out(b, u):
                act.wait_ge(s_pr, TPB * (b + 1))
                wait(act, s_V, UNITS * (b - 1))
                nc.scalar.copy(vx[u][:, :, :, 0:DH],
                               pr[:, u, :, 2 * D:QKV].rearrange("p t (h d) -> p t h d", d=DH)).then_inc(s_v, 1)

            def operands_out(b, u, n):
                t, w = OPERANDS[n]
                act.wait_ge(s_X, 4 * b + n + 1)
                if n == 2:
                    wait(act, s_E, UNITS * (b - 1))
                nc.scalar.copy((QT, KT)[w][u][:, :, t * P:(t + 1) * P],
                               bank_of[n][:, :].bitcast(BF16).rearrange("p (k q) -> p k q", k=8)).then_inc(s_QK[n], 1)

            def queries_out(b):
                act.wait_ge(s_Xm, TPB * (b + 1))
                wait(act, s_E, UNITS * b)
                nc.scalar.copy(QM[:, :, P:2 * P],
                               psD[:, :].bitcast(BF16).rearrange("p (k q) -> p k q", k=8)).then_inc(s_QM[1], 1)

            def weighted_out(b, u):
                act.wait_ge(s_V, UNITS * b + 8)
                nc.scalar.copy(oT[u][:, 0:2, :], psV[0][:, :, :]).then_inc(s_oT[0], 1)

            def divided_out(b):
                act.wait_ge(s_OT, b + 1)
                nc.scalar.copy(onT[:, :], back_bank[:, 0:SEQ]).then_inc(s_onT, 1)

            def unit_exp(b, c):
                g, r, kt = unit_c(c)
                q0 = P if causal and kt else 0
                act.wait_ge(s_E, UNITS * b + c + 1)
                wait(act, s_V, UNITS * b + c - 3)
                nc.scalar.activation(PT[:, c % 4, :, q0:SEQ], psE[c % 2][:, :, q0:SEQ], ACT.Exp).then_inc(s_e, 1)

            def step(s, u):
                v = 1 - u
                if has(s - 1):
                    queries_out(s - 1)

                def exps(lo, hi):
                    for c in range(lo, hi):
                        if has(s - 1):
                            unit_exp(s - 1, c)

                exps(0, 1)
                if has(s - 3):
                    route.act_T(act, s - 3, v, psA)
                exps(1, 3)
                if has(s) and causal:
                    values_out(s, u)
                exps(3, 4)
                if has(s + 2):
                    tiles_out(s + 2)
                exps(4, 5)
                if has(s + 1):
                    copies_of_a(s + 1, v)
                exps(5, 6)
                if has(s + 2) and causal:
                    project_out(s + 2, u, 0)
                exps(6, 8)
                if has(s + 1):
                    copies_of_b(s + 1, v)
                exps(8, 9)
                if has(s - 2):
                    divided_out(s - 2)
                if has(s + 2) and causal:
                    project_out(s + 2, u, 1)
                exps(9, 10)
                if has(s - 1):
                    weighted_out(s - 1, v)
                exps(10, 11)
                if has(s + 2) and not causal:
                    squares(s + 2, u)
                exps(11, 13)
                if has(s + 2) and not causal:
                    heads_rsqrt(s + 2)
                exps(13, 14)
                if has(s + 1):
                    operands_out(s + 1, v, 0)
                exps(14, 15)
                exps(15, 16)
                if has(s + 1):
                    operands_out(s + 1, v, 1)
                    operands_out(s + 1, v, 2)

            looped_steps(act, -3, 4, 12, 18, step)
            route.act_end(act)

        @block.tensor
        def _(pe):
            pe.wait_ge(s_ready, 1)
            pe.wait_ge(route.s_w, 16)

            def tiles(b, u):
                pe.wait_ge(norm.s_out, b + 1)
                if has(b - 5):
                    pe.wait_ge(route.s_xnT, b - 4)
                elif has(b - 3):
                    pe.wait_ge(s_QM[0], b - 2)
                elif has(b - 2):
                    pe.wait_ge(s_QK[1], b - 1)
                elif has(b - 1):
                    pe.wait_ge(s_pr, TPB * b)
                for t in range(TPB):
                    last = nc.tensor.transpose(psA[:, t * P:(t + 1) * P], norm.out[:, u, t, 0, :], keep.ident[:, :])
                last.then_inc(s_xaT_ps, 1)

            def project(b, t):
                if t == 0:
                    pe.wait_ge(s_xaT, b + 1)
                else:
                    pe.wait_ge(s_pr, TPB * b + t)
                nc.tensor.matmul(psA[:, 0:QKV], xaT[:, t * P:(t + 1) * P], wqkv[:, :],
                                 start=True, stop=True).then_inc(s_proj, 1)

            def operands(b, u, n):
                t, w = OPERANDS[n]
                if n == 0:
                    if has(b - 2):
                        pe.wait_ge(s_oT[0], b - 1)
                    elif has(b - 1):
                        pe.wait_ge(s_QK[3], b)
                    pe.wait_ge(s_ext, b + 1)
                    pe.wait_ge(s_copies, b + 1)
                if n == 1:
                    if has(b + 1):
                        pe.wait_ge(s_pr, TPB * (b + 2))
                    else:
                        pe.wait_ge(route.s_xnT, b - 3)
                if n == 2:
                    if has(b - 3):
                        pe.wait_ge(route.norm.s_var, b - 2)
                    elif has(b - 2):
                        pe.wait_ge(s_QM[1], b - 1)
                    elif has(b - 1):
                        pe.wait_ge(s_QK[2], b)
                if n == 3:
                    pe.wait_ge(s_QK[0], b + 1)
                src = ext[u][:, t, w, :, :].rearrange("p h r -> p (h r)")
                dst = bank_of[n][:, :].bitcast(BF16)
                for k in range(8):
                    last = nc.tensor.transpose(dst[:, k * P:(k + 1) * P], src[:, k * P:(k + 1) * P], identb[:, :])
                last.then_inc(s_X, 1)

            def unit_scores(b, u, c):
                t, g, r = unit_b(c)
                cols = P if causal and t == 0 else SEQ
                if c == 0:
                    for n in (0, 2) if causal else (0, 2, 3):
                        pe.wait_ge(s_QK[n], b + 1)
                if c == 8:
                    for n in (1, 3) if causal else (1,):
                        pe.wait_ge(s_QK[n], b + 1)
                wait(pe, s_max, UNITS * b + c - 1)
                if causal:
                    nc.tensor.matmul(psS[c % 2][:, :, t * P:(t + 1) * P], identb[:, :],
                                     masks[:, 0, :].unsqueeze(1).to_broadcast([P, 2, P]), start=True, stop=False,
                                     skip_group_check=True)
                for hh in range(2):
                    k = 2 * g + hh
                    last = nc.tensor.matmul(
                        psS[c % 2][:, hh, 0:cols], QT[u][64 * r:64 * r + MAXR, k, t * P:(t + 1) * P],
                        KT[u][64 * r:64 * r + MAXR, k, 0:cols], start=not causal, stop=True, skip_group_check=True)
                last.then_inc(s_S, 1)

            def queries(b, u, t):
                if t == 0:
                    pe.wait_ge(s_m, b + 1)
                if has(b + 1):
                    pe.wait_ge(s_QK[1 + t], b + 2)
                elif t == 0:
                    pe.wait_ge(route.s_xnT, b - 2)
                else:
                    pe.wait_ge(route.norm.s_var, b - 1)
                src = ext[u][:, t, 0, :, :].rearrange("p h r -> p (h r)")
                dst = (psA, psD)[t][:, :].bitcast(BF16)
                for k in range(8):
                    last = nc.tensor.transpose(dst[:, k * P:(k + 1) * P], src[:, k * P:(k + 1) * P], identb[:, :])
                last.then_inc(s_Xm, 1)

            def unit_e(b, u, c):
                g, r, kt = unit_c(c)
                q0 = P if causal and kt else 0
                if c == 0:
                    for t in range(TPB):
                        pe.wait_ge(s_QM[t], b + 1)
                wait(pe, s_e, UNITS * b + c - 1)
                if causal:
                    nc.tensor.matmul(psE[c % 2][:, :, kt * P:(kt + 1) * P], identb[:, :],
                                     masks[:, 1, :].unsqueeze(1).to_broadcast([P, 2, P]), start=True, stop=False,
                                     skip_group_check=True)
                for hh in range(2):
                    k = 2 * g + hh
                    last = nc.tensor.matmul(
                        psE[c % 2][:, hh, q0:SEQ], KT[u][64 * r:64 * r + MAXR + 2, k, kt * P:(kt + 1) * P],
                        QM[64 * r:64 * r + MAXR + 2, k, q0:SEQ], start=not causal, stop=True, skip_group_check=True)
                last.then_inc(s_E, 1)

            def unit_v(b, u, c):
                g, r, kt = unit_c(c)
                q0 = P if causal and kt else 0
                pe.wait_ge(s_e, UNITS * b + c + 1)
                if c == 0:
                    pe.wait_ge(s_v, b + 1)
                    if is_first(b):
                        pe.wait_ge(s_ones, 2)
                if c == 0:
                    if has(b + 1):
                        pe.wait_ge(s_QK[3], b + 2)
                    else:
                        pe.wait_ge(s_oT[0], b)
                if c == 8 and has(b - 1):
                    pe.wait_ge(s_onT, b)
                for hh in range(2):
                    head, quad = 4 * g + 2 * hh + r, 2 * hh + r
                    last = nc.tensor.matmul(
                        psV[g // 2][32 * quad:32 * quad + 32, g % 2, q0:SEQ], vx[u][:, kt, head, :],
                        PT[:, c % 4, hh, q0:SEQ], start=(kt == 0), stop=(kt == 1), skip_group_check=True,
                        tile_position=(0, 32 * quad))
                last.then_inc(s_V, 1)

            def back(b, u, t):
                if t == 0:
                    for n in range(2):
                        pe.wait_ge(s_oT[n], b + 1)
                else:
                    pe.wait_ge(s_o, TPB * b + 1)
                for g in range(G):
                    last = nc.tensor.transpose(back_bank[:, g * P:(g + 1) * P], oT[u][:, g, t * P:(t + 1) * P], keep.ident[:, :])
                last.then_inc(s_O, 1)

            def divided(b):
                pe.wait_ge(s_o, TPB * (b + 1))
                for t in range(TPB):
                    last = nc.tensor.transpose(back_bank[:, t * P:(t + 1) * P], o[:, t, :], keep.ident[:, :])
                last.then_inc(s_OT, 1)

            def output(b):
                if has(b - 1):
                    pe.wait_ge(route.s_A, b)
                elif has(b + 1):
                    pe.wait_ge(s_QM[1], b + 2)
                pe.wait_ge(s_onT, b + 1)
                for t in range(TPB):
                    dst = psD[:, t * P:(t + 1) * P]
                    last = nc.tensor.matmul(dst, onT[:, t * P:(t + 1) * P],
                                            par[:, WO0:WO0 + D], start=True, stop=True)
                last.then_inc(s_Y, 1)

            def routed_tiles(b, u):
                if has(b + 2):
                    pe.wait_ge(s_QM[0], b + 3)
                else:
                    pe.wait_ge(route.s_xnT, b)
                route.pe_T(pe, b, u, psA)

            def logits(b, u):
                if has(b + 2):
                    pe.wait_ge(s_QM[1], b + 3)
                else:
                    pe.wait_ge(route.norm.s_var, b + 1)
                route.pe_L(pe, b, u, psD)

            def step(s, u):
                v = 1 - u
                if has(s - 1):
                    queries(s - 1, v, 0)
                    queries(s - 1, v, 1)
                if has(s):
                    unit_scores(s, u, 0)
                    unit_scores(s, u, 1)
                if has(s - 3):
                    routed_tiles(s - 3, v)
                for n in range(UNITS):
                    if has(s - 1):
                        unit_e(s - 1, v, n)
                        if n >= 1:
                            unit_v(s - 1, v, n - 1)
                    if n == 0 and has(s - 2):
                        back(s - 2, u, 0)
                    if n == 2 and has(s + 2):
                        tiles(s + 2, u)
                    if n == 3 and has(s - 3):
                        logits(s - 3, v)
                    if n == 4 and has(s - 2):
                        back(s - 2, u, 1)
                    if n == 4 and has(s + 2):
                        project(s + 2, 0)
                    if n == 6 and has(s - 3):
                        route.pe_P(pe, s - 3, v, psD)
                    if n == 7 and has(s - 2):
                        divided(s - 2)
                    if n == 7 and has(s + 2):
                        project(s + 2, 1)
                    if n == 10 and has(s - 2):
                        output(s - 2)
                    if n == 12 and has(s + 1):
                        operands(s + 1, v, 0)
                    if n == 13 and has(s + 1):
                        operands(s + 1, v, 1)
                    if n == 14 and has(s + 1):
                        operands(s + 1, v, 2)
                    if has(s) and n < 14:
                        unit_scores(s, u, n + 2)
                if has(s - 1):
                    unit_v(s - 1, v, 15)
                if has(s + 1):
                    operands(s + 1, v, 3)

            looped_steps(pe, -3, 4, 12, 18, step)


def expert_stage(nc, keep, tag, slots_in, slots_out, packed, gated):
    HID = 2 if gated else 4
    WCOLS = packed.shape[2]
    DOWN0 = UP
    B1 = UP + HID * D
    B2 = B1 + UP // P
    U = TILES_HELD
    S = ROWS // P
    with ExitStack() as ctx:
        def sb(name, shape, dt):
            return ctx.enter_context(nc.sbuf_tensor(f"{tag}_{name}", shape, dt))

        def pb(name, shape, dt):
            return ctx.enter_context(nc.psum_tensor(f"{tag}_{name}", shape, dt))

        sem = stage_semaphores(nc, ctx, tag)
        w = sb("w", [P, U, WCOLS], F32)
        rows = sb("rows", [P, U, S, D + 1], F32)
        rowsT = sb("rowsT", [P, 2, ROWS], F32)
        hT = sb("hT", [P, 2, HID, ROWS], F32)
        sg = sb("sg", [P, 2, HID, ROWS], F32)
        y = sb("y", [P, U, S, D], F32)
        ids0 = sb("ids0", [P, U, S], I32)
        ids = sb("ids", [P, U, S], I32)
        psT = pb("psT", [P, 2, 256], F32)
        psH = [pb(f"psH{u}", [P, 4, ROWS], F32) for u in range(2)]
        psY = [pb(f"psY{u}", [P, 512], F32) for u in range(2)]
        s_w = [sem(f"w{u}") for u in range(U)]
        s_rows = [sem(f"rows{u}") for u in range(U)]
        s_T = sem("rows_T")
        s_rT = sem("rows_T_sbuf")
        s_H = sem("hidden")
        s_sg = sem("silu")
        s_h = sem("hidden_sbuf")
        s_Y = sem("result")
        s_y = sem("result_sbuf")
        s_pool = sem("pool_chain")
        s_st = [sem(f"stored{u}") for u in range(U)]
        block = ctx.enter_context(nc.Block())

        def row_view(dram, r):
            return dram[bass.ds(r, ROWS), :].rearrange("(p s) d -> p (s d)", p=P)

        @block.sync
        def _(sp):
            def load(j, u, first):
                e = sp.value_load(keep.table[0:1, bass.ds(j, 1), 0], min_val=0, max_val=E - 1)
                r = sp.value_load(keep.table[0:1, bass.ds(j, 1), 1], min_val=0, max_val=SPARE)
                if not first:
                    sp.wait_ge(s_y, j - U + 1)
                sp.dma_start(rows[:, u, :, :].rearrange("p s d -> p (s d)"),
                             row_view(slots_in, r)).then_inc(s_rows[u], 16)
                sp.dma_start(w[:, u, :], packed[bass.ds(e, 1), :, :].rearrange("a p n -> (a p) n")).then_inc(s_w[u], 16)

            for u in range(U):
                load(u, u, True)
            with sp.Fori(1, MOE_TILES // U) as i:
                for u in range(U):
                    load(i * U + u, u, False)

        @block.tensor
        def _(pe):
            def transpose_rows(j, u):
                pe.wait_ge(s_rows[u], (j - u) * (16 // U) + 16)
                for s in range(S):
                    last = nc.tensor.transpose(psT[:, u % 2, s * P:(s + 1) * P], rows[:, u, s, 0:D], keep.ident[:, :])
                last.then_inc(s_T, 1)

            def up(j, u):
                pe.wait_ge(s_w[u], (j - u) * (16 // U) + 16)
                pe.wait_ge(s_rT, j + 1)
                for c in range(4):
                    last = nc.tensor.matmul(psH[u % 2][:, c, :], w[:, u, c * P:(c + 1) * P], rowsT[:, u % 2, :],
                                            start=True, stop=True)
                last.then_inc(s_H, 1)

            def down(j, u):
                pe.wait_ge(s_h, j + 1)
                wait(pe, s_y, j - 1)
                for s in range(S):
                    for c in range(HID):
                        last = nc.tensor.matmul(
                            psY[u % 2][:, s * D:(s + 1) * D], hT[:, u % 2, c, s * P:(s + 1) * P],
                            w[:, u, DOWN0 + c * D:DOWN0 + (c + 1) * D], start=(c == 0), stop=(c == HID - 1))
                last.then_inc(s_Y, 1)

            def step(s, u):
                if has(s + 1, MOE_TILES):
                    up(s + 1, (u + 1) % U)
                if has(s + 2, MOE_TILES):
                    transpose_rows(s + 2, (u + 2) % U)
                if has(s, MOE_TILES):
                    down(s, u)

            looped_steps(pe, -2, 4, 36, 39, step, U)

        @block.scalar
        def _(act):
            with act.Fori(0, MOE_TILES // U) as i:
                for u in range(U):
                    act.wait_ge(s_H, i * U + u + 1)
                    if gated:
                        for c in range(HID):
                            ins = nc.scalar.activation(sg[:, u % 2, c, :], psH[u % 2][:, c, :], ACT.Silu,
                                                       bias=w[:, u, B1 + c:B1 + c + 1])
                        ins.then_inc(s_sg, 1)
                    else:
                        nc.scalar.activation(hT[:, u % 2, :, :], psH[u % 2][:, :, :], ACT.Gelu).then_inc(s_h, 1)

        @block.vector
        def _(dve):
            def step(s, u):
                if has(s + 2, MOE_TILES):
                    dve.wait_ge(s_T, s + 3)
                    nc.vector.tensor_copy(rowsT[:, u % 2, :], psT[:, u % 2, :]).then_inc(s_rT, 1)
                if gated and has(s + 1, MOE_TILES):
                    dve.wait_ge(s_sg, s + 2)
                    v = (u + 1) % U
                    for c in range(HID):
                        ins = nc.vector.scalar_tensor_tensor(
                            out=hT[:, v % 2, c, :], in0=psH[v % 2][:, HID + c, :],
                            scalar=w[:, v, B1 + HID + c:B1 + HID + c + 1], in1=sg[:, v % 2, c, :],
                            op0=ALU.add, op1=ALU.mult)
                    ins.then_inc(s_h, 1)
                if has(s, MOE_TILES):
                    wait(dve, s_st[u], (s - u) * (16 * S // U))
                    dve.wait_ge(s_Y, s + 1)
                    nc.vector.tensor_tensor(ids0[:, u, :], rows[:, u, :, D].bitcast(I32), keep.pad_ids[:, u, :],
                                            ALU.min)
                    src = psY[u % 2][:, 0:S * D].rearrange("p (s d) -> p s d", s=S)
                    if gated:
                        nc.vector.tensor_tensor(
                            y[:, u, :, :], src, w[:, u, B2:B2 + D].unsqueeze(1).to_broadcast([P, S, D]),
                            ALU.add).then_inc(s_y, 1)
                    else:
                        nc.vector.tensor_copy(y[:, u, :, :], src).then_inc(s_y, 1)

            looped_steps(dve, -2, 4, 36, 39, step, U)

        @block.gpsimd
        def _(pool):
            chain = Chain(pool, s_pool)

            def scatter(j, u):
                wait(pool, s_st[u], (j - u) * (16 * S // U))
                pool.wait_ge(s_y, j + 1)
                chain(nc.gpsimd.tensor_tensor(ids[:, u, :], ids0[:, u, :], keep.no_rows[:, 0:S], ALU.add))
                for s in range(S):
                    pool.indirect_dma_start(
                        slots_out, bass.IndirectOffsetOnAxis(ap=ids[:, u, s:s + 1].bitcast(U32), axis=0),
                        y[:, u, s, :], None).then_inc(s_st[u], 16)

            for u in range(U):
                scatter(u, u)
            chain.restart()
            with pool.Fori(1, MOE_TILES // U) as i:
                for u in range(U):
                    scatter(i * U + u, u)
                chain.restart()
            for u in range(U):
                pool.wait_ge(s_st[u], 16 * S * (MOE_TILES // U))


def program(nc, a, out):
    with ExitStack() as ctx:
        keep = Persistent(nc, ctx)
        slots_x = nc.dram_tensor("slots_x", (SLOT_ROWS, D + 1), F32, kind="Internal").ap()
        slots_y = nc.dram_tensor("slots_y", (RESULT_ROWS, D), F32, kind="Internal").ap()
        setup_stage(nc, keep, a["x"], a["consts"])
        token_stage(nc, keep, "t0", None, slots_x, a["wg"], False, capacity=True)
        expert_stage(nc, keep, "e0", slots_x, slots_y, a["pack0"], False)
        attention_stage(nc, keep, "a0", slots_y, slots_x, True, a["par0"], a["wg"], False, True)
        expert_stage(nc, keep, "e1", slots_x, slots_y, a["pack0"], False)
        token_stage(nc, keep, "t1", slots_y, slots_x, a["wr"], True)
        expert_stage(nc, keep, "e2", slots_x, slots_y, a["pack1"], True)
        attention_stage(nc, keep, "a1", slots_y, slots_x, False, a["par1"], a["wr"], True, False)
        expert_stage(nc, keep, "e3", slots_x, slots_y, a["pack1"], True)
        token_stage(nc, keep, "t2", slots_y, None, out=out)


def shape_constants():
    import numpy as np
    p = np.arange(P)[:, None]
    cols = [
        np.eye(P), (p < np.arange(P)[None, :]) * 1.0,
        np.broadcast_to(np.arange(E), (P, E)), np.broadcast_to(np.arange(E) * REGION, (P, E)),
        np.broadcast_to(np.arange(TOKENS // ROWS) * ROWS, (P, TOKENS // ROWS)),
        np.broadcast_to(np.arange(MOE_TILES), (P, MOE_TILES)),
        ((np.arange(TILES) * P + p)[:, :, None] * TOPK + np.arange(TOPK)).reshape(P, -1),
        TOKENS * TOPK + np.arange(TILES_HELD * ROWS // P) * P + p,
        np.full((P, ROWS // P), RESULT_ROWS),
    ]
    return np.concatenate(cols, 1).astype(np.float32)


def causal_constants():
    import math
    import numpy as np
    pos = (np.arange(P)[:, None] + P * np.arange(TPB)[None, :]).astype(np.float32)
    freq = np.float32(math.pi) ** (np.float32(1.0) - np.arange(0, DH, 2, dtype=np.float32) / np.float32(DH))
    ang = (pos[:, :, None] * freq.astype(np.float32)).reshape(P, -1)
    above = np.arange(P)[:, None] < np.arange(P)[None, :]
    return np.concatenate([ang, pos, above * MASKED, above.T * MASKED], 1).astype(np.float32)


def kernel(**inputs):
    import numpy as np
    import concourse.bacc as bacc
    from concourse.bass_utils import run_bass_kernel_spmd as run

    f = {k: np.asarray(v) for k, v in inputs.items()}

    def down(w):
        return w.reshape(E, -1, P, D).transpose(0, 2, 1, 3).reshape(E, P, -1)

    def rep(v):
        return np.broadcast_to(v.reshape(1, -1), (P, v.size))

    def per_head(name):
        return np.concatenate([np.tile(f[f"L1_attn_{n}_{name}"], HEADS) for n in "qkv"])

    arrays = {
        "x": f["L0_attn_x"].reshape(TOKENS, D),
        "consts": shape_constants(),
        "wg": np.tile(f["L0_ffn_wg"], (1, 2)),
        "wr": np.concatenate([f["L1_ffn_Wr"], rep(f["L1_ffn_br"])], 1),
        "pack0": np.concatenate([f["L0_ffn_w_gate"], down(f["L0_ffn_w_down"])], 2),
        "pack1": np.concatenate([
            f["L1_ffn_W1"], down(f["L1_ffn_W2"]), f["L1_ffn_b1"].reshape(E, UP // P, P).transpose(0, 2, 1),
            np.broadcast_to(f["L1_ffn_b2"][:, None, :], (E, P, D))], 2),
        "par0": np.concatenate([
            f["L0_attn_Wqkv"].T, f["L0_attn_Wo"].T, rep(f["L0_attn_pi_gate_logit"]), rep(f["L0_attn_e_gate_logit"]),
            rep(f["L0_attn_log_xi"]), causal_constants()], 1),
        "par1": np.concatenate([
            f["L1_attn_Wq"], f["L1_attn_Wk"], f["L1_attn_Wv"], f["L1_attn_Wo"],
            rep(np.concatenate([f["L1_attn_bq"], f["L1_attn_bk"], f["L1_attn_bv"]])),
            rep(per_head("scale")), rep(per_head("bias")), rep(f["L1_attn_bo"]),
            np.ones((P, P), np.float32)], 1),
    }
    nc = bacc.Bacc("TRN2", target_bir_lowering=False, num_devices=1)
    feeds, aps = {}, {}
    for name, v in arrays.items():
        v = np.ascontiguousarray(v)
        feeds[f"in_{name}"] = v
        aps[name] = nc.dram_tensor(f"in_{name}", v.shape, mybir.dt.from_np(v.dtype), kind="ExternalInput").ap()
    out = nc.dram_tensor("out_x", (TOKENS, D), F32, kind="ExternalOutput").ap()
    program(nc, aps, out)
    r = run(nc, [feeds], core_ids=[0])
    return r.results[0]["out_x"].reshape(BATCHES, SEQ, D)
```
